# Optimizing a Trainium2 kernel written in Bass

```python
import numpy as np
import jax
import jax.numpy as jnp

def _softmax(x, axis=-1):
    return jax.nn.softmax(x, axis=axis)

def _gelu(x):
    return jax.nn.gelu(x, approximate=True)

def _silu(x):
    return jax.nn.silu(x)

def _sigmoid(x):
    return jax.nn.sigmoid(x)

def _layernorm(x, axis=-1, eps=1e-05):
    m = jnp.mean(x, axis=axis, keepdims=True)
    v = jnp.var(x, axis=axis, keepdims=True)
    return (x - m) / jnp.sqrt(v + eps)

def _scatter_add(tgt, idx, src, axis=0):
    return tgt.at[idx].add(src)

def _segment_sum(src, seg, n):
    return jax.ops.segment_sum(src, seg, n)
kernel_name = 'mk_decoder_preln_d2_seqx_r4_3b2358'

def setup_inputs(seed: int=0):
    np.random.seed(seed)
    _w = jnp.asarray

    def _rec_inputs():
        import jax
        import jax.numpy as jnp
        _rk = jax.random.key(seed)
        x = -4.161e-06 + 1 * jax.random.normal(jax.random.fold_in(_rk, 1), (16, 112, 512), jnp.float32)
        _lenS = 112 - jax.random.randint(jax.random.fold_in(_rk, 7), (16,), 0, max(1, 112 // 4) + 1, jnp.int32)
        _lenS2 = 375 - jax.random.randint(jax.random.fold_in(_rk, 8), (16,), 0, max(1, 375 // 4) + 1, jnp.int32)
        _ctx_2048P = jax.random.normal(jax.random.fold_in(_rk, 11), (16, 16, 512), jnp.float32)
        _ctx_2048c = jax.random.dirichlet(jax.random.fold_in(_rk, 511), 0.3 * jnp.ones((16,), jnp.float32), (16, 375))
        _ctx_2048t = jnp.einsum('bsk,bkd->bsd', _ctx_2048c, _ctx_2048P)
        _ctx_2048t = _ctx_2048t * jax.lax.rsqrt(jnp.mean(jnp.square(_ctx_2048t)) + 1e-12) * 0.953939
        ctx_2048 = -0.000192764 + 0.999654 * (_ctx_2048t + 0.3 * jax.random.normal(jax.random.fold_in(_rk, 611), (16, 375, 512), jnp.float32))
        _validS = jnp.arange(112)[None, :] < _lenS[:, None]
        _validS2 = jnp.arange(375)[None, :] < _lenS2[:, None]
        _causal = jnp.tril(jnp.ones((112, 112), dtype=bool))
        mask_BxSx4224_bf0 = jnp.logical_not(jnp.ones((16, 112, 1056), dtype=bool))
        return (x, ctx_2048, mask_BxSx4224_bf0)
    x, ctx_2048, mask_BxSx4224_bf0 = _rec_inputs()

    def _L0_attn_setup():
        import jax, jax.numpy as jnp
        import numpy as np
        HIDDEN = 512
        NUM_HEADS = 16
        NUM_KV_HEADS = 4
        HEAD_DIM = HIDDEN // NUM_HEADS
        Q_PER_KV = NUM_HEADS // NUM_KV_HEADS
        GROUP_SIZE = (Q_PER_KV + 2) * HEAD_DIM
        TOTAL_PROJ = NUM_KV_HEADS * GROUP_SIZE
        SEQ, BATCH = (512, 2)
        key = jax.random.key(seed)
        k1, k2, k3 = jax.random.split(key, 3)
        x = jax.random.normal(k1, (SEQ, BATCH, HIDDEN), dtype=jnp.float32)
        weight_qkv = jax.random.normal(k2, (TOTAL_PROJ, HIDDEN), dtype=jnp.float32) * 0.02
        weight_proj = jax.random.normal(k3, (HIDDEN, NUM_HEADS * HEAD_DIM), dtype=jnp.float32) * 0.02
        return {'x': x, 'weight_qkv': weight_qkv, 'weight_proj': weight_proj}
    _L0_attn_all = _L0_attn_setup()
    _L0_attn_in = {k: v for k, v in _L0_attn_all.items() if k in ('weight_qkv', 'weight_proj')}
    del _L0_attn_all

    def _L0_xattn_setup():
        import jax, jax.numpy as jnp
        import numpy as np
        FP8_MAX = 448.0
        EPS = 1e-05

        def _fp8_roundtrip(x):
            return x.astype(jnp.float8_e4m3fn).astype(jnp.float32)

        def _div_clamp_fp8(x, scale):
            y = jnp.clip(x.astype(jnp.float32) / scale, -FP8_MAX, FP8_MAX)
            y = y.astype(jnp.bfloat16).astype(jnp.float32)
            return _fp8_roundtrip(y)

        def _ln(x, w, b):
            mu = jnp.mean(x, axis=-1, keepdims=True)
            var = jnp.mean(jnp.square(x - mu), axis=-1, keepdims=True)
            return (x - mu) * jax.lax.rsqrt(var + EPS) * w + b

        def _fp8_linear_pertensor(x, wq, w_scale, in_scale):
            xq = _div_clamp_fp8(x, in_scale)
            return jnp.einsum('bsi,oi->bso', xq * in_scale, wq) * w_scale

        def _gqa(q, k, v):
            scale = 1.0 / np.sqrt(q.shape[-1])
            scores = jnp.einsum('bsghd,btgd->bghst', q, k) * scale
            p = jax.nn.softmax(scores, axis=-1)
            return jnp.einsum('bghst,btgd->bsghd', p, v)
        key = jax.random.key(seed)
        ks = jax.random.split(key, 8)
        B, S, SC, H, NH, G, D = (2, 512, 128, 512, 16, 8, 128)

        def qw(k, out_f, in_f):
            w = jax.random.normal(k, (out_f, in_f), jnp.float32) * 0.02
            sc = jnp.max(jnp.abs(w)) / FP8_MAX
            return (_fp8_roundtrip(w / sc), sc.astype(jnp.float32))
        wq, wq_s = qw(ks[0], NH * D, H)
        wqx, wqx_s = qw(ks[1], NH * D, H)
        wk, wk_s = qw(ks[2], G * D, H)
        wv, wv_s = qw(ks[3], G * D, H)
        wproj, wp_s = qw(ks[4], H, 2 * NH * D)
        return {'hidden_states': jax.random.normal(ks[5], (B, S, H), jnp.float32), 'cond': jax.random.normal(ks[6], (B, SC, H), jnp.float32), 'ln_w': jnp.ones((H,), jnp.float32), 'ln_b': jnp.zeros((H,), jnp.float32), 'wq': wq, 'wq_scale': wq_s, 'q_in_scale': jnp.full((H,), 0.05, jnp.float32), 'wqx': wqx, 'wqx_scale': wqx_s, 'qx_in_scale': jnp.full((H,), 0.05, jnp.float32), 'wk': wk, 'wk_scale': wk_s, 'k_in_scale': jnp.full((H,), 0.05, jnp.float32), 'wv': wv, 'wv_scale': wv_s, 'v_in_scale': jnp.full((H,), 0.05, jnp.float32), 'w_kv_x': jax.random.normal(ks[7], (2 * G * D, H), jnp.float32) * 0.02, 'qln_w': jnp.ones((D,), jnp.float32), 'qln_b': jnp.zeros((D,), jnp.float32), 'kln_w': jnp.ones((D,), jnp.float32), 'kln_b': jnp.zeros((D,), jnp.float32), 'qxln_w': jnp.ones((D,), jnp.float32), 'qxln_b': jnp.zeros((D,), jnp.float32), 'kxln_w': jnp.ones((D,), jnp.float32), 'kxln_b': jnp.zeros((D,), jnp.float32), 'wproj': wproj, 'proj_w_scale': wp_s, 'proj_in_scale': jnp.asarray(0.05, jnp.float32), 'proj_smooth': jnp.full((2 * NH * D,), 0.05, jnp.float32)}
    _L0_xattn_all = _L0_xattn_setup()
    _L0_xattn_in = {k: v for k, v in _L0_xattn_all.items() if k in ('ln_w', 'ln_b', 'wq', 'wq_scale', 'q_in_scale', 'wqx', 'wqx_scale', 'qx_in_scale', 'wk', 'wk_scale', 'k_in_scale', 'wv', 'wv_scale', 'v_in_scale', 'w_kv_x', 'qln_w', 'qln_b', 'kln_w', 'kln_b', 'qxln_w', 'qxln_b', 'kxln_w', 'kxln_b', 'wproj', 'proj_w_scale', 'proj_in_scale', 'proj_smooth')}
    del _L0_xattn_all

    def _L0_ffn_setup():
        import jax, jax.numpy as jnp
        import numpy as np
        BS, SLEN, DIM, HID, E, TOPK = (4, 512, 512, 448, 8, 2)
        key = jax.random.key(seed)
        ks = jax.random.split(key, 9)
        s = 0.02
        return {'x': jax.random.normal(ks[0], (BS, SLEN, DIM), jnp.float32), 'gate_w': jax.random.normal(ks[1], (DIM, E), jnp.float32) * s, 'w1': jax.random.normal(ks[2], (E, DIM, HID), jnp.float32) * s, 'w2': jax.random.normal(ks[3], (E, HID, DIM), jnp.float32) * s, 'w3': jax.random.normal(ks[4], (E, DIM, HID), jnp.float32) * s, 'sw1': jax.random.normal(ks[5], (DIM, HID), jnp.float32) * s, 'sw2': jax.random.normal(ks[6], (HID, DIM), jnp.float32) * s, 'sw3': jax.random.normal(ks[7], (DIM, HID), jnp.float32) * s, 'expert_bias': jnp.zeros((E,), jnp.float32)}
    _L0_ffn_all = _L0_ffn_setup()
    _L0_ffn_in = {k: v for k, v in _L0_ffn_all.items() if k in ('gate_w', 'w1', 'w2', 'w3', 'sw1', 'sw2', 'sw3', 'expert_bias')}
    del _L0_ffn_all

    def _L1_attn_setup():
        import jax, jax.numpy as jnp
        import numpy as np
        N_HEADS = 16
        key = jax.random.key(seed)
        ks = jax.random.split(key, 9)
        B, S, D = (2, 512, 512)
        s = 0.02
        return {'X': jax.random.normal(ks[0], (B, S, D), jnp.float32), 'Wq': jax.random.normal(ks[1], (D, D), jnp.float32) * s, 'bq': jax.random.normal(ks[2], (D,), jnp.float32) * s, 'Wk': jax.random.normal(ks[3], (D, D), jnp.float32) * s, 'bk': jax.random.normal(ks[4], (D,), jnp.float32) * s, 'Wv': jax.random.normal(ks[5], (D, D), jnp.float32) * s, 'bv': jax.random.normal(ks[6], (D,), jnp.float32) * s, 'Wo': jax.random.normal(ks[7], (D, D), jnp.float32) * s, 'bo': jax.random.normal(ks[8], (D,), jnp.float32) * s}
    _L1_attn_all = _L1_attn_setup()
    _L1_attn_in = {k: v for k, v in _L1_attn_all.items() if k in ('Wq', 'bq', 'Wk', 'bk', 'Wv', 'bv', 'Wo', 'bo')}
    del _L1_attn_all

    def _L1_xattn_setup():
        import jax, jax.numpy as jnp
        import numpy as np
        import math
        DIM = 512
        B, Q_LEN, KV_LEN = (8, 128, 1024)
        key = jax.random.key(seed)
        ks = jax.random.split(key, 8)
        x = jax.random.normal(ks[0], (B, Q_LEN, DIM), dtype=jnp.float32)
        mask = jnp.zeros((B, Q_LEN, KV_LEN + Q_LEN), dtype=bool)
        k_cache = jax.random.normal(ks[1], (B, KV_LEN, DIM), dtype=jnp.float32)
        v_cache = jax.random.normal(ks[2], (B, KV_LEN, DIM), dtype=jnp.float32)
        scale = 1.0 / math.sqrt(DIM)
        wq = jax.random.normal(ks[3], (DIM, DIM), dtype=jnp.float32) * scale
        wk = jax.random.normal(ks[4], (DIM, DIM), dtype=jnp.float32) * scale
        wv = jax.random.normal(ks[5], (DIM, DIM), dtype=jnp.float32) * scale
        wo = jax.random.normal(ks[6], (DIM, DIM), dtype=jnp.float32) * scale
        return {'x': x, 'mask': mask, 'k_cache': k_cache, 'v_cache': v_cache, 'wq': wq, 'wk': wk, 'wv': wv, 'wo': wo}
    _L1_xattn_all = _L1_xattn_setup()
    _L1_xattn_in = {k: v for k, v in _L1_xattn_all.items() if k in ('wq', 'wk', 'wv', 'wo')}
    del _L1_xattn_all

    def _L1_ffn_setup():
        import jax, jax.numpy as jnp
        import numpy as np
        D_MODEL = 512
        D_EXPERT = 2048
        EPS = 1e-08

        def ternary_quant(w):
            scale = jnp.mean(jnp.abs(w)) + EPS
            q = jnp.clip(jnp.round(w / scale), -1.0, 1.0) * scale
            return w + jax.lax.stop_gradient(q - w)
        key = jax.random.key(seed)
        k_x, k_up, k_gate, k_down = jax.random.split(key, 4)
        std_in = 1.0 / np.sqrt(D_MODEL)
        std_exp = 1.0 / np.sqrt(D_EXPERT)
        return {'x': jax.random.normal(k_x, (4, 512, D_MODEL), dtype=jnp.float32), 'W_up': jax.random.normal(k_up, (D_EXPERT, D_MODEL), dtype=jnp.float32) * std_in, 'W_gate': jax.random.normal(k_gate, (D_EXPERT, D_MODEL), dtype=jnp.float32) * std_in, 'W_down': jax.random.normal(k_down, (D_MODEL, D_EXPERT), dtype=jnp.float32) * std_exp}
    _L1_ffn_all = _L1_ffn_setup()
    _L1_ffn_in = {k: v for k, v in _L1_ffn_all.items() if k in ('W_up', 'W_gate', 'W_down')}
    del _L1_ffn_all
    return {'x': x, 'ctx_2048': ctx_2048, 'mask_BxSx4224_bf0': mask_BxSx4224_bf0, 'L0_attn_weight_qkv': _L0_attn_in['weight_qkv'], 'L0_attn_weight_proj': _L0_attn_in['weight_proj'], 'L0_xattn_ln_w': _L0_xattn_in['ln_w'], 'L0_xattn_ln_b': _L0_xattn_in['ln_b'], 'L0_xattn_wq': _L0_xattn_in['wq'], 'L0_xattn_wq_scale': _L0_xattn_in['wq_scale'], 'L0_xattn_q_in_scale': _L0_xattn_in['q_in_scale'], 'L0_xattn_wqx': _L0_xattn_in['wqx'], 'L0_xattn_wqx_scale': _L0_xattn_in['wqx_scale'], 'L0_xattn_qx_in_scale': _L0_xattn_in['qx_in_scale'], 'L0_xattn_wk': _L0_xattn_in['wk'], 'L0_xattn_wk_scale': _L0_xattn_in['wk_scale'], 'L0_xattn_k_in_scale': _L0_xattn_in['k_in_scale'], 'L0_xattn_wv': _L0_xattn_in['wv'], 'L0_xattn_wv_scale': _L0_xattn_in['wv_scale'], 'L0_xattn_v_in_scale': _L0_xattn_in['v_in_scale'], 'L0_xattn_w_kv_x': _L0_xattn_in['w_kv_x'], 'L0_xattn_qln_w': _L0_xattn_in['qln_w'], 'L0_xattn_qln_b': _L0_xattn_in['qln_b'], 'L0_xattn_kln_w': _L0_xattn_in['kln_w'], 'L0_xattn_kln_b': _L0_xattn_in['kln_b'], 'L0_xattn_qxln_w': _L0_xattn_in['qxln_w'], 'L0_xattn_qxln_b': _L0_xattn_in['qxln_b'], 'L0_xattn_kxln_w': _L0_xattn_in['kxln_w'], 'L0_xattn_kxln_b': _L0_xattn_in['kxln_b'], 'L0_xattn_wproj': _L0_xattn_in['wproj'], 'L0_xattn_proj_w_scale': _L0_xattn_in['proj_w_scale'], 'L0_xattn_proj_in_scale': _L0_xattn_in['proj_in_scale'], 'L0_xattn_proj_smooth': _L0_xattn_in['proj_smooth'], 'L0_ffn_gate_w': _L0_ffn_in['gate_w'], 'L0_ffn_w1': _L0_ffn_in['w1'], 'L0_ffn_w2': _L0_ffn_in['w2'], 'L0_ffn_w3': _L0_ffn_in['w3'], 'L0_ffn_sw1': _L0_ffn_in['sw1'], 'L0_ffn_sw2': _L0_ffn_in['sw2'], 'L0_ffn_sw3': _L0_ffn_in['sw3'], 'L0_ffn_expert_bias': _L0_ffn_in['expert_bias'], 'L1_attn_Wq': _L1_attn_in['Wq'], 'L1_attn_bq': _L1_attn_in['bq'], 'L1_attn_Wk': _L1_attn_in['Wk'], 'L1_attn_bk': _L1_attn_in['bk'], 'L1_attn_Wv': _L1_attn_in['Wv'], 'L1_attn_bv': _L1_attn_in['bv'], 'L1_attn_Wo': _L1_attn_in['Wo'], 'L1_attn_bo': _L1_attn_in['bo'], 'L1_xattn_wq': _L1_xattn_in['wq'], 'L1_xattn_wk': _L1_xattn_in['wk'], 'L1_xattn_wv': _L1_xattn_in['wv'], 'L1_xattn_wo': _L1_xattn_in['wo'], 'L1_ffn_W_up': _L1_ffn_in['W_up'], 'L1_ffn_W_gate': _L1_ffn_in['W_gate'], 'L1_ffn_W_down': _L1_ffn_in['W_down']}

def reference(x, ctx_2048, mask_BxSx4224_bf0, L0_attn_weight_qkv, L0_attn_weight_proj, L0_xattn_ln_w, L0_xattn_ln_b, L0_xattn_wq, L0_xattn_wq_scale, L0_xattn_q_in_scale, L0_xattn_wqx, L0_xattn_wqx_scale, L0_xattn_qx_in_scale, L0_xattn_wk, L0_xattn_wk_scale, L0_xattn_k_in_scale, L0_xattn_wv, L0_xattn_wv_scale, L0_xattn_v_in_scale, L0_xattn_w_kv_x, L0_xattn_qln_w, L0_xattn_qln_b, L0_xattn_kln_w, L0_xattn_kln_b, L0_xattn_qxln_w, L0_xattn_qxln_b, L0_xattn_kxln_w, L0_xattn_kxln_b, L0_xattn_wproj, L0_xattn_proj_w_scale, L0_xattn_proj_in_scale, L0_xattn_proj_smooth, L0_ffn_gate_w, L0_ffn_w1, L0_ffn_w2, L0_ffn_w3, L0_ffn_sw1, L0_ffn_sw2, L0_ffn_sw3, L0_ffn_expert_bias, L1_attn_Wq, L1_attn_bq, L1_attn_Wk, L1_attn_bk, L1_attn_Wv, L1_attn_bv, L1_attn_Wo, L1_attn_bo, L1_xattn_wq, L1_xattn_wk, L1_xattn_wv, L1_xattn_wo, L1_ffn_W_up, L1_ffn_W_gate, L1_ffn_W_down):
    import jax
    import jax.numpy as jnp

    def _L0_attn_ref(x, weight_qkv, weight_proj):
        import jax, jax.numpy as jnp
        import numpy as np
        HIDDEN = 512
        NUM_HEADS = 16
        NUM_KV_HEADS = 4
        HEAD_DIM = HIDDEN // NUM_HEADS
        Q_PER_KV = NUM_HEADS // NUM_KV_HEADS
        GROUP_SIZE = (Q_PER_KV + 2) * HEAD_DIM
        TOTAL_PROJ = NUM_KV_HEADS * GROUP_SIZE
        SEQ, BATCH = (512, 2)
        seq, batch, hidden = x.shape
        q_size = Q_PER_KV * HEAD_DIM
        qkv = x.reshape(-1, hidden) @ weight_qkv.T
        qkv = qkv.reshape(-1, NUM_KV_HEADS, GROUP_SIZE)
        q = qkv[:, :, :q_size].reshape(seq, batch, NUM_HEADS, HEAD_DIM)
        k = qkv[:, :, q_size:q_size + HEAD_DIM].reshape(seq, batch, NUM_KV_HEADS, HEAD_DIM)
        v = qkv[:, :, q_size + HEAD_DIM:].reshape(seq, batch, NUM_KV_HEADS, HEAD_DIM)
        k = jnp.repeat(k, Q_PER_KV, axis=2)
        v = jnp.repeat(v, Q_PER_KV, axis=2)
        q = q.transpose(1, 2, 0, 3)
        k = k.transpose(1, 2, 0, 3)
        v = v.transpose(1, 2, 0, 3)
        scale = 1.0 / np.sqrt(HEAD_DIM)
        scores = jnp.einsum('bhqd,bhkd->bhqk', q, k) * scale
        causal = jnp.tril(jnp.ones((seq, seq), dtype=bool))
        scores = jnp.where(causal, scores, jnp.float32(-jnp.inf))
        probs = jax.nn.softmax(scores, axis=-1)
        attn = jnp.einsum('bhqk,bhkd->bhqd', probs, v)
        attn = attn.transpose(2, 0, 1, 3).reshape(seq * batch, NUM_HEADS * HEAD_DIM)
        out = attn @ weight_proj.T
        return out.reshape(seq, batch, hidden)

    def _L0_xattn_ref(hidden_states, cond, ln_w, ln_b, wq, wq_scale, q_in_scale, wqx, wqx_scale, qx_in_scale, wk, wk_scale, k_in_scale, wv, wv_scale, v_in_scale, w_kv_x, qln_w, qln_b, kln_w, kln_b, qxln_w, qxln_b, kxln_w, kxln_b, wproj, proj_w_scale, proj_in_scale, proj_smooth):
        import jax, jax.numpy as jnp
        import numpy as np
        FP8_MAX = 448.0
        EPS = 1e-05

        def _fp8_roundtrip(x):
            return x.astype(jnp.float8_e4m3fn).astype(jnp.float32)

        def _div_clamp_fp8(x, scale):
            y = jnp.clip(x.astype(jnp.float32) / scale, -FP8_MAX, FP8_MAX)
            y = y.astype(jnp.bfloat16).astype(jnp.float32)
            return _fp8_roundtrip(y)

        def _ln(x, w, b):
            mu = jnp.mean(x, axis=-1, keepdims=True)
            var = jnp.mean(jnp.square(x - mu), axis=-1, keepdims=True)
            return (x - mu) * jax.lax.rsqrt(var + EPS) * w + b

        def _fp8_linear_pertensor(x, wq, w_scale, in_scale):
            xq = _div_clamp_fp8(x, in_scale)
            return jnp.einsum('bsi,oi->bso', xq * in_scale, wq) * w_scale

        def _gqa(q, k, v):
            scale = 1.0 / np.sqrt(q.shape[-1])
            scores = jnp.einsum('bsghd,btgd->bghst', q, k) * scale
            p = jax.nn.softmax(scores, axis=-1)
            return jnp.einsum('bghst,btgd->bsghd', p, v)
        b, s, _ = hidden_states.shape
        sc = cond.shape[1]
        d = qln_w.shape[0]
        nh = wq.shape[0] // d
        g = wk.shape[0] // d
        hpg = nh // g
        ln_out = _ln(hidden_states, ln_w, ln_b)
        q = _fp8_linear_pertensor(ln_out, wq, wq_scale, q_in_scale).reshape(b, s, g, hpg, d)
        q = _ln(q, qln_w, qln_b)
        k = _fp8_linear_pertensor(ln_out, wk, wk_scale, k_in_scale).reshape(b, s, g, d)
        k = _ln(k, kln_w, kln_b)
        v = _fp8_linear_pertensor(ln_out, wv, wv_scale, v_in_scale).reshape(b, s, g, d)
        core = _gqa(q, k, v).reshape(b, s, nh * d)
        qx = _fp8_linear_pertensor(ln_out, wqx, wqx_scale, qx_in_scale).reshape(b, s, g, hpg, d)
        qx = _ln(qx, qxln_w, qxln_b)
        kvx = jnp.einsum('bsi,oi->bso', cond, w_kv_x)
        kx, vx = jnp.split(kvx, 2, axis=-1)
        kx = _ln(kx.reshape(b, sc, g, d), kxln_w, kxln_b)
        vx = vx.reshape(b, sc, g, d)
        xout = _gqa(qx, kx, vx).reshape(b, s, nh * d)
        cat = jnp.concatenate([core, xout], axis=-1)
        catq = _div_clamp_fp8(cat, proj_smooth)
        return jnp.einsum('bsi,oi->bso', catq, wproj) * (proj_in_scale * proj_w_scale)

    def _L0_ffn_ref(x, gate_w, w1, w2, w3, sw1, sw2, sw3, expert_bias):
        import jax, jax.numpy as jnp
        import numpy as np
        BS, SLEN, DIM, HID, E, TOPK = (4, 512, 512, 448, 8, 2)
        bs, slen, dim = x.shape
        T = bs * slen
        xf = x.reshape(T, dim)
        scores = jax.nn.softmax((xf @ gate_w).astype(jnp.float32), axis=-1)
        _, sel = jax.lax.top_k(scores + expert_bias[None, :], TOPK)
        top_scores = jnp.take_along_axis(scores, sel, axis=1)
        flat_sel = sel.reshape(-1)
        counts = jnp.bincount(flat_sel, length=E).astype(jnp.int32)
        order = jnp.argsort(flat_sel, stable=True)
        top_scores_sorted = top_scores.reshape(-1)[order]
        token_idx = order // TOPK
        routed_in = xf[token_idx] * top_scores_sorted[:, None]
        h = jax.nn.silu(jax.lax.ragged_dot(routed_in, w1, counts)) * jax.lax.ragged_dot(routed_in, w3, counts)
        routed_out = jax.lax.ragged_dot(h, w2, counts)
        out = jax.nn.silu(xf @ sw1) * (xf @ sw3) @ sw2
        out = out.at[token_idx].add(routed_out)
        return out.reshape(bs, slen, dim)

    def _L1_attn_ref(X, Wq, bq, Wk, bk, Wv, bv, Wo, bo):
        import jax, jax.numpy as jnp
        import numpy as np
        N_HEADS = 16
        B, S, D = X.shape
        H = N_HEADS
        d_head = D // H
        scale = jnp.asarray(1.0 / np.sqrt(np.sqrt(d_head)), X.dtype)
        Q = (X @ Wq.T + bq).reshape(B, S, H, d_head) * scale
        K = (X @ Wk.T + bk).reshape(B, S, H, d_head) * scale
        V = (X @ Wv.T + bv).reshape(B, S, H, d_head)
        scores = jnp.einsum('bqhd,bkhd->bhqk', Q, K)
        causal = jnp.tril(jnp.ones((S, S), bool))
        scores = jnp.where(causal[None, None], scores, -jnp.inf)
        attn = jax.nn.softmax(scores.astype(jnp.float32), axis=-1).astype(X.dtype)
        out = jnp.einsum('bhqk,bkhd->bqhd', attn, V).reshape(B, S, D)
        return out @ Wo.T + bo

    def _L1_xattn_ref(x, mask, k_cache, v_cache, wq, wk, wv, wo):
        import jax, jax.numpy as jnp
        import numpy as np
        import math
        DIM = 512
        B, Q_LEN, KV_LEN = (8, 128, 1024)
        q = jnp.einsum('bsd,ed->bse', x, wq)
        k_new = jnp.einsum('bsd,ed->bse', x, wk)
        v_new = jnp.einsum('bsd,ed->bse', x, wv)
        k = jnp.concatenate([k_cache, k_new], axis=1)
        v = jnp.concatenate([v_cache, v_new], axis=1)
        scale = 1.0 / math.sqrt(q.shape[-1])
        scores = jnp.einsum('bqd,bkd->bqk', q, k) * scale
        attn = jax.nn.softmax(scores, axis=-1)
        out = jnp.einsum('bqk,bkd->bqd', attn, v)
        return jnp.einsum('bqd,ed->bqe', out, wo)

    def _L1_ffn_ref(x, W_up, W_gate, W_down):
        import jax, jax.numpy as jnp
        import numpy as np
        D_MODEL = 512
        D_EXPERT = 2048
        EPS = 1e-08

        def ternary_quant(w):
            scale = jnp.mean(jnp.abs(w)) + EPS
            q = jnp.clip(jnp.round(w / scale), -1.0, 1.0) * scale
            return w + jax.lax.stop_gradient(q - w)
        wu = ternary_quant(W_up)
        wg = ternary_quant(W_gate)
        wd = ternary_quant(W_down)
        up = jnp.einsum('bsd,ed->bse', x, wu)
        gate = jnp.einsum('bsd,ed->bse', x, wg)
        hidden = jax.nn.silu(up) * gate
        return jnp.einsum('bse,de->bsd', hidden, wd)
    x = x + _L0_attn_ref(_layernorm(x, axis=-1), L0_attn_weight_qkv, L0_attn_weight_proj)
    x = x + _L0_xattn_ref(_layernorm(x, axis=-1), ctx_2048, L0_xattn_ln_w, L0_xattn_ln_b, L0_xattn_wq, L0_xattn_wq_scale, L0_xattn_q_in_scale, L0_xattn_wqx, L0_xattn_wqx_scale, L0_xattn_qx_in_scale, L0_xattn_wk, L0_xattn_wk_scale, L0_xattn_k_in_scale, L0_xattn_wv, L0_xattn_wv_scale, L0_xattn_v_in_scale, L0_xattn_w_kv_x, L0_xattn_qln_w, L0_xattn_qln_b, L0_xattn_kln_w, L0_xattn_kln_b, L0_xattn_qxln_w, L0_xattn_qxln_b, L0_xattn_kxln_w, L0_xattn_kxln_b, L0_xattn_wproj, L0_xattn_proj_w_scale, L0_xattn_proj_in_scale, L0_xattn_proj_smooth)
    x = x + _L0_ffn_ref(_layernorm(x, axis=-1), L0_ffn_gate_w, L0_ffn_w1, L0_ffn_w2, L0_ffn_w3, L0_ffn_sw1, L0_ffn_sw2, L0_ffn_sw3, L0_ffn_expert_bias)
    x = x + _L1_attn_ref(_layernorm(x, axis=-1), L1_attn_Wq, L1_attn_bq, L1_attn_Wk, L1_attn_bk, L1_attn_Wv, L1_attn_bv, L1_attn_Wo, L1_attn_bo)
    x = x + _L1_xattn_ref(_layernorm(x, axis=-1), mask_BxSx4224_bf0, ctx_2048, ctx_2048, L1_xattn_wq, L1_xattn_wk, L1_xattn_wv, L1_xattn_wo)
    x = x + _L1_ffn_ref(_layernorm(x, axis=-1), L1_ffn_W_up, L1_ffn_W_gate, L1_ffn_W_down)
    return x

_drawn_inputs = setup_inputs


def setup_inputs(seed=0):
    import zlib

    import numpy as np

    out = dict(_drawn_inputs(seed))
    spreads = {'L0_xattn_ln_w': (1.0, 0.2),
     'L0_xattn_ln_b': (0.0, 0.1),
     'L0_xattn_q_in_scale': (0.05000000074505806, 0.6),
     'L0_xattn_qx_in_scale': (0.05000000074505806, 0.6),
     'L0_xattn_k_in_scale': (0.05000000074505806, 0.6),
     'L0_xattn_v_in_scale': (0.05000000074505806, 0.6),
     'L0_xattn_qln_w': (1.0, 0.6),
     'L0_xattn_qln_b': (0.0, 0.8),
     'L0_xattn_kln_w': (1.0, 0.6),
     'L0_xattn_kln_b': (0.0, 2.0),
     'L0_xattn_qxln_w': (1.0, 0.6),
     'L0_xattn_qxln_b': (0.0, 0.727),
     'L0_xattn_kxln_w': (1.0, 0.6),
     'L0_xattn_kxln_b': (0.0, 2.0),
     'L0_xattn_proj_smooth': (0.05000000074505806, 0.2),
     'L0_ffn_expert_bias': (0.0, 0.8)}
    factors = {'L0_ffn_gate_w': 8.0,
     'L0_ffn_w1': 8.0,
     'L0_ffn_w2': 8.0,
     'L0_ffn_w3': 8.0,
     'L1_attn_Wq': 29.774,
     'L1_attn_bq': 64.0,
     'L1_attn_Wk': 27.924,
     'L1_attn_bk': 64.0,
     'L1_attn_bv': 50.856,
     'L1_attn_bo': 24.544,
     'L0_ffn_sw1': 8.0,
     'L0_ffn_sw2': 8.0,
     'L0_ffn_sw3': 8.0,
     'L1_attn_Wv': 3.714,
     'L1_attn_Wo': 3.523,
     'L1_xattn_wq': 3.963,
     'L1_xattn_wk': 8.0,
     'L1_xattn_wv': 8.0,
     'L1_ffn_W_up': 4.267,
     'L1_ffn_W_gate': 3.876,
     'L1_ffn_W_down': 3.887}
    for name, (base, spread) in spreads.items():
        noise = np.random.default_rng([zlib.crc32(name.encode()), seed]).standard_normal(out[name].shape)
        drawn = base * np.exp(spread * noise) if base else spread * noise
        out[name] = jnp.asarray(drawn.astype(out[name].dtype))
    for name, factor in factors.items():
        out[name] = (out[name] * factor).astype(out[name].dtype)
    return out
```

```python
from contextlib import ExitStack

import concourse.bass as bass
from concourse import mybir
from concourse.alu_op_type import AluOpType as ALU

F32 = mybir.dt.float32
F32R = mybir.dt.float32r
BF16 = mybir.dt.bfloat16
U16 = mybir.dt.uint16
ACT = mybir.ActivationFunctionType
AX = mybir.AxisListType

P = 128
B = 16
S = 112
D = 512
DC = D // P
EPS = 1e-5
MASKED = -1e30


def wait(eng, sem, value):
    if isinstance(value, int) and value <= 0:
        return
    eng.wait_ge(sem, value)


def product(pe, out, lhs, rhs, first, last):
    pairs = [(lhs[0], rhs[0])]
    if len(lhs) > 1:
        pairs.append((lhs[1], rhs[0]))
    if len(rhs) > 1:
        pairs.append((lhs[0], rhs[1]))
    for n, (a, b) in enumerate(pairs):
        mm = pe.matmul(out, a, b, start=first and n == 0, stop=last and n == len(pairs) - 1)
    return mm


class Core:

    def __init__(self, nc, ctx):
        self.nc = nc
        self.sem_ctx = ctx.enter_context(ExitStack())
        self.sems = []
        self.ps = [ctx.enter_context(nc.psum_tensor(f"bank{i}", [P, 512], F32)) for i in range(8)]
        self.ident = self.sb(ctx, "ident", [P, P], F32)
        self.ones = self.sb(ctx, "ones", [P, P], F32)
        self.half = self.sb(ctx, "minus_half", [P, 32], F32)
        self.mean_var = self.sb(ctx, "mean_var", [P, B, 2], F32)
        self.rstd = self.sb(ctx, "rstd", [P, B], F32)

    def sb(self, ctx, name, shape, dt):
        return ctx.enter_context(self.nc.sbuf_tensor(name, shape, dt))

    def sem(self, name):
        handle = self.sem_ctx.enter_context(self.nc.semaphore(name))
        self.sems.append(handle)
        return handle

    def recycle_semaphores(self):
        with self.nc.Block() as block:
            @block.gpsimd
            def _(pool):
                for handle in self.sems:
                    pool.sem_clear(handle)
        self.sem_ctx.close()
        self.sems = []


def constants(k):
    nc = k.nc
    zeroed = k.sem("const_zeroed")
    with nc.Block() as block:
        @block.gpsimd
        def _(pool):
            pool.memset(k.ident[:], 0.0).then_inc(zeroed, 1)
            pool.memset(k.ones[:], 1.0).then_inc(zeroed, 1)
            pool.memset(k.half[:], -0.5).then_inc(zeroed, 1)
            pool.wait_ge(zeroed, 1)
            pool.affine_select(out=k.ident[:], in_=k.ident[:], compare_op=ALU.not_equal, fill=1.0,
                               base=0, pattern=[[-1, P]], channel_multiplier=1).then_inc(zeroed, 1)
            pool.wait_ge(zeroed, 4)


def prepare(k, name, raw, pieces, rows=None, loads=(), width=2048):
    nc = k.nc
    chunks = []
    for src, hi, lo, scale in pieces:
        n = src.shape[1]
        for a in range(0, n, width):
            chunks.append((src.shape[0], src[:, a:min(n, a + width)], hi[:, a:min(n, a + width)],
                           lo[:, a:min(n, a + width)], scale))
    landed = [k.sem(f"{name}_raw_landed{i}") for i in range(2)]
    high_done, low_done = k.sem(f"{name}_high_done"), k.sem(f"{name}_low_done")
    loaded, stat, centre, vareps, rooted = (k.sem(f"{name}_{s}") for s in ("loaded", "stat", "centre", "vareps", "rooted"))
    with ExitStack() as ctx:
        stats = k.sb(ctx, f"{name}_stats", [P, B, 6], F32)
        ve = k.sb(ctx, f"{name}_ve", [P, B], F32)
        block = ctx.enter_context(nc.Block())

        @block.sync
        def _(sp):
            for dst, src in loads:
                sp.dma_start(dst, src).then_inc(loaded, 16)
            for i, (rows_, src, hi, lo, scale) in enumerate(chunks):
                wait(sp, low_done, i - 1)
                sp.dma_start(raw[0:rows_, i % 2, 0:src.shape[1]], src).then_inc(landed[i % 2], 16)

        @block.scalar
        def _(act):
            if loads:
                act.wait_ge(loaded, 16 * len(loads))
            for i, (rows_, src, hi, lo, scale) in enumerate(chunks):
                act.wait_ge(landed[i % 2], 16 * (i // 2 + 1))
                piece = raw[0:rows_, i % 2, 0:src.shape[1]]
                act.activation(hi, piece, ACT.Copy, scale=1.0 if scale is None else scale).then_inc(high_done, 1)

        @block.vector
        def _(dve):
            if loads:
                dve.wait_ge(loaded, 16 * len(loads))
            if rows:
                tiles, T, n = rows
                for t in range(n):
                    dve.bn_stats(stats[0:T, t, :], tiles[:, t, :]).then_inc(stat, 1)
                for t in range(n):
                    dve.wait_ge(stat, t + 1)
                    dve.bn_aggr(k.mean_var[0:T, t, :], stats[0:T, t, :]).then_inc(centre, 1)
                dve.wait_ge(centre, n)
                dve.tensor_scalar(ve[0:T, 0:n], k.mean_var[0:T, 0:n, 1], EPS, None, ALU.add).then_inc(vareps, 1)
            for i, (rows_, src, hi, lo, scale) in enumerate(chunks):
                dve.wait_ge(high_done, i + 1)
                piece = raw[0:rows_, i % 2, 0:src.shape[1]]
                dve.scalar_tensor_tensor(out=lo, in0=piece, scalar=1.0 if scale is None else scale,
                                         in1=hi.bitcast(F32), op0=ALU.mult, op1=ALU.subtract).then_inc(low_done, 1)

        @block.gpsimd
        def _(pool):
            if rows:
                tiles, T, n = rows
                pool.wait_ge(vareps, 1)
                pool.tensor_tensor(k.rstd[0:T, 0:n], ve[0:T, 0:n], k.half[0:T, 0:n], ALU.pow).then_inc(rooted, 1)
                pool.wait_ge(rooted, 1)


def small_head_attention(k, name, xt, NT, T, wq, wk, wv, wo, KC, head_of, v_at, mask,
                         bias_q=None, bias_k=None, bias_v=None, bias_o=None, store=None):
    nc, ps = k.nc, k.ps
    VN = wv[0].shape[2]
    scale = 32.0 ** -0.5
    names = ("z_ready", "zT_in_psum", "z_high", "z_low", "q_in_psum", "k_in_psum", "q_ready", "k_ready", "v_in_psum",
             "v_ready", "scores_in_psum", "scores_masked", "max_ready", "max_taken_off", "probs_ready", "sums_ready",
             "inverse_ready", "probsT_in_psum", "probsT_ready", "out_in_psum", "out_ready", "outT_in_psum",
             "out_high", "out_low", "y_in_psum", "y_biased", "x_done", "x_stored")
    s = {n: k.sem(f"{name}_{n}") for n in names}
    with ExitStack() as ctx:
        z = k.sb(ctx, f"{name}_z", [T, D], F32)
        zT = [k.sb(ctx, f"{name}_zT{i}", [P, DC, T], F32R) for i in range(2)]
        qT = k.sb(ctx, f"{name}_qT", [P, DC, T], F32)
        kT = k.sb(ctx, f"{name}_kT", [P, KC, T], F32)
        v = k.sb(ctx, f"{name}_v", [T, VN], F32)
        prob = k.sb(ctx, f"{name}_prob", [T, 4, 4, T], F32)
        probT = k.sb(ctx, f"{name}_probT", [T, 4, 4, T], F32)
        top = k.sb(ctx, f"{name}_top", [T, 4, 4], F32)
        total = k.sb(ctx, f"{name}_total", [T, 4, 4], F32)
        inverse = k.sb(ctx, f"{name}_inverse", [T, 4, 4], F32)
        o = k.sb(ctx, f"{name}_o", [T, D], F32)
        oT = [k.sb(ctx, f"{name}_oT{i}", [P, DC, T], F32R) for i in range(2)]
        block = ctx.enter_context(nc.Block())
        ident = k.ident

        def tiled(bank):
            return ps[bank][:, 0:4 * T].rearrange("p (c t) -> p c t", t=T)

        def part(w, c, cols):
            return [h[:, c, cols] for h in w]

        def over_loop(step):
            step(0, True, True)
            with block_engine[0].Fori(1, NT - 2) as t:
                step(t, True, True)
            step(NT - 2, True, False)
            step(NT - 1, False, False)

        block_engine = [None]

        @block.tensor
        def _(pe):
            def transpose_z(t):
                pe.wait_ge(s["z_ready"], t + 1)
                for c in range(DC):
                    mm = pe.transpose(tiled(6)[:, c, :], z[:, c * P:(c + 1) * P], ident[0:T, 0:T])
                mm.then_inc(s["zT_in_psum"], 1)

            def project_qk(t):
                pe.wait_ge(s["z_low"], t + 1)
                for w, n, bank, sem in ((wq, DC, 4, "q_in_psum"), (wk, KC, 5, "k_in_psum")):
                    for m in range(n):
                        for c in range(DC):
                            mm = product(pe, tiled(bank)[:, m, :], part(w, c, slice(m * P, (m + 1) * P)),
                                         part(zT, c, slice(0, T)), c == 0, c == DC - 1)
                    mm.then_inc(s[sem], 1)

            def project_v(t):
                if not (isinstance(t, int) and t == 0):
                    pe.wait_ge(s["out_ready"], t)
                for c in range(DC):
                    mm = product(pe, ps[7][0:T, 0:VN], part(zT, c, slice(0, T)), part(wv, c, slice(0, VN)),
                                 c == 0, c == DC - 1)
                mm.then_inc(s["v_in_psum"], 1)

            def step(t, one_more, two_more):
                pe.wait_ge(s["q_ready"], t + 1)
                pe.wait_ge(s["k_ready"], t + 1)
                wait(pe, s["scores_masked"], 4 * t)
                for c in range(4):
                    for r in range(4):
                        rows = slice(32 * r, 32 * r + 32)
                        mm = pe.matmul(tiled(r)[0:T, c, :], qT[rows, c, :], kT[rows, c if KC > 1 else 0, :],
                                       start=True, stop=True)
                mm.then_inc(s["scores_in_psum"], 1)
                if one_more:
                    project_qk(t + 1)
                for r in range(4):
                    pe.wait_ge(s["probs_ready"], 4 * t + r + 1)
                    if r >= 2:
                        pe.wait_ge(s["probsT_ready"], 4 * t + r - 1)
                    elif one_more:
                        pe.wait_ge(s[("q_ready", "k_ready")[r]], t + 2)
                    for c in range(4):
                        mm = pe.transpose(tiled(4 + r % 2)[0:T, c, :], prob[:, r, c, :], ident[0:T, 0:T])
                    mm.then_inc(s["probsT_in_psum"], 1)
                pe.wait_ge(s["v_ready"], t + 1)
                wait(pe, s["x_done"], t)
                for r in range(4):
                    pe.wait_ge(s["probsT_ready"], 4 * t + r + 1)
                    for c in range(4):
                        h = head_of(r, c)
                        mm = pe.matmul(ps[7][0:T, 32 * h:32 * h + 32], probT[:, r, c, :],
                                       v[:, v_at(r, c):v_at(r, c) + 32], start=True, stop=True)
                mm.then_inc(s["out_in_psum"], 1)
                if one_more:
                    project_v(t + 1)
                if two_more:
                    transpose_z(t + 2)
                    pe.wait_ge(s["z_low"], t + 3)
                pe.wait_ge(s["out_ready"], t + 1)
                for c in range(DC):
                    mm = pe.transpose(tiled(6)[:, c, :], o[:, c * P:(c + 1) * P], ident[0:T, 0:T])
                mm.then_inc(s["outT_in_psum"], 1)
                pe.wait_ge(s["out_low"], t + 1)
                if one_more:
                    pe.wait_ge(s["v_ready"], t + 2)
                for c in range(DC):
                    mm = product(pe, ps[7][0:T, :], part(oT, c, slice(0, T)), part(wo, c, slice(0, D)),
                                 c == 0, c == DC - 1)
                mm.then_inc(s["y_in_psum"], 1)

            transpose_z(0)
            project_qk(0)
            project_v(0)
            transpose_z(1)
            block_engine[0] = pe
            over_loop(step)

        @block.vector
        def _(dve):
            def normalise(t):
                wait(dve, s["zT_in_psum"], t)
                dve.tensor_scalar(z[:], xt[:, t, :], k.mean_var[0:T, t, 0:1], k.rstd[0:T, bass.ts(t, 1)],
                                  ALU.subtract, ALU.mult).then_inc(s["z_ready"], 1)

            def add_bias_v(t):
                if bias_v is not None:
                    dve.wait_ge(s["v_in_psum"], t + 1)
                    dve.tensor_tensor(v[:], ps[7][0:T, 0:VN], bias_v[:], ALU.add).then_inc(s["v_ready"], 1)

            def z_low(t):
                dve.wait_ge(s["z_high"], t + 1)
                dve.tensor_tensor(zT[1][:], tiled(6), zT[0][:].bitcast(F32), ALU.subtract).then_inc(s["z_low"], 1)

            def step(t, one_more, two_more):
                dve.wait_ge(s["scores_in_psum"], t + 1)
                for r in range(4):
                    dve.tensor_tensor(prob[:, r], tiled(r)[0:T], mask[:, None, :].to_broadcast([T, 4, T]),
                                      ALU.add).then_inc(s["scores_masked"], 1)
                for r in range(4):
                    dve.wait_ge(s["scores_masked"], 4 * t + r + 1)
                    dve.tensor_reduce(top[:, r], prob[:, r], AX.X, ALU.max).then_inc(s["max_ready"], 1)
                if two_more:
                    normalise(t + 2)
                for r in range(4):
                    dve.wait_ge(s["probs_ready"], 4 * t + r + 1)
                    dve.tensor_reduce(total[:, r], prob[:, r], AX.X, ALU.add).then_inc(s["sums_ready"], 1)
                dve.wait_ge(s["sums_ready"], 4 * t + 4)
                dve.reciprocal(inverse[:], total[:]).then_inc(s["inverse_ready"], 1)
                dve.wait_ge(s["inverse_ready"], t + 1)
                dve.wait_ge(s["out_in_psum"], t + 1)
                if head_of(0, 1) == 1:
                    heads = inverse[:].rearrange("p r c -> p (r c)")
                    dve.tensor_tensor(o[:].rearrange("p (h d) -> p h d", d=32),
                                      ps[7][0:T, :].rearrange("p (h d) -> p h d", d=32),
                                      heads[:, :, None].to_broadcast([T, 16, 32]), ALU.mult).then_inc(s["out_ready"], 1)
                else:
                    heads = inverse[:].rearrange("p r c -> p c r")
                    dve.tensor_tensor(o[:].rearrange("p (c r d) -> p c r d", r=4, d=32),
                                      ps[7][0:T, :].rearrange("p (c r d) -> p c r d", r=4, d=32),
                                      heads[:, :, :, None].to_broadcast([T, 4, 4, 32]),
                                      ALU.mult).then_inc(s["out_ready"], 1)
                if one_more:
                    add_bias_v(t + 1)
                if two_more:
                    z_low(t + 2)
                dve.wait_ge(s["out_high"], t + 1)
                dve.tensor_tensor(oT[1][:], tiled(6), oT[0][:].bitcast(F32), ALU.subtract).then_inc(s["out_low"], 1)
                dve.wait_ge(s["y_in_psum"], t + 1)
                dve.tensor_tensor(xt[:, t, :], ps[7][0:T, :], xt[:, t, :], ALU.add).then_inc(s["x_done"], 1)
                if bias_o is not None:
                    dve.wait_ge(s["x_done"], t + 1)
                    dve.tensor_tensor(xt[:, t, :], xt[:, t, :], bias_o[:], ALU.add).then_inc(s["y_biased"], 1)

            normalise(0)
            z_low(0)
            normalise(1)
            add_bias_v(0)
            z_low(1)
            block_engine[0] = dve
            over_loop(step)
            if bias_o is not None:
                dve.wait_ge(s["y_biased"], NT)

        @block.gpsimd
        def _(pool):
            def step(t, one_more, two_more):
                for r in range(4):
                    pool.wait_ge(s["max_ready"], 4 * t + r + 1)
                    pool.tensor_tensor(prob[:, r], prob[:, r], top[:, r, :, None].to_broadcast([T, 4, T]),
                                       ALU.subtract).then_inc(s["max_taken_off"], 1)
            block_engine[0] = pool
            over_loop(step)

        @block.scalar
        def _(act):
            def z_high(t):
                act.wait_ge(s["zT_in_psum"], t + 1)
                act.activation(zT[0][:], tiled(6), ACT.Copy).then_inc(s["z_high"], 1)

            def evacuate_qk(t):
                for ready, out, n, bank, bias, in_psum in (("q_ready", qT, DC, 4, bias_q, "q_in_psum"),
                                                           ("k_ready", kT, KC, 5, bias_k, "k_in_psum")):
                    act.wait_ge(s[in_psum], t + 1)
                    if bias is None:
                        act.activation(out[:], tiled(bank)[:, 0:n, :], ACT.Copy).then_inc(s[ready], 1)
                    else:
                        for m in range(n):
                            mm = act.activation(out[:, m, :], tiled(bank)[:, m, :], ACT.Identity,
                                                bias=bias[:, m:m + 1])
                        mm.then_inc(s[ready], 1)

            def evacuate_v(t):
                if bias_v is None:
                    act.wait_ge(s["v_in_psum"], t + 1)
                    act.activation(v[:], ps[7][0:T, 0:VN], ACT.Copy).then_inc(s["v_ready"], 1)

            def step(t, one_more, two_more):
                for r in range(4):
                    act.wait_ge(s["max_taken_off"], 4 * t + r + 1)
                    act.activation(prob[:, r], prob[:, r], ACT.Exp, scale=scale).then_inc(s["probs_ready"], 1)
                if one_more:
                    evacuate_qk(t + 1)
                for r in range(4):
                    act.wait_ge(s["probsT_in_psum"], 4 * t + r + 1)
                    act.activation(probT[:, r], tiled(4 + r % 2)[0:T], ACT.Copy).then_inc(s["probsT_ready"], 1)
                if one_more:
                    evacuate_v(t + 1)
                if two_more:
                    z_high(t + 2)
                act.wait_ge(s["outT_in_psum"], t + 1)
                act.activation(oT[0][:], tiled(6), ACT.Copy).then_inc(s["out_high"], 1)

            act.preload_act_table(ACT.Exp)
            z_high(0)
            evacuate_qk(0)
            evacuate_v(0)
            z_high(1)
            block_engine[0] = act
            over_loop(step)

        if store is not None:
            @block.sync
            def _(sp):
                with sp.Fori(0, NT) as t:
                    sp.wait_ge(s["x_done"], t + 1)
                    sp.dma_start(store[t], xt[:, t, :]).then_inc(s["x_stored"], 16)
                sp.wait_ge(s["x_stored"], 16 * NT)


IN_SCALE = 0
W_SCALE = 16
PROJ_SCALE = 20
LN_W, LN_B = 22, 26
HEAD_LN = 30
SMOOTH = 38
COLUMNS = 70
KEYS = 375
HALF_HEADS = 8
FP8_MAX = 448.0


def column_products(k, cols, packed, raw_scale, in_inverse, smooth_inverse, proj_scale, head_ln):
    nc = k.nc
    landed, products, squared = k.sem("cols_landed"), k.sem("cols_products"), k.sem("cols_squared")
    with nc.Block() as block:
        @block.sync
        def _(sp):
            sp.dma_start(cols[:], packed).then_inc(landed, 16)

        @block.vector
        def _(dve):
            dve.wait_ge(landed, 16)
            dve.tensor_tensor(raw_scale[:], cols[:, IN_SCALE:IN_SCALE + 16].rearrange("p (v c) -> p v c", c=DC),
                              cols[:, W_SCALE:W_SCALE + 4, None].to_broadcast([P, 4, DC]), ALU.mult).then_inc(products, 1)
            dve.reciprocal(in_inverse[:], cols[:, IN_SCALE:IN_SCALE + 16]).then_inc(products, 1)
            dve.reciprocal(smooth_inverse[:], cols[:, SMOOTH:SMOOTH + 32]).then_inc(products, 1)
            dve.tensor_tensor(proj_scale[:], cols[:, PROJ_SCALE:PROJ_SCALE + 1],
                              cols[:, PROJ_SCALE + 1:PROJ_SCALE + 2], ALU.mult).then_inc(products, 1)
            dve.tensor_copy(head_ln[:], cols[:, HEAD_LN:HEAD_LN + 8]).then_inc(products, 1)
            dve.wait_ge(products, 5)
            for n in (0, 4):
                dve.tensor_scalar(head_ln[:, n:n + 2], head_ln[:, n:n + 2], P ** -0.5, None, ALU.mult).then_inc(squared, 1)
            dve.wait_ge(squared, 2)


def quantise_inputs(k, x, cols, in_inverse, xq_dram):
    nc, ps = k.nc, k.ps
    G, GB = 4, B // 4
    names = ("z_ready", "stat", "centre", "vareps", "rooted", "z2_ready", "zT_in_psum", "ln_ready", "scaled", "clipped",
             "exponent", "magic", "shifted", "rounded", "stored")
    s = {n: k.sem(f"quant_{n}") for n in names}
    stored = [k.sem(f"quant_stored{v}") for v in range(2)]
    with ExitStack() as ctx:
        z = k.sb(ctx, "quant_z", [S, B, D], F32)
        stats = k.sb(ctx, "quant_stats", [S, B, 6], F32)
        mv = k.sb(ctx, "quant_mv", [S, B, 2], F32)
        ve = k.sb(ctx, "quant_ve", [S, B], F32)
        rstd = k.sb(ctx, "quant_rstd", [S, B], F32)
        ln = k.sb(ctx, "quant_ln", [P, GB, DC, S], F32)
        y = k.sb(ctx, "quant_y", [P, 2, GB, DC, S], BF16)
        expo = k.sb(ctx, "quant_expo", [P, 2, GB, DC, S], BF16)
        magic = k.sb(ctx, "quant_magic", [P, 2, GB, DC, S], BF16)
        shifted = k.sb(ctx, "quant_shifted", [P, 2, GB, DC, S], F32)
        q = k.sb(ctx, "quant_q", [P, 2, GB, DC, S], BF16)
        block = ctx.enter_context(nc.Block())

        @block.vector
        def _(dve):
            for b in range(B):
                dve.tensor_scalar(z[:, b, :], x[:, b, :], k.mean_var[0:S, b, 0:1], k.rstd[0:S, b:b + 1],
                                  ALU.subtract, ALU.mult).then_inc(s["z_ready"], 1)
            for b in range(B):
                dve.wait_ge(s["z_ready"], b + 1)
                dve.bn_stats(stats[:, b, :], z[:, b, :]).then_inc(s["stat"], 1)
            for b in range(B):
                dve.wait_ge(s["stat"], b + 1)
                dve.bn_aggr(mv[:, b, :], stats[:, b, :]).then_inc(s["centre"], 1)
            dve.wait_ge(s["centre"], B)
            dve.tensor_scalar(ve[:], mv[:, :, 1], EPS, None, ALU.add).then_inc(s["vareps"], 1)
            dve.wait_ge(s["rooted"], 1)
            for b in range(B):
                dve.tensor_scalar(z[:, b, :], z[:, b, :], mv[:, b, 0:1], rstd[:, b:b + 1],
                                  ALU.subtract, ALU.mult).then_inc(s["z2_ready"], 1)
            for g in range(G):
                dve.wait_ge(s["ln_ready"], 4 * (g + 1))
                for v in range(4):
                    n = 4 * g + v
                    i = n % 2
                    wait(dve, s["rounded"], n - 1)
                    for c in range(DC):
                        dve.tensor_scalar(y[:, i, :, c, :], ln[:, :, c, :], in_inverse[:, 4 * v + c:4 * v + c + 1],
                                          FP8_MAX, ALU.mult, ALU.min).then_inc(s["scaled"], 1)
                    dve.wait_ge(s["scaled"], 4 * n + 4)
                    dve.tensor_scalar(y[:, i], y[:, i], -FP8_MAX, None, ALU.max).then_inc(s["clipped"], 1)
                    dve.wait_ge(s["clipped"], n + 1)
                    dve.tensor_scalar(expo[:, i].bitcast(U16), y[:, i].bitcast(U16), 0x7F80, 0x7F80,
                                      ALU.bitwise_and, ALU.bitwise_and).then_inc(s["exponent"], 1)
                    dve.wait_ge(s["exponent"], n + 1)
                    dve.tensor_scalar(magic[:, i], expo[:, i], 2.0 ** -6, 1.5 * 2.0 ** 20,
                                      ALU.max, ALU.mult).then_inc(s["magic"], 1)
                    dve.wait_ge(s["magic"], n + 1)
                    dve.tensor_tensor(shifted[:, i], y[:, i], magic[:, i], ALU.add).then_inc(s["shifted"], 1)

        @block.gpsimd
        def _(pool):
            pool.wait_ge(s["vareps"], 1)
            pool.tensor_tensor(rstd[:], ve[:], k.half[0:S, 0:B], ALU.pow).then_inc(s["rooted"], 1)
            for n in range(4 * G):
                pool.wait_ge(s["shifted"], n + 1)
                if n >= 2:
                    pool.wait_ge(stored[n % 2], 16 * (n // 2))
                pool.tensor_tensor(q[:, n % 2], shifted[:, n % 2], magic[:, n % 2], ALU.subtract).then_inc(s["rounded"], 1)

        @block.tensor
        def _(pe):
            for g in range(G):
                wait(pe, s["ln_ready"], 4 * g)
                for j in range(GB):
                    b = GB * g + j
                    pe.wait_ge(s["z2_ready"], b + 1)
                    for c in range(DC):
                        mm = pe.transpose(ps[c][:, j * S:(j + 1) * S], z[:, b, c * P:(c + 1) * P], k.ident[0:S, 0:S])
                mm.then_inc(s["zT_in_psum"], 1)

        @block.scalar
        def _(act):
            for g in range(G):
                act.wait_ge(s["zT_in_psum"], g + 1)
                wait(act, s["scaled"], 16 * g)
                for c in range(DC):
                    act.activation(ln[:, :, c, :], ps[c][:, 0:GB * S].rearrange("p (b t) -> p b t", t=S), ACT.Identity,
                                   scale=cols[:, LN_W + c:LN_W + c + 1],
                                   bias=cols[:, LN_B + c:LN_B + c + 1]).then_inc(s["ln_ready"], 1)

        @block.sync
        def _(sp):
            for g in range(G):
                for v in range(4):
                    n = 4 * g + v
                    sp.wait_ge(s["rounded"], n + 1)
                    sp.dma_start(xq_dram[v, GB * g:GB * (g + 1)].rearrange("b p n -> p b n"),
                                 q[:, n % 2].rearrange("p b c t -> p b (c t)")).then_inc(stored[n % 2], 16)
            for v in range(2):
                sp.wait_ge(stored[v], 16 * 2 * G)


def normed_attention(k, name, x, xq_dram, kinds, wq, wk, wv, wo, ln_q, ln_k, smooth_inverse, head_ln, ctxT_dram=None):
    nc, ps = k.nc, k.ps
    own = ctxT_dram is None
    KT, KN = (1, S) if own else (3, KEYS // 3)
    NK = KT * KN
    H, GR = HALF_HEADS, HALF_HEADS // 2
    U = 2 + 2 * KT
    LU = 2 + KT
    KG = [[0, 1, 2, 3]] if own else [[0], [1], [2], [3]]
    TG = 2 + len(KG)
    TBANK = [6, 7, 5, 3, 6, 7][:TG]
    NV = len(kinds)
    names = ("xq_landed", "xq_ready", "ctx_landed", "ctx_high", "ctx_low", "unit_in_psum", "stat", "centre", "mean", "vareps",
             "rooted", "normed", "v_ready", "turned_in_psum", "turned_ready", "scores_in_psum", "minus_max", "exp_done",
             "inverse", "probs_ready", "probsT_in_psum", "probsT_ready", "cat_in_psum", "cat_scaled", "cat_clipped",
             "cat_exponent", "cat_magic", "cat_shifted", "cat_rounded", "y_in_psum", "x_done")
    s = {n: k.sem(f"{name}_{n}") for n in names}
    with ExitStack() as ctx:
        def sb(n, shape, dt=F32):
            return k.sb(ctx, f"{name}_{n}", shape, dt)
        xq_raw = sb("xq_raw", [P, NV, DC * S], BF16)
        xq = sb("xq", [P, NV, DC, S], F32R)
        if not own:
            ctx_raw = sb("ctx_raw", [P, DC, NK])
            ctx_part = [sb(f"ctx_part{i}", [P, DC, NK], F32R) for i in range(2)]
        stats = sb("stats", [P, LU, 4, 6])
        pair = sb("pair", [P, LU, 4, 4])
        mean = sb("mean", [P, LU, 4])
        ve = sb("ve", [P, LU, 4])
        rstd = sb("rstd", [P, LU, 4])
        qn = sb("qn", [S, H, P])
        kn = sb("kn", [KN, KT, GR, P])
        v = sb("v", [KN, KT, GR * P])
        qT = sb("qT", [P, H, S])
        kT = sb("kT", [P, GR, NK])
        neg_max = sb("neg_max", [S, H])
        total = sb("total", [S, H])
        inverse = sb("inverse", [S, H])
        prob = sb("prob", [S, 2, NK])
        probT = sb("probT", [KN, 2, KT, 2, S])
        scaled = sb("scaled", [P, H, S])
        clipped = sb("clipped", [P, H, S], BF16)
        expo = sb("expo", [P, H, S], BF16)
        magic = sb("magic", [P, H, S], BF16)
        catq = sb("catq", [P, H, S], F32R)
        block = ctx.enter_context(nc.Block())

        def over_loop(eng, step):
            step(0, True)
            with eng.Fori(1, B - 1) as b:
                step(b, True)
            step(B - 1, False)

        def unit_bank(n):
            return ps[n % 3]

        def unit_rows(n):
            return S if n < 2 else KN

        @block.sync
        def _(sp):
            def load(b):
                wait(sp, s["xq_ready"], b)
                sp.dma_start(xq_raw[:], xq_dram[kinds[0]:kinds[0] + NV, b, :, :].rearrange("v p n -> p v n"))\
                    .then_inc(s["xq_landed"], 16)
                if not own:
                    wait(sp, s["ctx_low"], b)
                    sp.dma_start(ctx_raw[:], ctxT_dram[b].rearrange("p (c n) -> p c n", c=DC)).then_inc(s["ctx_landed"], 16)
            load(0)
            with sp.Fori(1, B) as b:
                load(b)

        @block.gpsimd
        def _(pool):
            def root(b, n):
                rows = unit_rows(n)
                pool.wait_ge(s["vareps"], LU * b + n + 1)
                pool.tensor_tensor(rstd[0:rows, n, :], ve[0:rows, n, :], k.half[0:rows, 0:4], ALU.pow)\
                    .then_inc(s["rooted"], 1)

            def round_cat(b):
                pool.wait_ge(s["cat_magic"], b + 1)
                pool.tensor_tensor(scaled[:], clipped[:], magic[:], ALU.add).then_inc(s["cat_shifted"], 1)
                pool.wait_ge(s["cat_shifted"], b + 1)
                pool.tensor_tensor(catq[:], scaled[:], magic[:], ALU.subtract).then_inc(s["cat_rounded"], 1)

            def step(b, one_more):
                if one_more:
                    for n in range(LU):
                        root(b + 1, n)
                round_cat(b)
            for n in range(LU):
                root(0, n)
            over_loop(pool, step)

        @block.tensor
        def _(pe):
            def unit(b, n):
                bank = unit_bank(n)[0:unit_rows(n), :]
                if n == 0:
                    pe.wait_ge(s["xq_ready"], b + 1)
                if n == 2 and not own:
                    pe.wait_ge(s["ctx_low"], b + 1)
                if n >= 3:
                    pe.wait_ge(s["normed"], LU * b + n - 2) if n - 3 < LU else None
                else:
                    last = max(m for m in range(U) if m % 3 == n)
                    if last < LU:
                        wait(pe, s["normed"], LU * (b - 1) + last + 1)
                    else:
                        wait(pe, s["v_ready"], KT * (b - 1) + last - LU + 1)
                for c in range(DC):
                    if n < 2:
                        lhs, rhs = [xq[:, 0, c, :]], [h[:, c, n * 512:(n + 1) * 512] for h in wq]
                    else:
                        key = n < LU
                        j = (n - 2) % KT
                        rhs = [h[:, c, 0:512] for h in (wk if key else wv)]
                        lhs = [xq[:, 1 if key else 2, c, :]] if own else \
                            [h[:, c, j * KN:(j + 1) * KN] for h in ctx_part]
                    mm = product(pe, bank, lhs, rhs, c == 0, c == DC - 1)
                mm.then_inc(s["unit_in_psum"], 1)

            def turn(b):
                for g in range(2):
                    pe.wait_ge(s["normed"], LU * b + g + 1)
                    wait(pe, s["cat_scaled"], 2 * b)
                    for h in range(4):
                        mm = pe.transpose(ps[TBANK[g]][:, h * S:(h + 1) * S], qn[:, 4 * g + h, :], k.ident[0:S, 0:S])
                    mm.then_inc(s["turned_in_psum"], 1)
                pe.wait_ge(s["normed"], LU * b + LU)
                for n, groups in enumerate(KG):
                    if n >= 2:
                        pe.wait_ge(s["turned_ready"], TG * b + n - 1)
                    for i, g in enumerate(groups):
                        for j in range(KT):
                            at = (i * KT + j) * KN
                            mm = pe.transpose(ps[TBANK[2 + n]][:, at:at + KN], kn[:, j, g, :], k.ident[0:KN, 0:KN])
                    mm.then_inc(s["turned_in_psum"], 1)

            def project_out(b):
                pe.wait_ge(s["cat_rounded"], b + 1)
                for h in range(H):
                    mm = product(pe, ps[3][0:S, :], [catq[:, h, :]], [w[:, h, :] for w in wo], h == 0, h == H - 1)
                mm.then_inc(s["y_in_psum"], 1)

            def scores(b, h):
                if h == 0:
                    pe.wait_ge(s["turned_ready"], TG * b + TG)
                else:
                    pe.wait_ge(s["exp_done"], H * b + h - 1) if h >= 2 else None
                if h == 1:
                    wait(pe, s["x_done"], b)
                pe.matmul(ps[4 - h % 2][0:S, 0:NK], qT[:, h, :], kT[:, h // 2, :], start=True, stop=True)\
                    .then_inc(s["scores_in_psum"], 1)

            def turn_probs(b, h):
                pe.wait_ge(s["probs_ready"], H * b + h + 1)
                wait(pe, s["probsT_ready"], H * b + h)
                for j in range(KT):
                    mm = pe.transpose(ps[5][0:KN, j * S:(j + 1) * S], prob[:, h % 2, j * KN:(j + 1) * KN],
                                      k.ident[0:S, 0:S])
                mm.then_inc(s["probsT_in_psum"], 1)

            def weigh_values(b, pair):
                if pair == 0:
                    pe.wait_ge(s["v_ready"], KT * (b + 1))
                pe.wait_ge(s["probsT_ready"], H * b + 2 * pair + 2)
                at = (pair % 2) * 2 * S
                for j in range(KT):
                    mm = pe.matmul(ps[6 + pair // 2][:, at:at + 2 * S], v[:, j, pair * P:(pair + 1) * P],
                                   probT[:, pair % 2, j, :, :].rearrange("p a t -> p (a t)"),
                                   start=j == 0, stop=j == KT - 1)
                if pair % 2:
                    mm.then_inc(s["cat_in_psum"], 1)

            def step(b, one_more):
                turn(b)
                if not isinstance(b, int) or b > 0:
                    if 3 in TBANK:
                        pe.wait_ge(s["turned_ready"], TG * b + TBANK.index(3) + 1)
                    project_out(b - 1)
                scores(b, 0)
                for h in range(H):
                    if h + 1 < H:
                        scores(b, h + 1)
                    if one_more and h < U:
                        unit(b + 1, h)
                    turn_probs(b, h)
                    if h >= 2 and h % 2 == 0:
                        weigh_values(b, h // 2 - 1)
                weigh_values(b, GR - 1)

            pe_units = range(U)
            for n in pe_units:
                unit(0, n)
            over_loop(pe, step)
            project_out(B - 1)

        @block.scalar
        def _(act):
            def cast(b):
                act.wait_ge(s["xq_landed"], 16 * b + 16)
                wait(act, s["unit_in_psum"], U * b)
                act.activation(xq[:].rearrange("p v c t -> p v (c t)"), xq_raw[:], ACT.Copy).then_inc(s["xq_ready"], 1)

            def split_ctx(b):
                act.wait_ge(s["ctx_landed"], 16 * b + 16)
                wait(act, s["unit_in_psum"], U * b)
                act.activation(ctx_part[0][:], ctx_raw[:], ACT.Copy).then_inc(s["ctx_high"], 1)

            def take_values(b, before):
                for j in range(KT):
                    act.wait_ge(s["unit_in_psum"], U * b + LU + j + 1)
                    if j == 0 and before is not None:
                        act.wait_ge(s["cat_in_psum"], 2 * before + 2)
                    act.activation(v[:, j, :], unit_bank(LU + j)[0:KN, :], ACT.Copy).then_inc(s["v_ready"], 1)

            def take_turned(b):
                for n in range(TG):
                    act.wait_ge(s["turned_in_psum"], TG * b + n + 1)
                    if n < 2:
                        out = qT[:, 4 * n:4 * n + 4, :].rearrange("p h t -> p (h t)")
                        at = ln_q
                    else:
                        out = kT[:, KG[n - 2][0]:KG[n - 2][-1] + 1, :].rearrange("p g t -> p (g t)")
                        at = ln_k
                    act.activation(out, ps[TBANK[n]][:, 0:out.shape[1]], ACT.Identity, scale=head_ln[:, at:at + 1],
                                   bias=head_ln[:, at + 1:at + 2]).then_inc(s["turned_ready"], 1)

            def exponential(b, h):
                act.wait_ge(s["minus_max"], H * b + h + 1)
                if h >= 2:
                    act.wait_ge(s["probsT_in_psum"], H * b + h - 1)
                act.activation(prob[:, h % 2, :], ps[4 - h % 2][0:S, 0:NK], ACT.Exp, bias=neg_max[:, h:h + 1],
                               accum_out=total[:, h:h + 1]).then_inc(s["exp_done"], 1)

            def take_probsT(b, h):
                act.wait_ge(s["probsT_in_psum"], H * b + h + 1)
                act.activation(probT[:, (h // 2) % 2, :, h % 2, :], ps[5][0:KN, 0:KT * S].rearrange(
                    "p (j t) -> p j t", t=S), ACT.Copy).then_inc(s["probsT_ready"], 1)

            def step(b, one_more):
                take_turned(b)
                if one_more:
                    cast(b + 1)
                if one_more and not own:
                    split_ctx(b + 1)
                for h in range(H):
                    exponential(b, h)
                    if h:
                        take_probsT(b, h - 1)
                take_probsT(b, H - 1)
                if one_more:
                    take_values(b + 1, b)
            act.preload_act_table(ACT.Exp)
            cast(0)
            if not own:
                split_ctx(0)
            take_values(0, None)
            over_loop(act, step)

        @block.vector
        def _(dve):
            def split_ctx(b):
                dve.wait_ge(s["ctx_high"], b + 1)
                dve.tensor_tensor(ctx_part[1][:], ctx_raw[:], ctx_part[0][:].bitcast(F32), ALU.subtract)\
                    .then_inc(s["ctx_low"], 1)

            def measure(b, n):
                rows = unit_rows(n)
                dve.wait_ge(s["unit_in_psum"], U * b + n + 1)
                for h in range(4):
                    dve.bn_stats(stats[0:rows, n, h, :], unit_bank(n)[0:rows, h * P:(h + 1) * P]).then_inc(s["stat"], 1)
                dve.wait_ge(s["stat"], 4 * LU * b + 4 * n + 4)
                st = stats[0:rows, n, :, :]
                dve.tensor_tensor(pair[0:rows, n, 0, :], st[:, :, 1], st[:, :, 4], ALU.add).then_inc(s["centre"], 1)
                dve.tensor_tensor(pair[0:rows, n, 1, :], st[:, :, 1], st[:, :, 4], ALU.subtract).then_inc(s["centre"], 1)
                dve.tensor_tensor(pair[0:rows, n, 2, :], st[:, :, 2], st[:, :, 5], ALU.add).then_inc(s["centre"], 1)
                dve.wait_ge(s["centre"], 5 * (LU * b + n) + 3)
                dve.tensor_scalar(mean[0:rows, n, :], pair[0:rows, n, 0, :], 0.5, None, ALU.mult).then_inc(s["mean"], 1)
                dve.scalar_tensor_tensor(out=pair[0:rows, n, 3, :], in0=pair[0:rows, n, 1, :], scalar=0.25,
                                         in1=pair[0:rows, n, 1, :], op0=ALU.mult, op1=ALU.mult).then_inc(s["centre"], 1)
                dve.tensor_scalar(pair[0:rows, n, 2, :], pair[0:rows, n, 2, :], 1.0 / P, EPS,
                                  ALU.mult, ALU.add).then_inc(s["centre"], 1)
                dve.wait_ge(s["centre"], 5 * (LU * b + n) + 5)
                dve.tensor_tensor(ve[0:rows, n, :], pair[0:rows, n, 2, :], pair[0:rows, n, 3, :], ALU.add)\
                    .then_inc(s["vareps"], 1)

            def normalise(b, n):
                rows = unit_rows(n)
                dve.wait_ge(s["rooted"], LU * b + n + 1)
                dve.wait_ge(s["mean"], LU * b + n + 1)
                if n == 0:
                    wait(dve, s["turned_in_psum"], TG * b)
                for h in range(4):
                    out = qn[:, 4 * n + h, :] if n < 2 else kn[:, n - 2, h, :]
                    op = dve.tensor_scalar(out, unit_bank(n)[0:rows, h * P:(h + 1) * P], mean[0:rows, n, h:h + 1],
                                           rstd[0:rows, n, h:h + 1], ALU.subtract, ALU.mult)
                op.then_inc(s["normed"], 1)

            def top(b, h):
                dve.wait_ge(s["scores_in_psum"], H * b + h + 1)
                dve.tensor_reduce(neg_max[:, h:h + 1], ps[4 - h % 2][0:S, 0:NK], AX.X, ALU.max, negate=True)\
                    .then_inc(s["minus_max"], 1)

            def probabilities(b, h):
                dve.wait_ge(s["exp_done"], H * b + h + 1)
                dve.reciprocal(inverse[:, h:h + 1], total[:, h:h + 1]).then_inc(s["inverse"], 1)
                dve.wait_ge(s["inverse"], H * b + h + 1)
                dve.tensor_scalar(prob[:, h % 2, :], prob[:, h % 2, :], inverse[:, h:h + 1], None, ALU.mult)\
                    .then_inc(s["probs_ready"], 1)

            def scale_cat(b, i):
                dve.wait_ge(s["cat_in_psum"], 2 * b + i + 1)
                if i == 0:
                    wait(dve, s["cat_rounded"], b)
                dve.tensor_tensor(scaled[:, 4 * i:4 * i + 4, :], ps[6 + i][:, 0:4 * S].rearrange("p (h t) -> p h t", t=S),
                                  smooth_inverse[:, 4 * i:4 * i + 4, None].to_broadcast([P, 4, S]), ALU.mult)\
                    .then_inc(s["cat_scaled"], 1)

            def round_cat(b):
                dve.wait_ge(s["cat_scaled"], 2 * b + 2)
                dve.tensor_scalar(clipped[:], scaled[:], FP8_MAX, -FP8_MAX, ALU.min, ALU.max).then_inc(s["cat_clipped"], 1)
                dve.wait_ge(s["cat_clipped"], b + 1)
                dve.tensor_scalar(expo[:].bitcast(U16), clipped[:].bitcast(U16), 0x7F80, 0x7F80,
                                  ALU.bitwise_and, ALU.bitwise_and).then_inc(s["cat_exponent"], 1)
                dve.wait_ge(s["cat_exponent"], b + 1)
                dve.tensor_scalar(magic[:], expo[:], 2.0 ** -6, 1.5 * 2.0 ** 20, ALU.max, ALU.mult)\
                    .then_inc(s["cat_magic"], 1)

            def add_out(b):
                dve.wait_ge(s["y_in_psum"], b + 1)
                dve.tensor_tensor(x[:, b, :], ps[3][0:S, :], x[:, b, :], ALU.add).then_inc(s["x_done"], 1)

            def step(b, one_more):
                if one_more and not own:
                    split_ctx(b + 1)
                if not isinstance(b, int) or b > 0:
                    add_out(b - 1)
                top(b, 0)
                for h in range(H):
                    if h + 1 < H:
                        top(b, h + 1)
                    probabilities(b, h)
                    if one_more and h < LU:
                        measure(b + 1, h)
                    if one_more and 1 <= h <= LU:
                        normalise(b + 1, h - 1)
                    if h == 6:
                        scale_cat(b, 0)
                scale_cat(b, 1)
                round_cat(b)

            if not own:
                split_ctx(0)
            for n in range(LU):
                measure(0, n)
                normalise(0, n)
            over_loop(dve, step)
            add_out(B - 1)
            dve.wait_ge(s["x_done"], B)


def cross_attention_layer(k, x, io, x1, test=None):
    nc = k.nc
    xq_dram = nc.dram_tensor("L0_quantised_inputs", (4, B, P, DC * S), BF16, kind="Internal").ap()
    with ExitStack() as ctx:
        cols = k.sb(ctx, "cols", [P, COLUMNS], F32)
        raw_scale = k.sb(ctx, "raw_scale", [P, 4, DC], F32)
        in_inverse = k.sb(ctx, "in_inverse", [P, 16], F32)
        smooth_inverse = k.sb(ctx, "smooth_inverse", [P, 32], F32)
        proj_scale = k.sb(ctx, "proj_scale", [P, 1], F32)
        head_ln = k.sb(ctx, "head_ln", [P, 8], F32)
        column_products(k, cols, io["L0x_columns"], raw_scale, in_inverse, smooth_inverse, proj_scale, head_ln)
        prepare(k, "x0stats", None, [], rows=(x, S, B), loads=[(x[:], x1.rearrange("(s b) d -> s b d", b=B))])
        quantise_inputs(k, x, cols, in_inverse, xq_dram)
        k.recycle_semaphores()
        for phase in ("self", "cross"):
            for half in range(2):
                name = f"{phase}{half}"
                with ExitStack() as weights:
                    w = [k.sb(weights, f"{name}_w{i}", [P, DC, 2048], F32R) for i in range(2)]
                    wo = [k.sb(weights, f"{name}_wo{i}", [P, HALF_HEADS, D], F32R) for i in range(2)]
                    kinds = [0, 1, 2] if phase == "self" else [3]
                    src = io[f"L0x_{phase}"][half]
                    pieces = []
                    for c in range(DC):
                        parts = [(0, 1024, kinds[0])]
                        parts += [(1024, 1536, 1), (1536, 2048, 2)] if phase == "self" else [(1024, 2048, None)]
                        for a, b, kind in parts:
                            pieces.append((src[:, c * 2048 + a:c * 2048 + b], w[0][:, c, a:b], w[1][:, c, a:b],
                                           None if kind is None else raw_scale[:, kind, c:c + 1]))
                    first = (16 if phase == "cross" else 0) + HALF_HEADS * half
                    for h in range(0, HALF_HEADS, 2):
                        n = first + h
                        pieces.append((io["L0x_proj"][:, n * D:(n + 2) * D],
                                       wo[0][:, h:h + 2, :].rearrange("p h n -> p (h n)"),
                                       wo[1][:, h:h + 2, :].rearrange("p h n -> p (h n)"), proj_scale[:]))
                    with ExitStack() as stage:
                        raw = k.sb(stage, f"{name}_raw", [P, 2, 1024], F32)
                        prepare(k, f"{name}w", raw, pieces, width=1024)
                    normed_attention(k, name, x, xq_dram, kinds, [h[:, :, 0:1024] for h in w],
                                     [h[:, :, 1024:1536] for h in w], [h[:, :, 1536:2048] for h in w],
                                     [h[:] for h in wo], 0 if phase == "self" else 4, 2 if phase == "self" else 6,
                                     smooth_inverse[:, first:first + HALF_HEADS], head_ln,
                                     io["ctxT"] if phase == "cross" else None)
                k.recycle_semaphores()


EXPERTS = 8
HID = 448
HC, HP = 4, 112
TOKENS = B * S


def route(k, x, io, zT, scores_dram):
    nc, ps = k.nc, k.ps
    E = EXPERTS
    names = ("loaded", "gate_high", "gate_low", "z_ready", "zT_in_psum", "z_high", "z_low", "logitsT_in_psum",
             "logitsT_ready", "logits_in_psum", "exp_done", "chain", "chosen", "chosenT_in_psum", "chosenT_ready",
             "iota_ready", "stored")
    s = {n: k.sem(f"route_{n}") for n in names}
    with ExitStack() as ctx:
        def sb(n, shape, dt=F32):
            return k.sb(ctx, f"route_{n}", shape, dt)
        gate_raw = sb("gate_raw", [P, DC * E])
        gate = [sb(f"gate{i}", [P, DC, E], F32R) for i in range(2)]
        bias = sb("bias", [S, E])
        z = sb("z", [S, 2, D])
        logitsT = sb("logitsT", [E, B, S])
        rank = sb("rank", [S, E])
        a = sb("a", [S, B, E])
        score = sb("score", [S, B, E])
        biased = sb("biased", [S, B, E])
        hit = sb("hit", [S, B, E])
        first = sb("first", [S, B, E])
        row = sb("row", [S, B])
        row2 = sb("row2", [S, B])
        chosenT = sb("chosenT", [E, B, S])
        shared = sb("shared", [1, TOKENS])
        block = ctx.enter_context(nc.Block())

        @block.sync
        def _(sp):
            sp.dma_start(gate_raw[:], io["moe_gate"]).then_inc(s["loaded"], 16)
            sp.dma_start(bias[:], io["moe_bias"].to_broadcast([S, E])).then_inc(s["loaded"], 16)
            sp.wait_ge(s["iota_ready"], 2)
            sp.dma_start(scores_dram[E:E + 1, :], shared[:]).then_inc(s["stored"], 16)
            sp.wait_ge(s["chosenT_ready"], 4)
            sp.dma_start(scores_dram[0:E, :], chosenT[:].rearrange("e b t -> e (b t)")).then_inc(s["stored"], 16)
            sp.wait_ge(s["stored"], 32)

        @block.gpsimd
        def _(pool):
            pool.memset(shared[:], 1.0).then_inc(s["iota_ready"], 1)
            pool.iota(rank[:], pattern=[[-1, E]], base=E, channel_multiplier=0,
                      allow_small_or_imprecise_dtypes=True).then_inc(s["iota_ready"], 1)

        @block.scalar
        def _(act):
            act.wait_ge(s["loaded"], 32)
            act.activation(gate[0][:].rearrange("p c e -> p (c e)"), gate_raw[:], ACT.Copy).then_inc(s["gate_high"], 1)
            for b in range(B):
                act.wait_ge(s["zT_in_psum"], b + 1)
                act.activation(zT[0][:, :, b, :], ps[b % 2][:, 0:DC * S].rearrange("p (c t) -> p c t", t=S),
                               ACT.Copy).then_inc(s["z_high"], 1)
            for g in range(4):
                act.wait_ge(s["logitsT_in_psum"], g + 1)
                act.activation(logitsT[:, 4 * g:4 * g + 4, :].rearrange("e b t -> e (b t)"), ps[2 + g][0:E, 0:4 * S],
                               ACT.Copy).then_inc(s["logitsT_ready"], 1)
            act.wait_ge(s["chain"], 2)
            act.activation(a[:], a[:], ACT.Exp).then_inc(s["exp_done"], 1)
            for g in range(4):
                act.wait_ge(s["chosenT_in_psum"], g + 1)
                act.activation(chosenT[:, 4 * g:4 * g + 4, :].rearrange("e b t -> e (b t)"), ps[2 + g][0:E, 0:4 * S],
                               ACT.Copy).then_inc(s["chosenT_ready"], 1)

        @block.tensor
        def _(pe):
            for b in range(B):
                pe.wait_ge(s["z_ready"], b + 1)
                wait(pe, s["z_low"], b - 1)
                for c in range(DC):
                    mm = pe.transpose(ps[b % 2][:, c * S:(c + 1) * S], z[:, b % 2, c * P:(c + 1) * P], k.ident[0:S, 0:S])
                mm.then_inc(s["zT_in_psum"], 1)
            pe.wait_ge(s["z_low"], B)
            pe.wait_ge(s["gate_low"], 1)
            for g in range(4):
                for c in range(DC):
                    mm = product(pe, ps[2 + g][0:E, 0:4 * S], [h[:, c, :] for h in gate],
                                 [t[:, c, 4 * g:4 * g + 4, :].rearrange("p b t -> p (b t)") for t in zT],
                                 c == 0, c == DC - 1)
                mm.then_inc(s["logitsT_in_psum"], 1)
            for b in range(B):
                pe.wait_ge(s["logitsT_ready"], b // 4 + 1)
                mm = pe.transpose(ps[0][0:S, b * E:(b + 1) * E], logitsT[:, b, :], k.ident[0:E, 0:E])
            mm.then_inc(s["logits_in_psum"], 1)
            pe.wait_ge(s["chosen"], 1)
            for b in range(B):
                mm = pe.transpose(ps[2 + b // 4][0:E, (b % 4) * S:(b % 4 + 1) * S], first[:, b, :], k.ident[0:S, 0:S])
                if b % 4 == 3:
                    mm.then_inc(s["chosenT_in_psum"], 1)

        @block.vector
        def _(dve):
            for b in range(B):
                wait(dve, s["zT_in_psum"], b - 1)
                dve.tensor_scalar(z[:, b % 2, :], x[:, b, :], k.mean_var[0:S, b, 0:1], k.rstd[0:S, b:b + 1],
                                  ALU.subtract, ALU.mult).then_inc(s["z_ready"], 1)
                if b:
                    dve.wait_ge(s["z_high"], b)
                    dve.tensor_tensor(zT[1][:, :, b - 1, :],
                                      ps[(b - 1) % 2][:, 0:DC * S].rearrange("p (c t) -> p c t", t=S),
                                      zT[0][:, :, b - 1, :].bitcast(F32), ALU.subtract).then_inc(s["z_low"], 1)
            dve.wait_ge(s["z_high"], B)
            dve.tensor_tensor(zT[1][:, :, B - 1, :], ps[(B - 1) % 2][:, 0:DC * S].rearrange("p (c t) -> p c t", t=S),
                              zT[0][:, :, B - 1, :].bitcast(F32), ALU.subtract).then_inc(s["z_low"], 1)
            dve.wait_ge(s["gate_high"], 1)
            dve.tensor_tensor(gate[1][:].rearrange("p c e -> p (c e)"), gate_raw[:],
                              gate[0][:].rearrange("p c e -> p (c e)").bitcast(F32), ALU.subtract)\
                .then_inc(s["gate_low"], 1)

            done = [0]

            def after(op):
                op.then_inc(s["chain"], 1)
                done[0] += 1
                dve.wait_ge(s["chain"], done[0])

            def every(column):
                return column[:, :, None].to_broadcast([S, B, E])

            def each(line):
                return line[:, None, :].to_broadcast([S, B, E])
            dve.wait_ge(s["logits_in_psum"], 1)
            logits = ps[0][0:S, 0:B * E].rearrange("p (b e) -> p b e", e=E)
            after(dve.tensor_reduce(row[:], logits, AX.X, ALU.max))
            after(dve.tensor_tensor(a[:], logits, every(row), ALU.subtract))
            dve.wait_ge(s["exp_done"], 1)
            after(dve.tensor_reduce(row[:], a[:], AX.X, ALU.add))
            after(dve.reciprocal(row2[:], row[:]))
            after(dve.tensor_tensor(score[:], a[:], every(row2), ALU.mult))
            after(dve.tensor_tensor(biased[:], score[:], each(bias), ALU.add))
            dve.wait_ge(s["iota_ready"], 2)
            for turn in range(2):
                after(dve.tensor_reduce(row[:], biased[:], AX.X, ALU.max))
                after(dve.tensor_tensor(hit[:], biased[:], every(row), ALU.is_equal))
                after(dve.tensor_tensor(hit[:], hit[:], each(rank), ALU.mult))
                after(dve.tensor_reduce(row[:], hit[:], AX.X, ALU.max))
                out = first if turn == 0 else a
                after(dve.tensor_tensor(out[:], hit[:], every(row), ALU.is_equal))
                if turn == 0:
                    after(dve.scalar_tensor_tensor(out=biased[:].rearrange("p b e -> p (b e)"),
                                                   in0=first[:].rearrange("p b e -> p (b e)"), scalar=MASKED,
                                                   in1=biased[:].rearrange("p b e -> p (b e)"),
                                                   op0=ALU.mult, op1=ALU.add))
            after(dve.tensor_tensor(a[:], a[:], first[:], ALU.add))
            dve.tensor_tensor(first[:], a[:], score[:], ALU.mult).then_inc(s["chosen"], 1)


def expert_layer(k, x, io):
    nc, ps = k.nc, k.ps
    E1 = EXPERTS + 1
    G, GB = 4, B // 4
    N = GB * S
    scores_dram = nc.dram_tensor("expert_scores", (E1, TOKENS), F32, kind="Internal").ap()
    names = ("score_landed", "w1_landed", "w3_landed", "w2_landed", "up_high", "up_low", "down_high", "down_low", "up_in_psum",
             "gate_in_psum", "up_scaled", "gate_scaled", "silu_ready", "h_ready", "h_high", "h_low", "y_in_psum",
             "x_done")
    with ExitStack() as ctx:
        zT = [k.sb(ctx, f"moe_zT{i}", [P, DC, B, S], F32R) for i in range(2)]
        prepare(k, "moestats", None, [], rows=(x, S, B))
        route(k, x, io, zT, scores_dram)
        k.recycle_semaphores()
        s = {n: k.sem(f"moe_{n}") for n in names}

        def sb(n, shape, dt=F32):
            return k.sb(ctx, f"moe_{n}", shape, dt)
        raw_up = sb("raw_up", [P, 2, DC * HID])
        raw_down = sb("raw_down", [HP, HC * D])
        up = [sb(f"up{i}", [P, 2, DC, HID], F32R) for i in range(2)]
        down = [sb(f"down{i}", [HP, HC, D], F32R) for i in range(2)]
        score = sb("score", [HP, TOKENS])
        u = sb("u", [HP, 2, N])
        g3 = sb("g3", [HP, 2, N])
        silu = sb("silu", [HP, 2, N])
        h = sb("h", [HP, 2, N])
        hT = [sb(f"hT{i}", [HP, 2, HC, N], F32R) for i in range(2)]
        block = ctx.enter_context(nc.Block())

        def over_loop(eng, step):
            step(0)
            with eng.Fori(1, E1) as e:
                step(e)

        @block.sync
        def _(sp):
            def step(e):
                wait(sp, s["up_low"], e)
                sp.dma_start(raw_up[:, 0, :], io["moe_w1"][e]).then_inc(s["w1_landed"], 16)
                sp.dma_start(raw_up[:, 1, :], io["moe_w3"][e]).then_inc(s["w3_landed"], 16)
                wait(sp, s["down_low"], e)
                sp.dma_start(raw_down[:], io["moe_w2"][e]).then_inc(s["w2_landed"], 16)
                wait(sp, s["gate_scaled"], 16 * e)
                sp.dma_start(score[:], scores_dram[bass.ts(e, 1), :].to_broadcast([HP, TOKENS]))\
                    .then_inc(s["score_landed"], 16)
            over_loop(sp, step)

        @block.tensor
        def _(pe):
            def down_group(e, g):
                if g == 0:
                    pe.wait_ge(s["down_low"], e + 1)
                pe.wait_ge(s["h_low"], 16 * e + 4 * g + 4)
                for j in range(GB):
                    wait(pe, s["x_done"], 16 * e + 4 * (g - 1) + j + 1)
                    for c in range(HC):
                        mm = product(pe, ps[4 + j][0:S, :], [t[:, g % 2, c, j * S:(j + 1) * S] for t in hT],
                                     [w[:, c, :] for w in down], c == 0, c == HC - 1)
                    mm.then_inc(s["y_in_psum"], 1)

            def step(e):
                pe.wait_ge(s["up_low"], e + 1)
                for g in range(G):
                    for c in range(HC):
                        n = 16 * e + 4 * g + c
                        for i, sem, used in ((0, "up_in_psum", "up_scaled"), (1, "gate_in_psum", "gate_scaled")):
                            wait(pe, s[used], n - 1)
                            for kc in range(DC):
                                mm = product(pe, ps[2 * i + c % 2][0:HP, 0:N],
                                             [w[:, i, kc, c * HP:(c + 1) * HP] for w in up],
                                             [t[:, kc, GB * g:GB * (g + 1), :].rearrange("p b t -> p (b t)") for t in zT],
                                             kc == 0, kc == DC - 1)
                            mm.then_inc(s[sem], 1)
                    if g:
                        down_group(e, g - 1)
                down_group(e, G - 1)
            over_loop(pe, step)

        @block.scalar
        def _(act):
            def step(e):
                act.wait_ge(s["w1_landed"], 16 * e + 16)
                act.wait_ge(s["w3_landed"], 16 * e + 16)
                wait(act, s["gate_in_psum"], 16 * e)
                act.activation(up[0][:].rearrange("p i c n -> p (i c n)"), raw_up[:].rearrange("p i n -> p (i n)"),
                               ACT.Copy).then_inc(s["up_high"], 1)
                for g in range(G):
                    for c in range(HC):
                        n = 16 * e + 4 * g + c
                        act.wait_ge(s["up_scaled"], n + 1)
                        wait(act, s["h_ready"], n - 1)
                        act.activation(silu[:, c % 2, :], u[:, c % 2, :], ACT.Silu).then_inc(s["silu_ready"], 1)
                        if g == 0 and c == 0:
                            act.wait_ge(s["w2_landed"], 16 * e + 16)
                            wait(act, s["y_in_psum"], 16 * e)
                            act.activation(down[0][:].rearrange("p c n -> p (c n)"), raw_down[:], ACT.Copy)\
                                .then_inc(s["down_high"], 1)
                        act.wait_ge(s["h_ready"], n + 1)
                        if c == 0 and g >= 2:
                            act.wait_ge(s["y_in_psum"], 16 * e + 4 * (g - 1))
                        act.activation(hT[0][:, g % 2, c, :], h[:, c % 2, :], ACT.Copy).then_inc(s["h_high"], 1)
            act.preload_act_table(ACT.Silu)
            over_loop(act, step)

        @block.vector
        def _(dve):
            def step(e):
                dve.wait_ge(s["up_high"], e + 1)
                dve.tensor_tensor(up[1][:].rearrange("p i c n -> p (i c n)"), raw_up[:].rearrange("p i n -> p (i n)"),
                                  up[0][:].rearrange("p i c n -> p (i c n)").bitcast(F32), ALU.subtract)\
                    .then_inc(s["up_low"], 1)

                def add(g):
                    for j in range(GB):
                        dve.wait_ge(s["y_in_psum"], 16 * e + 4 * g + j + 1)
                        dve.tensor_tensor(x[:, GB * g + j, :], ps[4 + j][0:S, :], x[:, GB * g + j, :], ALU.add)\
                            .then_inc(s["x_done"], 1)
                for g in range(G):
                    for c in range(HC):
                        n = 16 * e + 4 * g + c
                        for out, bank, ready, used, src in ((u, 0, "up_scaled", "silu_ready", "up_in_psum"),
                                                            (g3, 2, "gate_scaled", "h_ready", "gate_in_psum")):
                            if g == 0 and c == 0 and bank == 0:
                                dve.wait_ge(s["score_landed"], 16 * e + 16)
                            wait(dve, s[used], n - 1)
                            dve.wait_ge(s[src], n + 1)
                            dve.tensor_tensor(out[:, c % 2, :], ps[bank + c % 2][0:HP, 0:N], score[:, g * N:(g + 1) * N],
                                              ALU.mult).then_inc(s[ready], 1)
                        if g == 0 and c == 0:
                            dve.wait_ge(s["down_high"], e + 1)
                            dve.tensor_tensor(down[1][:].rearrange("p c n -> p (c n)"), raw_down[:],
                                              down[0][:].rearrange("p c n -> p (c n)").bitcast(F32), ALU.subtract)\
                                .then_inc(s["down_low"], 1)
                    if g:
                        add(g - 1)
                add(G - 1)
            over_loop(dve, step)
            dve.wait_ge(s["x_done"], 16 * E1)

        @block.gpsimd
        def _(pool):
            def step(e):
                for g in range(G):
                    for c in range(HC):
                        n = 16 * e + 4 * g + c
                        pool.wait_ge(s["gate_scaled"], n + 1)
                        pool.wait_ge(s["silu_ready"], n + 1)
                        wait(pool, s["h_low"], n - 1)
                        pool.tensor_tensor(h[:, c % 2, :], g3[:, c % 2, :], silu[:, c % 2, :], ALU.mult)\
                            .then_inc(s["h_ready"], 1)
                        pool.wait_ge(s["h_high"], n + 1)
                        pool.tensor_tensor(hT[1][:, g % 2, c, :], h[:, c % 2, :], hT[0][:, g % 2, c, :].bitcast(F32),
                                           ALU.subtract).then_inc(s["h_low"], 1)
            over_loop(pool, step)
    k.recycle_semaphores()


def causal_mask(k, mask, done):
    with k.nc.Block() as block:
        @block.gpsimd
        def _(pool):
            pool.memset(mask[:], 0.0).then_inc(done, 1)
            pool.wait_ge(done, 1)
            pool.affine_select(out=mask[:], in_=mask[:], compare_op=ALU.is_ge, fill=MASKED, base=0,
                               pattern=[[-1, S]], channel_multiplier=1).then_inc(done, 1)
            pool.wait_ge(done, 2)


def flat(t):
    return t[:].rearrange("p c n -> p (c n)")


def second_attention_layer(k, x, io):
    with ExitStack() as ctx:
        w = [[k.sb(ctx, f"a1_{n}{i}", [P, DC, D], F32R) for i in range(2)] for n in ("q", "k", "v", "o")]
        mask = k.sb(ctx, "a1_mask", [S, S], F32)
        bias_cols = k.sb(ctx, "a1_bias_cols", [P, 2 * DC], F32)
        bias_v = k.sb(ctx, "a1_bias_v", [S, D], F32)
        bias_o = k.sb(ctx, "a1_bias_o", [S, D], F32)
        causal_mask(k, mask, k.sem("mask1_done"))
        with ExitStack() as stage:
            raw = k.sb(stage, "a1_raw", [P, 2, 2048], F32)
            prepare(k, "a1w", raw, [(io[f"L1_{n}"], flat(h), flat(lo), None) for n, (h, lo) in zip("qkvo", w)],
                    rows=(x, S, B), loads=[
                        (bias_cols[:], io["L1_bias_cols"]),
                        (bias_v[:], io["L1_bias_v"].to_broadcast([S, D])),
                        (bias_o[:], io["L1_bias_o"].to_broadcast([S, D]))])
        full = [[h[:] for h in part] for part in w]
        small_head_attention(k, "a1", x, B, S, *full, DC, lambda r, c: 4 * c + r, lambda r, c: 32 * (4 * c + r), mask,
                             bias_q=bias_cols[:, 0:DC], bias_k=bias_cols[:, DC:2 * DC], bias_v=bias_v, bias_o=bias_o)
        k.recycle_semaphores()


def wide_attention_layer(k, x, io):
    nc, ps = k.nc, k.ps
    JN, J = KEYS // 3, 3
    NK = KEYS + S
    names = ("z_ready", "zT_in_psum", "z_high", "z_low", "ctxT_landed", "ctx_landed", "q_in_psum", "k_in_psum",
             "v_in_psum", "q_ready", "k_ready", "v_ready", "scores_in_psum", "minus_max", "exp_done", "inverse_ready",
             "probsT_in_psum", "probsT_ready", "out_in_psum", "out_ready", "outT_in_psum", "out_high", "out_low",
             "y_in_psum", "x_done")
    with ExitStack() as ctx:
        def sb(n, shape, dt=F32):
            return k.sb(ctx, f"wide_{n}", shape, dt)
        wq, wk, wv, wo = [[sb(f"w{n}{i}", [P, DC, D], F32R) for i in range(2)] for n in "qkvo"]
        with ExitStack() as stage:
            raw = k.sb(stage, "wide_raw", [P, 2, 2048], F32)
            prepare(k, "widew", raw, [(io[f"L1x_{n}"], flat(h), flat(lo), None)
                                      for n, (h, lo) in zip("qkvo", (wq, wk, wv, wo))], rows=(x, S, B))
        k.recycle_semaphores()
        s = {n: k.sem(f"wide_{n}") for n in names}
        z = sb("z", [S, D])
        zT = [sb(f"zT{i}", [P, DC, S], F32R) for i in range(2)]
        ctxT = sb("ctxT", [P, DC, KEYS])
        ctx_rows = sb("ctx_rows", [JN, J, D])
        qT = sb("qT", [P, DC, S])
        kT = sb("kT", [P, DC, S])
        v = sb("v", [S, D])
        prob = sb("prob", [S, NK])
        probT = sb("probT", [JN, J + 1, S])
        neg_max = sb("neg_max", [S, 1])
        total = sb("total", [S, 1])
        inverse = sb("inverse", [S, 1])
        o = sb("o", [S, D])
        oT = [sb(f"oT{i}", [P, DC, S], F32R) for i in range(2)]
        block = ctx.enter_context(nc.Block())

        def over_loop(eng, step):
            step(0, True, True)
            with eng.Fori(1, B - 2) as b:
                step(b, True, True)
            step(B - 2, True, False)
            step(B - 1, False, False)

        def tiled(bank):
            return ps[bank][:, 0:DC * S].rearrange("p (c t) -> p c t", t=S)

        @block.sync
        def _(sp):
            def load(b):
                wait(sp, s["scores_in_psum"], b)
                sp.dma_start(ctxT[:], io["ctxT"][b].rearrange("p (c n) -> p c n", c=DC)).then_inc(s["ctxT_landed"], 16)
                wait(sp, s["out_in_psum"], b)
                sp.dma_start(ctx_rows[:], io["ctx"][b].rearrange("(j p) d -> p j d", p=JN)).then_inc(s["ctx_landed"], 16)
            load(0)
            with sp.Fori(1, B) as b:
                load(b)

        @block.tensor
        def _(pe):
            def transpose_z(b):
                pe.wait_ge(s["z_ready"], b + 1)
                for c in range(DC):
                    mm = pe.transpose(tiled(6)[:, c, :], z[:, c * P:(c + 1) * P], k.ident[0:S, 0:S])
                mm.then_inc(s["zT_in_psum"], 1)

            def project(b):
                pe.wait_ge(s["z_low"], b + 1)
                for w, bank, sem, ready in ((wq, 0, "q_in_psum", "q_ready"), (wk, 1, "k_in_psum", "k_ready")):
                    for m in range(DC):
                        for c in range(DC):
                            mm = product(pe, tiled(bank)[:, m, :], [h[:, c, m * P:(m + 1) * P] for h in w],
                                         [h[:, c, :] for h in zT], c == 0, c == DC - 1)
                    mm.then_inc(s[sem], 1)
                for c in range(DC):
                    mm = product(pe, ps[2][0:S, :], [h[:, c, :] for h in zT], [h[:, c, :] for h in wv],
                                 c == 0, c == DC - 1)
                mm.then_inc(s["v_in_psum"], 1)

            def step(b, one_more, two_more):
                pe.wait_ge(s["ctxT_landed"], 16 * b + 16)
                pe.wait_ge(s["q_ready"], b + 1)
                for c in range(DC):
                    pe.matmul(ps[3][0:S, 0:KEYS], qT[:, c, :], ctxT[:, c, :], start=c == 0, stop=c == DC - 1)
                pe.wait_ge(s["k_ready"], b + 1)
                for c in range(DC):
                    mm = pe.matmul(ps[3][0:S, KEYS:NK], qT[:, c, :], kT[:, c, :], start=c == 0, stop=c == DC - 1)
                mm.then_inc(s["scores_in_psum"], 1)
                if one_more:
                    pe.wait_ge(s["v_ready"], b + 1)
                    project(b + 1)
                pe.wait_ge(s["exp_done"], b + 1)
                for j in range(J + 1):
                    n = JN if j < J else S
                    mm = pe.transpose(tiled(4)[0:n, j, :], prob[:, j * JN:j * JN + n], k.ident[0:S, 0:S])
                mm.then_inc(s["probsT_in_psum"], 1)
                if two_more:
                    transpose_z(b + 2)
                pe.wait_ge(s["ctx_landed"], 16 * b + 16)
                pe.wait_ge(s["v_ready"], b + 1)
                pe.wait_ge(s["probsT_ready"], 2 * b + 2)
                for j in range(J + 1):
                    n = JN if j < J else S
                    mm = pe.matmul(ps[5][0:S, :], probT[0:n, j, :], ctx_rows[:, j, :] if j < J else v[:],
                                   start=j == 0, stop=j == J)
                mm.then_inc(s["out_in_psum"], 1)
                if two_more:
                    pe.wait_ge(s["z_low"], b + 3)
                pe.wait_ge(s["out_ready"], b + 1)
                for c in range(DC):
                    mm = pe.transpose(tiled(6)[:, c, :], o[:, c * P:(c + 1) * P], k.ident[0:S, 0:S])
                mm.then_inc(s["outT_in_psum"], 1)
                wait(pe, s["x_done"], b)
                pe.wait_ge(s["out_low"], b + 1)
                for c in range(DC):
                    mm = product(pe, ps[7][0:S, :], [h[:, c, :] for h in oT], [h[:, c, :] for h in wo],
                                 c == 0, c == DC - 1)
                mm.then_inc(s["y_in_psum"], 1)

            transpose_z(0)
            project(0)
            transpose_z(1)
            over_loop(pe, step)

        @block.scalar
        def _(act):
            def z_high(b):
                act.wait_ge(s["zT_in_psum"], b + 1)
                act.activation(zT[0][:], tiled(6), ACT.Copy).then_inc(s["z_high"], 1)

            def take(b):
                act.wait_ge(s["q_in_psum"], b + 1)
                act.activation(qT[:], tiled(0), ACT.Copy, scale=D ** -0.5).then_inc(s["q_ready"], 1)
                act.wait_ge(s["k_in_psum"], b + 1)
                act.activation(kT[:], tiled(1), ACT.Copy).then_inc(s["k_ready"], 1)

            def take_v(b, before):
                act.wait_ge(s["v_in_psum"], b + 1)
                if before is not None:
                    act.wait_ge(s["out_in_psum"], before + 1)
                act.activation(v[:], ps[2][0:S, :], ACT.Copy).then_inc(s["v_ready"], 1)

            def step(b, one_more, two_more):
                act.wait_ge(s["minus_max"], b + 1)
                act.activation(prob[:], ps[3][0:S, 0:NK], ACT.Exp, bias=neg_max[:], accum_out=total[:])\
                    .then_inc(s["exp_done"], 1)
                if one_more:
                    take(b + 1)
                act.wait_ge(s["probsT_in_psum"], b + 1)
                act.activation(probT[:, 0:J, :], tiled(4)[0:JN, 0:J, :], ACT.Copy).then_inc(s["probsT_ready"], 1)
                act.activation(probT[0:S, J, :], tiled(4)[0:S, J, :], ACT.Copy).then_inc(s["probsT_ready"], 1)
                if two_more:
                    z_high(b + 2)
                act.wait_ge(s["outT_in_psum"], b + 1)
                act.activation(oT[0][:], tiled(6), ACT.Copy).then_inc(s["out_high"], 1)
                if one_more:
                    take_v(b + 1, b)

            act.preload_act_table(ACT.Exp)
            z_high(0)
            take(0)
            take_v(0, None)
            z_high(1)
            over_loop(act, step)

        @block.vector
        def _(dve):
            def normalise(b):
                wait(dve, s["zT_in_psum"], b)
                dve.tensor_scalar(z[:], x[:, b, :], k.mean_var[0:S, b, 0:1], k.rstd[0:S, bass.ts(b, 1)],
                                  ALU.subtract, ALU.mult).then_inc(s["z_ready"], 1)

            def z_low(b):
                dve.wait_ge(s["z_high"], b + 1)
                dve.tensor_tensor(zT[1][:], tiled(6), zT[0][:].bitcast(F32), ALU.subtract).then_inc(s["z_low"], 1)

            def step(b, one_more, two_more):
                dve.wait_ge(s["scores_in_psum"], b + 1)
                dve.tensor_reduce(neg_max[:], ps[3][0:S, 0:NK], AX.X, ALU.max, negate=True).then_inc(s["minus_max"], 1)
                if two_more:
                    normalise(b + 2)
                    z_low(b + 2)
                dve.wait_ge(s["exp_done"], b + 1)
                dve.reciprocal(inverse[:], total[:]).then_inc(s["inverse_ready"], 1)
                dve.wait_ge(s["inverse_ready"], b + 1)
                dve.wait_ge(s["out_in_psum"], b + 1)
                dve.tensor_scalar(o[:], ps[5][0:S, :], inverse[:], None, ALU.mult).then_inc(s["out_ready"], 1)
                dve.wait_ge(s["out_high"], b + 1)
                dve.tensor_tensor(oT[1][:], tiled(6), oT[0][:].bitcast(F32), ALU.subtract).then_inc(s["out_low"], 1)
                dve.wait_ge(s["y_in_psum"], b + 1)
                dve.tensor_tensor(x[:, b, :], ps[7][0:S, :], x[:, b, :], ALU.add).then_inc(s["x_done"], 1)

            normalise(0)
            z_low(0)
            normalise(1)
            z_low(1)
            over_loop(dve, step)
            dve.wait_ge(s["x_done"], B)
    k.recycle_semaphores()


HIDDEN = 2048
MC = HIDDEN // P


def ternary(k, sources, signs, neg_scale, half):
    nc, ps = k.nc, k.ps
    N = DC * HIDDEN
    CH = 4
    W = N // CH
    names = ("sums_ready", "sum_ready", "total_in_psum", "mean_ready", "scale_ready", "above", "pattern")
    s = {n: k.sem(f"tern_{n}") for n in names}
    landed = [k.sem(f"tern_landed{i}") for i in range(2)]
    with ExitStack() as ctx:
        raw = k.sb(ctx, "tern_raw", [P, N], F32)
        above = k.sb(ctx, "tern_above", [P, 2, W], F32)
        sums = k.sb(ctx, "tern_sums", [P, 3, CH], F32)
        one = k.sb(ctx, "tern_sum", [P, 3], F32)
        mean = k.sb(ctx, "tern_mean", [P, 3], F32)
        block = ctx.enter_context(nc.Block())

        @block.sync
        def _(sp):
            for m, src in enumerate(sources):
                for i in range(CH):
                    wait(sp, s["pattern"], CH * (m - 1) + i + 1)
                    sp.dma_start(raw[:, i * W:(i + 1) * W], src[:, i * W:(i + 1) * W]).then_inc(landed[i % 2], 16)

        @block.vector
        def _(dve):
            for m in range(3):
                dve.wait_ge(landed[0], 16 * 2 * (m + 1))
                dve.wait_ge(landed[1], 16 * 2 * (m + 1))
                for i in range(CH):
                    dve.tensor_reduce(sums[:, m, i:i + 1], raw[:, i * W:(i + 1) * W], AX.X, ALU.add,
                                      apply_absolute_value=True).then_inc(s["sums_ready"], 1)
                dve.wait_ge(s["sums_ready"], CH * (m + 1))
                dve.tensor_reduce(one[:, m:m + 1], sums[:, m, :], AX.X, ALU.add).then_inc(s["sum_ready"], 1)
                dve.wait_ge(s["total_in_psum"], m + 1)
                dve.tensor_scalar(mean[:, m:m + 1], ps[0][:, m:m + 1], 1.0 / (P * N), 1e-8, ALU.mult, ALU.add)\
                    .then_inc(s["mean_ready"], 1)
                dve.wait_ge(s["mean_ready"], m + 1)
                dve.tensor_scalar(neg_scale[:, m:m + 1], mean[:, m:m + 1], -1.0, None, ALU.mult)\
                    .then_inc(s["scale_ready"], 1)
                dve.tensor_scalar(half[:, m, 0:1], mean[:, m:m + 1], 0.5, None, ALU.mult).then_inc(s["scale_ready"], 1)
                dve.tensor_scalar(half[:, m, 1:2], mean[:, m:m + 1], -0.5, None, ALU.mult).then_inc(s["scale_ready"], 1)
                dve.wait_ge(s["scale_ready"], 3 * (m + 1))
                for i in range(CH):
                    n = CH * m + i
                    wait(dve, s["pattern"], n - 1)
                    dve.tensor_scalar(above[:, i % 2, :], raw[:, i * W:(i + 1) * W], half[:, m, 0:1], None,
                                      ALU.is_gt).then_inc(s["above"], 1)
                    dve.wait_ge(s["above"], n + 1)
                    dve.scalar_tensor_tensor(out=signs[m][:, i * W:(i + 1) * W], in0=raw[:, i * W:(i + 1) * W],
                                             scalar=half[:, m, 1:2], in1=above[:, i % 2, :], op0=ALU.is_lt,
                                             op1=ALU.subtract).then_inc(s["pattern"], 1)
            dve.wait_ge(s["pattern"], 3 * CH)

        @block.tensor
        def _(pe):
            for m in range(3):
                pe.wait_ge(s["sum_ready"], m + 1)
                wait(pe, s["mean_ready"], m)
                pe.matmul(ps[0][:, m:m + 1], k.ones[:], one[:, m:m + 1], start=True, stop=True)\
                    .then_inc(s["total_in_psum"], 1)


def ternary_mlp_layer(k, x, io):
    nc, ps = k.nc, k.ps
    GB = 4
    G = B // GB
    names = ("z_ready", "zT_in_psum", "z_high", "z_low", "up_in_psum", "gate_in_psum", "silu_ready", "h_ready",
             "h_high", "h_low", "y_in_psum", "x_done", "x_stored")
    with ExitStack() as ctx:
        signs = [k.sb(ctx, f"signs_{n}", [P, DC * HIDDEN], F32R) for n in ("up", "gate", "down")]
        neg_scale = k.sb(ctx, "neg_scale", [P, 3], F32)
        half = k.sb(ctx, "half_scale", [P, 3, 2], F32)
        ternary(k, [io["L1f_up"], io["L1f_gate"], io["L1f_down"]], [w[:] for w in signs], neg_scale, half)
        prepare(k, "mlpstats", None, [], rows=(x, S, B))
        k.recycle_semaphores()
        s = {n: k.sem(f"mlp_{n}") for n in names}
        up_w, gate_w = [w[:].rearrange("p (c n) -> p c n", c=DC) for w in signs[0:2]]
        down_w = signs[2][:].rearrange("p (m n) -> p m n", m=MC)
        z = k.sb(ctx, "mlp_z", [S, 2, D], F32)
        zT = [k.sb(ctx, f"mlp_zT{i}", [P, DC, GB, S], F32R) for i in range(2)]
        silu = k.sb(ctx, "mlp_silu", [P, 2, GB * S], F32)
        h = k.sb(ctx, "mlp_h", [P, 2, GB * S], F32)
        hT = [k.sb(ctx, f"mlp_hT{i}", [P, 2, GB * S], F32R) for i in range(2)]
        block = ctx.enter_context(nc.Block())
        N = GB * S

        def over_loop(eng, step):
            step(0)
            with eng.Fori(1, G) as g:
                step(g)

        @block.tensor
        def _(pe):
            def down(g, m):
                n = MC * g + m
                pe.wait_ge(s["h_low"], n + 1)
                for j in range(GB):
                    if m == 0:
                        wait(pe, s["x_done"], GB * (g - 1) + j + 1)
                    mm = product(pe, ps[4 + j][0:S, :], [t[:, m % 2, j * S:(j + 1) * S] for t in hT],
                                 [down_w[:, m, :]], m == 0, m == MC - 1)
                mm.then_inc(s["y_in_psum"], 1)

            def step(g):
                for j in range(GB):
                    b = GB * g + j
                    pe.wait_ge(s["z_ready"], b + 1)
                    if j >= 2:
                        pe.wait_ge(s["z_low"], b - 1)
                    else:
                        wait(pe, s[("silu_ready")], MC * g)
                    for c in range(DC):
                        mm = pe.transpose(ps[j % 2][:, c * S:(c + 1) * S], z[:, j % 2, c * P:(c + 1) * P],
                                          k.ident[0:S, 0:S])
                    mm.then_inc(s["zT_in_psum"], 1)
                for m in range(MC):
                    n = MC * g + m
                    for w, bank, sem, used in ((up_w, 0, "up_in_psum", "silu_ready"),
                                               (gate_w, 2, "gate_in_psum", "h_ready")):
                        if m < 2 and bank == 0:
                            pe.wait_ge(s["z_low"], GB * g + GB)
                        else:
                            wait(pe, s[used], n - 1)
                        for c in range(DC):
                            mm = product(pe, ps[bank + m % 2][:, 0:N], [w[:, c, m * P:(m + 1) * P]],
                                         [t[:, c].rearrange("p b t -> p (b t)") for t in zT], c == 0, c == DC - 1)
                        mm.then_inc(s[sem], 1)
                    if m:
                        down(g, m - 1)
                down(g, MC - 1)
            over_loop(pe, step)

        @block.scalar
        def _(act):
            def step(g):
                for j in range(GB):
                    act.wait_ge(s["zT_in_psum"], GB * g + j + 1)
                    act.activation(zT[0][:, :, j, :], ps[j % 2][:, 0:DC * S].rearrange("p (c t) -> p c t", t=S),
                                   ACT.Copy).then_inc(s["z_high"], 1)

                def high(m):
                    act.wait_ge(s["h_ready"], MC * g + m + 1)
                    act.activation(hT[0][:, m % 2, :], h[:, m % 2, :], ACT.Copy).then_inc(s["h_high"], 1)
                for m in range(MC):
                    n = MC * g + m
                    act.wait_ge(s["up_in_psum"], n + 1)
                    act.activation(silu[:, m % 2, :], ps[m % 2][:, 0:N], ACT.Silu, scale=neg_scale[:, 0:1])\
                        .then_inc(s["silu_ready"], 1)
                    if m:
                        if m >= 3:
                            act.wait_ge(s["y_in_psum"], n - 2)
                        high(m - 1)
                act.wait_ge(s["y_in_psum"], MC * g + MC - 2)
                high(MC - 1)
            act.preload_act_table(ACT.Silu)
            over_loop(act, step)

        @block.vector
        def _(dve):
            def step(g):
                for j in range(GB):
                    b = GB * g + j
                    if j >= 2:
                        dve.wait_ge(s["zT_in_psum"], b - 1)
                    dve.tensor_scalar(z[:, j % 2, :], x[:, b, :], k.mean_var[0:S, b, 0:1], k.rstd[0:S, bass.ts(b, 1)],
                                      ALU.subtract, ALU.mult).then_inc(s["z_ready"], 1)
                    dve.wait_ge(s["z_high"], b + 1)
                    dve.tensor_tensor(zT[1][:, :, j, :], ps[j % 2][:, 0:DC * S].rearrange("p (c t) -> p c t", t=S),
                                      zT[0][:, :, j, :].bitcast(F32), ALU.subtract).then_inc(s["z_low"], 1)

                def low(m):
                    dve.wait_ge(s["h_high"], MC * g + m + 1)
                    dve.tensor_tensor(hT[1][:, m % 2, :], h[:, m % 2, :], hT[0][:, m % 2, :].bitcast(F32),
                                      ALU.subtract).then_inc(s["h_low"], 1)
                for m in range(MC):
                    n = MC * g + m
                    dve.wait_ge(s["gate_in_psum"], n + 1)
                    dve.wait_ge(s["silu_ready"], n + 1)
                    dve.scalar_tensor_tensor(out=h[:, m % 2, :], in0=ps[2 + m % 2][:, 0:N], scalar=neg_scale[:, 1:2],
                                             in1=silu[:, m % 2, :], op0=ALU.mult, op1=ALU.mult).then_inc(s["h_ready"], 1)
                    if m:
                        low(m - 1)
                low(MC - 1)
                dve.wait_ge(s["y_in_psum"], MC * g + MC)
                for j in range(GB):
                    dve.scalar_tensor_tensor(out=x[:, GB * g + j, :], in0=ps[4 + j][0:S, :], scalar=neg_scale[0:S, 2:3],
                                             in1=x[:, GB * g + j, :], op0=ALU.mult, op1=ALU.add).then_inc(s["x_done"], 1)
            over_loop(dve, step)

        @block.sync
        def _(sp):
            with sp.Fori(0, B) as b:
                sp.wait_ge(s["x_done"], b + 1)
                sp.dma_start(io["out"][b], x[:, b, :]).then_inc(s["x_stored"], 16)
            sp.wait_ge(s["x_stored"], 16 * B)
    k.recycle_semaphores()


def decoder(nc, io):
    with ExitStack() as top:
        k = Core(nc, top)
        constants(k)
        x1 = nc.dram_tensor("x_after_L0_attention", (S * B, D), F32, kind="Internal").ap()

        with ExitStack() as ctx:
            T, NT = P, S * B // P
            xt = k.sb(ctx, "x_by_position", [P, NT, D], F32)
            raw = k.sb(ctx, "a0_raw", [P, 2, 2048], F32)
            w = [k.sb(ctx, f"a0_qkv{i}", [P, DC, 768], F32R) for i in range(2)]
            wo = [k.sb(ctx, f"a0_o{i}", [P, DC, D], F32R) for i in range(2)]
            mask = k.sb(ctx, "a0_mask", [P, P], F32)
            block_causal_mask(k, mask)

            def flat(t):
                return t[:].rearrange("p c n -> p (c n)")
            prepare(k, "a0w", raw, [(io["L0_qkv"], flat(w[0]), flat(w[1]), None),
                                    (io["L0_proj"], flat(wo[0]), flat(wo[1]), None)],
                    rows=(xt, T, NT), loads=[(xt[:], io["x_by_position"].rearrange("(t p) d -> p t d", p=P))])
            small_head_attention(
                k, "a0", xt, NT, T, [h[:, :, 0:512] for h in w], [h[:, :, 512:640] for h in w],
                [h[:, :, 640:768] for h in w], [h[:] for h in wo], 1, lambda r, c: 4 * r + c, lambda r, c: 32 * r,
                mask, store=x1.rearrange("(t p) d -> t p d", p=P))

        k.recycle_semaphores()
        x = k.sb(top, "x", [S, B, D], F32)
        cross_attention_layer(k, x, io, x1)
        expert_layer(k, x, io)
        second_attention_layer(k, x, io)
        wide_attention_layer(k, x, io)
        ternary_mlp_layer(k, x, io)


def block_causal_mask(k, mask):
    nc = k.nc
    done = k.sem("mask0_done")
    with nc.Block() as block:
        @block.gpsimd
        def _(pool):
            pool.memset(mask[:], 0.0).then_inc(done, 1)
            pool.wait_ge(done, 1)
            pool.affine_select(out=mask[:], in_=mask[:], compare_op=ALU.is_ge, fill=MASKED, base=0,
                               pattern=[[-1, P]], channel_multiplier=1).then_inc(done, 1)
            pool.wait_ge(done, 2)
            pool.affine_select(out=mask[:], in_=mask[:], compare_op=ALU.is_ge, fill=MASKED, base=15,
                               pattern=[[B, P // B], [0, B]], channel_multiplier=-1).then_inc(done, 1)
            pool.wait_ge(done, 3)


def _columns(w):
    n_out, n_in = w.shape
    return w.T.reshape(n_in // 128, 128, n_out).transpose(1, 0, 2).reshape(128, -1)


def kernel(**inputs):
    import numpy as np
    import concourse.bacc as _bacc
    from concourse import mybir as _mybir
    from concourse.bass_utils import run_bass_kernel_spmd as _run

    a = {n: np.asarray(v) for n, v in inputs.items()}
    lay = {}
    lay["x_by_position"] = a["x"].transpose(1, 0, 2).reshape(1792, 512)
    g = a["L0_attn_weight_qkv"].reshape(4, 6, 32, 512)
    lay["L0_qkv"] = _columns(np.concatenate([g[:, 0:4].transpose(1, 0, 2, 3).reshape(512, 512),
                                             g[:, 4].reshape(128, 512), g[:, 5].reshape(128, 512)]))
    lay["L0_proj"] = _columns(a["L0_attn_weight_proj"])
    kx, vx = a["L0_xattn_w_kv_x"][:1024], a["L0_xattn_w_kv_x"][1024:]
    for phase, q, key, val in (("self", a["L0_xattn_wq"], a["L0_xattn_wk"], a["L0_xattn_wv"]),
                               ("cross", a["L0_xattn_wqx"], kx, vx)):
        lay[f"L0x_{phase}"] = np.stack([_columns(np.concatenate(
            [q[1024 * i:1024 * (i + 1)], key[512 * i:512 * (i + 1)], val[512 * i:512 * (i + 1)]])) for i in range(2)])
    lay["L0x_proj"] = _columns(a["L0_xattn_wproj"])

    def chunks(v):
        return v.reshape(-1, 128).T

    def everywhere(v):
        return np.broadcast_to(v.reshape(1, 1), (128, 1))
    lay["L0x_columns"] = np.concatenate(
        [chunks(a[f"L0_xattn_{n}_in_scale"]) for n in ("q", "k", "v", "qx")]
        + [everywhere(a[f"L0_xattn_{n}_scale"]) for n in ("wq", "wk", "wv", "wqx")]
        + [everywhere(a["L0_xattn_proj_in_scale"]), everywhere(a["L0_xattn_proj_w_scale"])]
        + [chunks(a["L0_xattn_ln_w"]), chunks(a["L0_xattn_ln_b"])]
        + [a[f"L0_xattn_{n}ln_{p}"].reshape(128, 1) for n in ("q", "k", "qx", "kx") for p in "wb"]
        + [chunks(a["L0_xattn_proj_smooth"])], axis=1)
    ctx = a["ctx_2048"]
    lay["ctxT"] = ctx.transpose(0, 2, 1).reshape(16, 4, 128, 375).transpose(0, 2, 1, 3).reshape(16, 128, 1500)
    lay["ctx"] = ctx
    for n in "qkvo":
        lay[f"L1_{n}"] = _columns(a[f"L1_attn_W{n}"])
        lay[f"L1x_{n}"] = _columns(a[f"L1_xattn_w{n}"])
    lay["L1_bias_cols"] = np.concatenate([chunks(a["L1_attn_bq"]), chunks(a["L1_attn_bk"])], axis=1)
    lay["L1_bias_v"], lay["L1_bias_o"] = a["L1_attn_bv"].reshape(1, 512), a["L1_attn_bo"].reshape(1, 512)
    lay["L1f_up"], lay["L1f_gate"], lay["L1f_down"] = (_columns(a[f"L1_ffn_W_{n}"]) for n in ("up", "gate", "down"))
    def up_columns(experts, own):
        w = np.concatenate([experts, own[None]])
        return w.reshape(9, 4, 128, 448).transpose(0, 2, 1, 3).reshape(9, 128, 1792)
    lay["moe_w1"] = up_columns(a["L0_ffn_w1"], a["L0_ffn_sw1"])
    lay["moe_w3"] = up_columns(a["L0_ffn_w3"], a["L0_ffn_sw3"])
    lay["moe_w2"] = np.concatenate([a["L0_ffn_w2"], a["L0_ffn_sw2"][None]]).reshape(9, 4, 112, 512)\
        .transpose(0, 2, 1, 3).reshape(9, 112, 2048)
    lay["moe_gate"] = _columns(a["L0_ffn_gate_w"].T)
    lay["moe_bias"] = a["L0_ffn_expert_bias"].reshape(1, 8)
    lay = {n: np.ascontiguousarray(v) for n, v in lay.items()}
    nc = _bacc.Bacc("TRN2", target_bir_lowering=False, num_devices=1)
    io = {n: nc.dram_tensor(f"in_{n}", v.shape, _mybir.dt.from_np(v.dtype), kind="ExternalInput").ap()
          for n, v in lay.items()}
    out = nc.dram_tensor("out", (16, 112, 512), _mybir.dt.float32, kind="ExternalOutput").ap()
    io["out"] = out
    decoder(nc, io)
    r = _run(nc, [{f"in_{n}": v for n, v in lay.items()}], core_ids=[0])
    return r.results[0]["out"]
```

```python
from contextlib import ExitStack

import concourse.bass as bass
from concourse import mybir
from concourse.alu_op_type import AluOpType as ALU

F32 = mybir.dt.float32
F32R = mybir.dt.float32r
BF16 = mybir.dt.bfloat16
U16 = mybir.dt.uint16
ACT = mybir.ActivationFunctionType
AX = mybir.AxisListType

P = 128
B = 16
S = 112
D = 512
DC = D // P
EPS = 1e-5
MASKED = -1e30


def wait(eng, sem, value):
    if isinstance(value, int) and value <= 0:
        return
    eng.wait_ge(sem, value)


def product(pe, out, lhs, rhs, first, last):
    pairs = [(lhs[0], rhs[0])]
    if len(lhs) > 1:
        pairs.append((lhs[1], rhs[0]))
    if len(rhs) > 1:
        pairs.append((lhs[0], rhs[1]))
    for n, (a, b) in enumerate(pairs):
        mm = pe.matmul(out, a, b, start=first and n == 0, stop=last and n == len(pairs) - 1)
    return mm


class Core:

    def __init__(self, nc, ctx):
        self.nc = nc
        self.sem_ctx = ctx.enter_context(ExitStack())
        self.sems = []
        self.ps = [ctx.enter_context(nc.psum_tensor(f"bank{i}", [P, 512], F32)) for i in range(8)]
        self.ident = self.sb(ctx, "ident", [P, P], F32)
        self.ones = self.sb(ctx, "ones", [P, P], F32)
        self.half = self.sb(ctx, "minus_half", [P, 32], F32)
        self.eps = self.sb(ctx, "eps", [P, 32], F32)
        self.mean_var = self.sb(ctx, "mean_var", [P, B, 2], F32)
        self.rstd = self.sb(ctx, "rstd", [P, B], F32)

    def sb(self, ctx, name, shape, dt):
        return ctx.enter_context(self.nc.sbuf_tensor(name, shape, dt))

    def sem(self, name):
        handle = self.sem_ctx.enter_context(self.nc.semaphore(name))
        self.sems.append(handle)
        return handle

    def recycle_semaphores(self):
        with self.nc.Block() as block:
            @block.gpsimd
            def _(pool):
                for handle in self.sems:
                    pool.sem_clear(handle)
        self.sem_ctx.close()
        self.sems = []


def constants(k):
    nc = k.nc
    zeroed = k.sem("const_zeroed")
    with nc.Block() as block:
        @block.gpsimd
        def _(pool):
            pool.memset(k.ident[:], 0.0).then_inc(zeroed, 1)
            pool.memset(k.ones[:], 1.0).then_inc(zeroed, 1)
            pool.memset(k.half[:], -0.5).then_inc(zeroed, 1)
            pool.memset(k.eps[:], EPS).then_inc(zeroed, 1)
            pool.wait_ge(zeroed, 1)
            pool.affine_select(out=k.ident[:], in_=k.ident[:], compare_op=ALU.not_equal, fill=1.0,
                               base=0, pattern=[[-1, P]], channel_multiplier=1).then_inc(zeroed, 1)
            pool.wait_ge(zeroed, 5)


def prepare(k, name, raw, pieces, rows=None, loads=()):
    nc = k.nc
    width = raw.shape[2] if pieces else 0
    chunks = []
    for src, hi, lo, scale in pieces:
        n = src.shape[1]
        for a in range(0, n, width):
            chunks.append((src.shape[0], src[:, a:min(n, a + width)], hi[:, a:min(n, a + width)],
                           lo[:, a:min(n, a + width)], scale))
    slots = raw.shape[1] if chunks else 0
    landed = [k.sem(f"{name}_raw_landed{i}") for i in range(slots)]
    high_done, low_done = k.sem(f"{name}_high_done"), k.sem(f"{name}_low_done")
    loaded, stat, centre, vareps, rooted = (k.sem(f"{name}_{s}") for s in ("loaded", "stat", "centre", "vareps", "rooted"))
    with ExitStack() as ctx:
        stats = k.sb(ctx, f"{name}_stats", [P, B, 6], F32)
        ve = k.sb(ctx, f"{name}_ve", [P, B], F32)
        block = ctx.enter_context(nc.Block())

        @block.sync
        def _(sp):
            for dst, src in loads:
                sp.dma_start(dst, src).then_inc(loaded, 16)
            for i, (rows_, src, hi, lo, scale) in enumerate(chunks):
                wait(sp, low_done, i - slots + 1)
                sp.dma_start(raw[0:rows_, i % slots, 0:src.shape[1]], src).then_inc(landed[i % slots], 16)

        @block.scalar
        def _(act):
            if loads:
                act.wait_ge(loaded, 16 * len(loads))
            for i, (rows_, src, hi, lo, scale) in enumerate(chunks):
                act.wait_ge(landed[i % slots], 16 * (i // slots + 1))
                piece = raw[0:rows_, i % slots, 0:src.shape[1]]
                act.activation(hi, piece, ACT.Copy, scale=1.0 if scale is None else scale).then_inc(high_done, 1)

        @block.vector
        def _(dve):
            if loads:
                dve.wait_ge(loaded, 16 * len(loads))
            if rows:
                tiles, T, n = rows
                for t in range(n):
                    dve.bn_stats(stats[0:T, t, :], tiles[:, t, :]).then_inc(stat, 1)
                for t in range(n):
                    dve.wait_ge(stat, t + 1)
                    dve.bn_aggr(k.mean_var[0:T, t, :], stats[0:T, t, :]).then_inc(centre, 1)
                dve.wait_ge(centre, n)
                dve.tensor_scalar(ve[0:T, 0:n], k.mean_var[0:T, 0:n, 1], EPS, None, ALU.add).then_inc(vareps, 1)
            for i, (rows_, src, hi, lo, scale) in enumerate(chunks):
                dve.wait_ge(high_done, i + 1)
                piece = raw[0:rows_, i % slots, 0:src.shape[1]]
                dve.scalar_tensor_tensor(out=lo, in0=piece, scalar=1.0 if scale is None else scale,
                                         in1=hi.bitcast(F32), op0=ALU.mult, op1=ALU.subtract).then_inc(low_done, 1)

        @block.gpsimd
        def _(pool):
            if rows:
                tiles, T, n = rows
                pool.wait_ge(vareps, 1)
                pool.tensor_tensor(k.rstd[0:T, 0:n], ve[0:T, 0:n], k.half[0:T, 0:n], ALU.pow).then_inc(rooted, 1)
                pool.wait_ge(rooted, 1)


def small_head_attention(k, name, xt, NT, T, wq, wk, wv, wo, KC, head_of, v_at, mask,
                         bias_q=None, bias_k=None, bias_v=None, bias_o=None, store=None):
    nc, ps = k.nc, k.ps
    VN = wv[0].shape[2]
    scale = 32.0 ** -0.5
    names = ("z_ready", "zT_in_psum", "z_high", "z_low", "q_in_psum", "k_in_psum", "q_taken", "k_taken",
             "qT_in_psum", "kT_in_psum", "q_ready", "k_ready", "v_in_psum",
             "v_ready", "scores_in_psum", "scores_masked", "max_ready", "max_taken_off", "probs_ready", "sums_ready",
             "inverse_ready", "probsT_in_psum", "probsT_ready", "out_in_psum", "out_ready", "outT_in_psum",
             "out_high", "out_low", "y_in_psum", "y_biased", "x_done", "x_stored")
    s = {n: k.sem(f"{name}_{n}") for n in names}
    with ExitStack() as ctx:
        z = k.sb(ctx, f"{name}_z", [T, D], F32)
        zT = [k.sb(ctx, f"{name}_zT{i}", [P, DC, T], F32R) for i in range(2)]
        q = k.sb(ctx, f"{name}_q", [T, D], F32)
        key = k.sb(ctx, f"{name}_key", [T, KC * P], F32)
        qT = k.sb(ctx, f"{name}_qT", [P, DC, T], F32)
        kT = k.sb(ctx, f"{name}_kT", [P, KC, T], F32)
        v = k.sb(ctx, f"{name}_v", [T, VN], F32)
        prob = k.sb(ctx, f"{name}_prob", [T, 4, 4, T], F32)
        probT = k.sb(ctx, f"{name}_probT", [T, 4, 4, T], F32)
        top = k.sb(ctx, f"{name}_top", [T, 4, 4], F32)
        total = k.sb(ctx, f"{name}_total", [T, 4, 4], F32)
        inverse = k.sb(ctx, f"{name}_inverse", [T, 4, 4], F32)
        o = k.sb(ctx, f"{name}_o", [T, D], F32)
        oT = [k.sb(ctx, f"{name}_oT{i}", [P, DC, T], F32R) for i in range(2)]
        block = ctx.enter_context(nc.Block())
        ident = k.ident

        def tiled(bank):
            return ps[bank][:, 0:4 * T].rearrange("p (c t) -> p c t", t=T)

        def part(w, c, cols):
            return [h[:, c, cols] for h in w]

        def over_loop(step):
            step(0, True, True)
            with block_engine[0].Fori(1, NT - 2) as t:
                step(t, True, True)
            step(NT - 2, True, False)
            step(NT - 1, False, False)

        block_engine = [None]

        @block.tensor
        def _(pe):
            def transpose_z(t):
                pe.wait_ge(s["z_ready"], t + 1)
                for c in range(DC):
                    mm = pe.transpose(tiled(5)[:, c, :], z[:, c * P:(c + 1) * P], ident[0:T, 0:T])
                mm.then_inc(s["zT_in_psum"], 1)

            def project_qk(t):
                pe.wait_ge(s["z_low"], t + 1)
                for w, n, bank, sem in ((wq, D, 4, "q_in_psum"), (wk, KC * P, 5, "k_in_psum")):
                    for c in range(DC):
                        mm = product(pe, ps[bank][0:T, 0:n], part(zT, c, slice(0, T)), part(w, c, slice(0, n)),
                                     c == 0, c == DC - 1)
                    mm.then_inc(s[sem], 1)

            def transpose_q(t):
                pe.wait_ge(s["q_taken"], t + 1)
                for c in range(DC):
                    mm = pe.transpose(tiled(6)[:, c, :], q[:, c * P:(c + 1) * P], ident[0:T, 0:T])
                mm.then_inc(s["qT_in_psum"], 1)

            def transpose_k(t):
                pe.wait_ge(s["k_taken"], t + 1)
                for c in range(KC):
                    mm = pe.transpose(tiled(4)[:, c, :], key[:, c * P:(c + 1) * P], ident[0:T, 0:T])
                mm.then_inc(s["kT_in_psum"], 1)

            def project_v(t):
                pe.wait_ge(s["q_ready"], t + 1)
                for c in range(DC):
                    mm = product(pe, ps[6][0:T, 0:VN], part(zT, c, slice(0, T)), part(wv, c, slice(0, VN)),
                                 c == 0, c == DC - 1)
                mm.then_inc(s["v_in_psum"], 1)

            def transpose_out(t):
                pe.wait_ge(s["out_ready"], t + 1)
                for c in range(DC):
                    mm = pe.transpose(tiled(6)[:, c, :], o[:, c * P:(c + 1) * P], ident[0:T, 0:T])
                mm.then_inc(s["outT_in_psum"], 1)

            def project_out(t):
                pe.wait_ge(s["out_low"], t + 1)
                for c in range(DC):
                    mm = product(pe, ps[7][0:T, :], part(oT, c, slice(0, T)), part(wo, c, slice(0, D)),
                                 c == 0, c == DC - 1)
                mm.then_inc(s["y_in_psum"], 1)

            def step(t, one_more, two_more):
                first = isinstance(t, int) and t == 0
                pe.wait_ge(s["q_ready"], t + 1)
                pe.wait_ge(s["k_ready"], t + 1)
                wait(pe, s["scores_masked"], 4 * t)
                for c in range(4):
                    for r in range(4):
                        rows = slice(32 * r, 32 * r + 32)
                        mm = pe.matmul(tiled(r)[0:T, c, :], qT[rows, c, :], kT[rows, c if KC > 1 else 0, :],
                                       start=True, stop=True)
                mm.then_inc(s["scores_in_psum"], 1)
                pe.wait_ge(s["v_ready"], t + 1)
                if not first:
                    transpose_out(t - 1)
                if one_more:
                    project_qk(t + 1)
                    wait(pe, s["out_low"], t)
                    transpose_q(t + 1)
                if not first:
                    project_out(t - 1)
                if one_more:
                    transpose_k(t + 1)
                for r in range(4):
                    pe.wait_ge(s["probs_ready"], 4 * t + r + 1)
                    if r >= 2:
                        pe.wait_ge(s["probsT_ready"], 4 * t + r - 1)
                    elif r == 1 and one_more:
                        pe.wait_ge(s["k_ready"], t + 2)
                    for c in range(4):
                        mm = pe.transpose(tiled(5 - r % 2)[0:T, c, :], prob[:, r, c, :], ident[0:T, 0:T])
                    mm.then_inc(s["probsT_in_psum"], 1)
                wait(pe, s["x_done"], t)
                for r in range(4):
                    pe.wait_ge(s["probsT_ready"], 4 * t + r + 1)
                    for c in range(4):
                        h = head_of(r, c)
                        mm = pe.matmul(ps[7][0:T, 32 * h:32 * h + 32], probT[:, r, c, :],
                                       v[:, v_at(r, c):v_at(r, c) + 32], start=True, stop=True)
                mm.then_inc(s["out_in_psum"], 1)
                if one_more:
                    project_v(t + 1)
                if two_more:
                    transpose_z(t + 2)

            transpose_z(0)
            project_qk(0)
            transpose_q(0)
            transpose_k(0)
            project_v(0)
            transpose_z(1)
            block_engine[0] = pe
            over_loop(step)
            transpose_out(NT - 1)
            project_out(NT - 1)

        @block.vector
        def _(dve):
            def normalise(t):
                wait(dve, s["zT_in_psum"], t)
                dve.tensor_scalar(z[:], xt[:, t, :], k.mean_var[0:T, t, 0:1], k.rstd[0:T, bass.ts(t, 1)],
                                  ALU.subtract, ALU.mult).then_inc(s["z_ready"], 1)

            def add_bias_v(t):
                if bias_v is not None:
                    dve.wait_ge(s["v_in_psum"], t + 1)
                    dve.tensor_tensor(v[:], ps[6][0:T, 0:VN], bias_v[:], ALU.add).then_inc(s["v_ready"], 1)

            def z_low(t):
                dve.wait_ge(s["z_high"], t + 1)
                dve.tensor_tensor(zT[1][:], tiled(5), zT[0][:].bitcast(F32), ALU.subtract).then_inc(s["z_low"], 1)

            def out_low(t):
                dve.wait_ge(s["out_high"], t + 1)
                dve.tensor_tensor(oT[1][:], tiled(6), oT[0][:].bitcast(F32), ALU.subtract).then_inc(s["out_low"], 1)

            def add_out(t):
                dve.wait_ge(s["y_in_psum"], t + 1)
                dve.tensor_tensor(xt[:, t, :], ps[7][0:T, :], xt[:, t, :], ALU.add).then_inc(s["x_done"], 1)
                if bias_o is not None:
                    dve.wait_ge(s["x_done"], t + 1)
                    dve.tensor_tensor(xt[:, t, :], xt[:, t, :], bias_o[:], ALU.add).then_inc(s["y_biased"], 1)

            def step(t, one_more, two_more):
                first = isinstance(t, int) and t == 0
                dve.wait_ge(s["scores_in_psum"], t + 1)
                for r in range(4):
                    dve.tensor_tensor(prob[:, r], tiled(r)[0:T], mask[:, None, :].to_broadcast([T, 4, T]),
                                      ALU.add).then_inc(s["scores_masked"], 1)
                for r in range(4):
                    dve.wait_ge(s["scores_masked"], 4 * t + r + 1)
                    dve.tensor_reduce(top[:, r], prob[:, r], AX.X, ALU.max).then_inc(s["max_ready"], 1)
                if not first:
                    out_low(t - 1)
                if two_more:
                    normalise(t + 2)
                for r in range(4):
                    dve.wait_ge(s["probs_ready"], 4 * t + r + 1)
                    dve.tensor_reduce(total[:, r], prob[:, r], AX.X, ALU.add).then_inc(s["sums_ready"], 1)
                dve.wait_ge(s["sums_ready"], 4 * t + 4)
                dve.reciprocal(inverse[:], total[:]).then_inc(s["inverse_ready"], 1)
                if not first:
                    add_out(t - 1)
                dve.wait_ge(s["inverse_ready"], t + 1)
                dve.wait_ge(s["out_in_psum"], t + 1)
                if head_of(0, 1) == 1:
                    heads = inverse[:].rearrange("p r c -> p (r c)")
                    dve.tensor_tensor(o[:].rearrange("p (h d) -> p h d", d=32),
                                      ps[7][0:T, :].rearrange("p (h d) -> p h d", d=32),
                                      heads[:, :, None].to_broadcast([T, 16, 32]), ALU.mult).then_inc(s["out_ready"], 1)
                else:
                    heads = inverse[:].rearrange("p r c -> p c r")
                    dve.tensor_tensor(o[:].rearrange("p (c r d) -> p c r d", r=4, d=32),
                                      ps[7][0:T, :].rearrange("p (c r d) -> p c r d", r=4, d=32),
                                      heads[:, :, :, None].to_broadcast([T, 4, 4, 32]),
                                      ALU.mult).then_inc(s["out_ready"], 1)
                if one_more:
                    add_bias_v(t + 1)
                if two_more:
                    z_low(t + 2)

            normalise(0)
            z_low(0)
            normalise(1)
            add_bias_v(0)
            z_low(1)
            block_engine[0] = dve
            over_loop(step)
            out_low(NT - 1)
            add_out(NT - 1)
            if bias_o is not None:
                dve.wait_ge(s["y_biased"], NT)

        @block.gpsimd
        def _(pool):
            def step(t, one_more, two_more):
                for r in range(4):
                    pool.wait_ge(s["max_ready"], 4 * t + r + 1)
                    pool.tensor_tensor(prob[:, r], prob[:, r], top[:, r, :, None].to_broadcast([T, 4, T]),
                                       ALU.subtract).then_inc(s["max_taken_off"], 1)
            block_engine[0] = pool
            over_loop(step)

        @block.scalar
        def _(act):
            def z_high(t):
                act.wait_ge(s["zT_in_psum"], t + 1)
                act.activation(zT[0][:], tiled(5), ACT.Copy).then_inc(s["z_high"], 1)

            def take_q(t):
                act.wait_ge(s["q_in_psum"], t + 1)
                act.activation(q[:], ps[4][0:T, :], ACT.Copy).then_inc(s["q_taken"], 1)

            def take_k(t):
                act.wait_ge(s["k_in_psum"], t + 1)
                act.activation(key[:], ps[5][0:T, 0:KC * P], ACT.Copy).then_inc(s["k_taken"], 1)

            def evacuate_qk(t):
                for ready, out, n, bank, bias, in_psum in (("q_ready", qT, DC, 6, bias_q, "qT_in_psum"),
                                                           ("k_ready", kT, KC, 4, bias_k, "kT_in_psum")):
                    act.wait_ge(s[in_psum], t + 1)
                    if bias is None:
                        act.activation(out[:], tiled(bank)[:, 0:n, :], ACT.Copy).then_inc(s[ready], 1)
                    else:
                        for m in range(n):
                            mm = act.activation(out[:, m, :], tiled(bank)[:, m, :], ACT.Identity,
                                                bias=bias[:, m:m + 1])
                        mm.then_inc(s[ready], 1)

            def evacuate_v(t):
                if bias_v is None:
                    act.wait_ge(s["v_in_psum"], t + 1)
                    act.activation(v[:], ps[6][0:T, 0:VN], ACT.Copy).then_inc(s["v_ready"], 1)

            def out_high(t):
                act.wait_ge(s["outT_in_psum"], t + 1)
                act.activation(oT[0][:], tiled(6), ACT.Copy).then_inc(s["out_high"], 1)

            def step(t, one_more, two_more):
                if not (isinstance(t, int) and t == 0):
                    out_high(t - 1)
                if one_more:
                    take_q(t + 1)
                for r in range(4):
                    if r == 2 and one_more:
                        take_k(t + 1)
                    act.wait_ge(s["max_taken_off"], 4 * t + r + 1)
                    act.activation(prob[:, r], prob[:, r], ACT.Exp, scale=scale).then_inc(s["probs_ready"], 1)
                if one_more:
                    evacuate_qk(t + 1)
                for r in range(4):
                    act.wait_ge(s["probsT_in_psum"], 4 * t + r + 1)
                    act.activation(probT[:, r], tiled(5 - r % 2)[0:T], ACT.Copy).then_inc(s["probsT_ready"], 1)
                if one_more:
                    evacuate_v(t + 1)
                if two_more:
                    z_high(t + 2)

            act.preload_act_table(ACT.Exp)
            z_high(0)
            take_q(0)
            take_k(0)
            evacuate_qk(0)
            evacuate_v(0)
            z_high(1)
            block_engine[0] = act
            over_loop(step)
            out_high(NT - 1)

        if store is not None:
            @block.sync
            def _(sp):
                with sp.Fori(0, NT) as t:
                    sp.wait_ge(s["x_done"], t + 1)
                    sp.dma_start(store[t], xt[:, t, :]).then_inc(s["x_stored"], 16)
                sp.wait_ge(s["x_stored"], 16 * NT)


IN_SCALE = 0
W_SCALE = 16
PROJ_SCALE = 20
LN_W, LN_B = 22, 26
HEAD_LN = 30
SMOOTH = 38
COLUMNS = 70
KEYS = 375
HALF_HEADS = 8
FP8_MAX = 448.0


def column_products(k, cols, packed, raw_scale, in_inverse, smooth_inverse, proj_scale, head_ln):
    nc = k.nc
    landed, products, squared = k.sem("cols_landed"), k.sem("cols_products"), k.sem("cols_squared")
    with nc.Block() as block:
        @block.sync
        def _(sp):
            sp.dma_start(cols[:], packed).then_inc(landed, 16)

        @block.vector
        def _(dve):
            dve.wait_ge(landed, 16)
            dve.tensor_tensor(raw_scale[:], cols[:, IN_SCALE:IN_SCALE + 16].rearrange("p (v c) -> p v c", c=DC),
                              cols[:, W_SCALE:W_SCALE + 4, None].to_broadcast([P, 4, DC]), ALU.mult).then_inc(products, 1)
            dve.reciprocal(in_inverse[:], cols[:, IN_SCALE:IN_SCALE + 16]).then_inc(products, 1)
            dve.reciprocal(smooth_inverse[:], cols[:, SMOOTH:SMOOTH + 32]).then_inc(products, 1)
            dve.tensor_tensor(proj_scale[:], cols[:, PROJ_SCALE:PROJ_SCALE + 1],
                              cols[:, PROJ_SCALE + 1:PROJ_SCALE + 2], ALU.mult).then_inc(products, 1)
            dve.tensor_copy(head_ln[:], cols[:, HEAD_LN:HEAD_LN + 8]).then_inc(products, 1)
            dve.wait_ge(products, 5)
            for n in (0, 4):
                dve.tensor_scalar(head_ln[:, n:n + 2], head_ln[:, n:n + 2], P ** -0.5, None, ALU.mult).then_inc(squared, 1)
            dve.wait_ge(squared, 2)


def quantise_inputs(k, x, cols, in_inverse, xq_dram):
    nc, ps = k.nc, k.ps
    G, GB = 4, B // 4
    names = ("z_ready", "stat", "centre", "vareps", "rooted", "z2_ready", "zT_in_psum", "ln_ready", "scaled", "clipped",
             "exponent", "magic", "shifted", "rounded", "stored")
    s = {n: k.sem(f"quant_{n}") for n in names}
    stored = [k.sem(f"quant_stored{v}") for v in range(2)]
    with ExitStack() as ctx:
        z = k.sb(ctx, "quant_z", [S, B, D], F32)
        stats = k.sb(ctx, "quant_stats", [S, B, 6], F32)
        mv = k.sb(ctx, "quant_mv", [S, B, 2], F32)
        ve = k.sb(ctx, "quant_ve", [S, B], F32)
        rstd = k.sb(ctx, "quant_rstd", [S, B], F32)
        ln = k.sb(ctx, "quant_ln", [P, GB, DC, S], F32)
        y = k.sb(ctx, "quant_y", [P, 2, GB, DC, S], BF16)
        expo = k.sb(ctx, "quant_expo", [P, 2, GB, DC, S], BF16)
        magic = k.sb(ctx, "quant_magic", [P, 2, GB, DC, S], BF16)
        shifted = k.sb(ctx, "quant_shifted", [P, 2, GB, DC, S], F32)
        q = k.sb(ctx, "quant_q", [P, 2, GB, DC, S], BF16)
        block = ctx.enter_context(nc.Block())

        @block.vector
        def _(dve):
            for b in range(B):
                dve.tensor_scalar(z[:, b, :], x[:, b, :], k.mean_var[0:S, b, 0:1], k.rstd[0:S, b:b + 1],
                                  ALU.subtract, ALU.mult).then_inc(s["z_ready"], 1)
            for b in range(B):
                dve.wait_ge(s["z_ready"], b + 1)
                dve.bn_stats(stats[:, b, :], z[:, b, :]).then_inc(s["stat"], 1)
            for b in range(B):
                dve.wait_ge(s["stat"], b + 1)
                dve.bn_aggr(mv[:, b, :], stats[:, b, :]).then_inc(s["centre"], 1)
            dve.wait_ge(s["centre"], B)
            dve.tensor_scalar(ve[:], mv[:, :, 1], EPS, None, ALU.add).then_inc(s["vareps"], 1)
            dve.wait_ge(s["rooted"], 1)
            for b in range(B):
                dve.tensor_scalar(z[:, b, :], z[:, b, :], mv[:, b, 0:1], rstd[:, b:b + 1],
                                  ALU.subtract, ALU.mult).then_inc(s["z2_ready"], 1)
            for g in range(G):
                for v in range(4):
                    n = 4 * g + v
                    i = n % 2
                    wait(dve, s["rounded"], n - 1)
                    dve.wait_ge(s["scaled"], 4 * n + 4)
                    dve.tensor_scalar(y[:, i], y[:, i], FP8_MAX, -FP8_MAX, ALU.min, ALU.max).then_inc(s["clipped"], 1)
                    dve.wait_ge(s["clipped"], n + 1)
                    dve.tensor_scalar(expo[:, i].bitcast(U16), y[:, i].bitcast(U16), 0x7F80, 0x7F80,
                                      ALU.bitwise_and, ALU.bitwise_and).then_inc(s["exponent"], 1)
                    dve.wait_ge(s["exponent"], n + 1)
                    dve.tensor_scalar(magic[:, i], expo[:, i], 2.0 ** -6, 1.5 * 2.0 ** 20,
                                      ALU.max, ALU.mult).then_inc(s["magic"], 1)
                    dve.wait_ge(s["magic"], n + 1)
                    dve.tensor_tensor(shifted[:, i], y[:, i], magic[:, i], ALU.add).then_inc(s["shifted"], 1)

        @block.gpsimd
        def _(pool):
            pool.wait_ge(s["vareps"], 1)
            pool.tensor_tensor(rstd[:], ve[:], k.half[0:S, 0:B], ALU.pow).then_inc(s["rooted"], 1)
            for n in range(4 * G):
                pool.wait_ge(s["shifted"], n + 1)
                if n >= 2:
                    pool.wait_ge(stored[n % 2], 16 * (n // 2))
                pool.tensor_tensor(q[:, n % 2], shifted[:, n % 2], magic[:, n % 2], ALU.subtract).then_inc(s["rounded"], 1)

        @block.tensor
        def _(pe):
            for g in range(G):
                wait(pe, s["ln_ready"], 4 * g)
                for j in range(GB):
                    b = GB * g + j
                    pe.wait_ge(s["z2_ready"], b + 1)
                    for c in range(DC):
                        mm = pe.transpose(ps[c][:, j * S:(j + 1) * S], z[:, b, c * P:(c + 1) * P], k.ident[0:S, 0:S])
                mm.then_inc(s["zT_in_psum"], 1)

        @block.scalar
        def _(act):
            for g in range(G):
                act.wait_ge(s["zT_in_psum"], g + 1)
                wait(act, s["scaled"], 16 * g)
                for c in range(DC):
                    act.activation(ln[:, :, c, :], ps[c][:, 0:GB * S].rearrange("p (b t) -> p b t", t=S), ACT.Identity,
                                   scale=cols[:, LN_W + c:LN_W + c + 1],
                                   bias=cols[:, LN_B + c:LN_B + c + 1]).then_inc(s["ln_ready"], 1)
                act.wait_ge(s["ln_ready"], 4 * (g + 1))
                for v in range(4):
                    n = 4 * g + v
                    wait(act, s["shifted"], n - 1)
                    for c in range(DC):
                        act.activation(y[:, n % 2, :, c, :], ln[:, :, c, :], ACT.Copy,
                                       scale=in_inverse[:, 4 * v + c:4 * v + c + 1]).then_inc(s["scaled"], 1)

        @block.sync
        def _(sp):
            for g in range(G):
                for v in range(4):
                    n = 4 * g + v
                    sp.wait_ge(s["rounded"], n + 1)
                    sp.dma_start(xq_dram[v, GB * g:GB * (g + 1)].rearrange("b p n -> p b n"),
                                 q[:, n % 2].rearrange("p b c t -> p b (c t)")).then_inc(stored[n % 2], 16)
            for v in range(2):
                sp.wait_ge(stored[v], 16 * 2 * G)


def normed_attention(k, name, x, xq_dram, kinds, wq, wk, wv, wo, ln_q, ln_k, smooth_inverse, head_ln, ctxT_dram=None):
    nc, ps = k.nc, k.ps
    own = ctxT_dram is None
    KT, KN = (1, S) if own else (3, KEYS // 3)
    NK = KT * KN
    H, GR = HALF_HEADS, HALF_HEADS // 2
    HS = 4 if own else 1
    NS = H // HS
    AHEAD = 2
    SLOTS = 2 if own else 3
    U = 2 + 2 * KT
    LU = 2 + KT
    UNIT_BANK = [0, 1, 4, 0] if own else [n % 2 for n in range(U)]
    NEXT_AT = {t: t - 1 for t in range(1, 1 + LU)}
    KG = [[0, 1, 2, 3]] if own else [[0], [1], [2], [3]]
    TG = 2 + len(KG)
    TBANK = [2, 3, 4] if own else [6, 7, 5, 3, 2, 4]
    Y_BANK = 5 if own else 6
    NV = len(kinds)
    NQ = min(NV, 2)
    names = ("xq_landed", "xq_ready", "xv_landed", "xv_ready", "ctx_landed", "ctx_high", "ctx_low", "unit_in_psum", "stat", "centre", "vareps",
             "rooted", "normed", "v_ready", "turned_in_psum", "turned_ready", "scores_in_psum", "minus_max", "exp_done",
             "inverse", "probs_ready", "probsT_in_psum", "probsT_ready", "cat_in_psum", "cat_scaled", "cat_clipped",
             "cat_exponent", "cat_magic", "cat_shifted", "cat_rounded", "y_in_psum", "x_done")
    s = {n: k.sem(f"{name}_{n}") for n in names}
    with ExitStack() as ctx:
        def sb(n, shape, dt=F32):
            return k.sb(ctx, f"{name}_{n}", shape, dt)
        xq_raw = sb("xq_raw", [P, NV, DC * S], BF16)
        xq = sb("xq", [P, NV, DC, S], F32R)
        if not own:
            ctx_raw = sb("ctx_raw", [P, DC, NK])
            ctx_part = [sb(f"ctx_part{i}", [P, DC, NK], F32R) for i in range(2)]
        stats = sb("stats", [P, LU, 4, 6])
        mv = sb("mv", [P, LU, 4, 2])
        ve = sb("ve", [P, LU, 4])
        rstd = sb("rstd", [P, LU, 4])
        qn = sb("qn", [S, H, P])
        kn = sb("kn", [KN, KT, GR, P])
        v = sb("v", [KN, KT, GR * P])
        qT = sb("qT", [P, H, S])
        kT = sb("kT", [P, GR, NK])
        carry = sb("carry", [1, 1])
        neg_max = sb("neg_max", [S, H])
        total = sb("total", [S, H])
        inverse = sb("inverse", [S, H])
        prob = sb("prob", [S, SLOTS, HS, NK])
        probT = sb("probT", [KN, 2, KT, 4 if own else 2, S])
        scaled = sb("scaled", [P, H, S])
        clipped = sb("clipped", [P, H, S], BF16)
        expo = sb("expo", [P, H, S], BF16)
        magic = sb("magic", [P, H, S], BF16)
        catq = sb("catq", [P, H, S], F32R)
        block = ctx.enter_context(nc.Block())

        def over_loop(eng, step):
            step(0, True)
            with eng.Fori(1, B - 1) as b:
                step(b, True)
            step(B - 1, False)

        def unit_bank(n):
            return ps[UNIT_BANK[n]]

        def unit_rows(n):
            return S if n < 2 else KN

        def score_bank(t):
            return ps[2 + t % 3]

        def probsT_of(pair, j):
            if own:
                return probT[:, pair // 2, 0, 2 * (pair % 2):2 * (pair % 2) + 2, :].rearrange("p a t -> p (a t)")
            return probT[:, pair % 2, j, :, :].rearrange("p a t -> p (a t)")

        @block.sync
        def _(sp):
            def load(b):
                wait(sp, s["xq_ready"], b)
                sp.dma_start(xq_raw[:, 0:NQ], xq_dram[kinds[0]:kinds[0] + NQ, b, :, :].rearrange("v p n -> p v n"))\
                    .then_inc(s["xq_landed"], 16)
                if own:
                    wait(sp, s["xv_ready"], b)
                    sp.dma_start(xq_raw[:, 2], xq_dram[kinds[2], b, :, :]).then_inc(s["xv_landed"], 16)
                else:
                    wait(sp, s["ctx_low"], b)
                    sp.dma_start(ctx_raw[:], ctxT_dram[b].rearrange("p (c n) -> p c n", c=DC)).then_inc(s["ctx_landed"], 16)
            load(0)
            with sp.Fori(1, B) as b:
                load(b)

        @block.gpsimd
        def _(pool):
            def root(b, n):
                rows = unit_rows(n)
                pool.wait_ge(s["centre"], 4 * (LU * b + n + 1))
                pool.tensor_tensor(ve[0:rows, n, :], mv[0:rows, n, :, 1], k.eps[0:rows, 0:4], ALU.add)\
                    .then_inc(s["vareps"], 1)
                pool.wait_ge(s["vareps"], LU * b + n + 1)
                pool.tensor_tensor(rstd[0:rows, n, :], ve[0:rows, n, :], k.half[0:rows, 0:4], ALU.pow)\
                    .then_inc(s["rooted"], 1)

            def round_cat(b):
                pool.wait_ge(s["cat_magic"], b + 1)
                pool.tensor_tensor(scaled[:], clipped[:], magic[:], ALU.add).then_inc(s["cat_shifted"], 1)
                pool.wait_ge(s["cat_shifted"], b + 1)
                pool.tensor_tensor(catq[:], scaled[:], magic[:], ALU.subtract).then_inc(s["cat_rounded"], 1)

            def step(b, one_more):
                if one_more:
                    for n in range(LU):
                        root(b + 1, n)
                round_cat(b)
            for n in range(LU):
                root(0, n)
            over_loop(pool, step)

        @block.tensor
        def _(pe):
            def unit(b, n):
                bank = unit_bank(n)[0:unit_rows(n), :]
                if n == 0:
                    pe.wait_ge(s["xq_ready"], b + 1)
                if n == 2 and not own:
                    pe.wait_ge(s["ctx_low"], b + 1)
                if n == LU and own:
                    pe.wait_ge(s["xv_ready"], b + 1)
                last = max((m for m in range(n) if UNIT_BANK[m] == UNIT_BANK[n]), default=None)
                entry = b
                if last is None:
                    last, entry = max(m for m in range(U) if UNIT_BANK[m] == UNIT_BANK[n]), b - 1
                if last >= LU:
                    wait(pe, s["v_ready"], KT * entry + last - LU + 1)
                else:
                    wait(pe, s["normed"], LU * entry + last + 1)
                for c in range(DC):
                    if n < 2:
                        lhs, rhs = [xq[:, 0, c, :]], [h[:, c, n * 512:(n + 1) * 512] for h in wq]
                    else:
                        key = n < LU
                        j = (n - 2) % KT
                        rhs = [h[:, c, 0:512] for h in (wk if key else wv)]
                        lhs = [xq[:, 1 if key else 2, c, :]] if own else \
                            [h[:, c, j * KN:(j + 1) * KN] for h in ctx_part]
                    mm = product(pe, bank, lhs, rhs, c == 0, c == DC - 1)
                mm.then_inc(s["unit_in_psum"], 1)

            def turn(b):
                for g in range(2):
                    pe.wait_ge(s["normed"], LU * b + g + 1)
                    if not own:
                        wait(pe, s["cat_scaled"], 2 * b)
                    for h in range(4):
                        mm = pe.transpose(ps[TBANK[g]][:, h * S:(h + 1) * S], qn[:, 4 * g + h, :], k.ident[0:S, 0:S])
                    mm.then_inc(s["turned_in_psum"], 1)
                pe.wait_ge(s["normed"], LU * b + LU)
                for n, groups in enumerate(KG):
                    for i, g in enumerate(groups):
                        for j in range(KT):
                            at = (i * KT + j) * KN
                            mm = pe.transpose(ps[TBANK[2 + n]][:, at:at + KN], kn[:, j, g, :], k.ident[0:KN, 0:KN])
                    mm.then_inc(s["turned_in_psum"], 1)

            def project_out(b):
                pe.wait_ge(s["cat_rounded"], b + 1)
                for h in range(H):
                    mm = product(pe, ps[Y_BANK][0:S, :], [catq[:, h, :]], [w[:, h, :] for w in wo], h == 0, h == H - 1)
                mm.then_inc(s["y_in_psum"], 1)

            def scores(b, t):
                if t == 0:
                    pe.wait_ge(s["turned_ready"], TG * b + TG)
                if t >= 3:
                    pe.wait_ge(s["exp_done"], NS * b + t - 2)
                for i in range(HS):
                    h = HS * t + i
                    mm = pe.matmul(score_bank(t)[0:S, i * NK:(i + 1) * NK], qT[:, h, :], kT[:, h // 2, :],
                                   start=True, stop=True)
                mm.then_inc(s["scores_in_psum"], 1)

            def turn_probs(b, t):
                pe.wait_ge(s["probs_ready"], NS * b + t + 1)
                wait(pe, s["probsT_ready"], NS * b + t)
                if own and t == 0:
                    wait(pe, s["x_done"], b - 1)
                for i in range(HS):
                    for j in range(KT):
                        at = (i * KT + j) * S
                        mm = pe.transpose(ps[5][0:KN, at:at + S], prob[:, t % SLOTS, i, j * KN:(j + 1) * KN],
                                          k.ident[0:S, 0:S])
                mm.then_inc(s["probsT_in_psum"], 1)

            def weigh_values(b, pair):
                if pair == 0:
                    pe.wait_ge(s["v_ready"], KT * (b + 1))
                    if own:
                        wait(pe, s["cat_scaled"], 2 * b)
                    else:
                        wait(pe, s["x_done"], b)
                pe.wait_ge(s["probsT_ready"], NS * b + (2 * pair + 1) // HS + 1)
                at = (pair % 2) * 2 * S
                for j in range(KT):
                    mm = pe.matmul(ps[6 + pair // 2][:, at:at + 2 * S], v[:, j, pair * P:(pair + 1) * P],
                                   probsT_of(pair, j), start=j == 0, stop=j == KT - 1)
                if pair % 2:
                    mm.then_inc(s["cat_in_psum"], 1)

            def step(b, one_more):
                first = isinstance(b, int) and b == 0
                if own:
                    turn(b)
                    unit(b, LU)
                    scores(b, 0)
                    scores(b, 1)
                    if one_more:
                        unit(b + 1, 0)
                        unit(b + 1, 1)
                    turn_probs(b, 0)
                    if one_more:
                        unit(b + 1, 2)
                    turn_probs(b, 1)
                    if not first:
                        pe.wait_ge(s["probsT_ready"], NS * b + 2)
                        project_out(b - 1)
                    for pair in range(GR):
                        weigh_values(b, pair)
                else:
                    unit(b, LU)
                    turn(b)
                    unit(b, LU + 1)
                    unit(b, LU + 2)
                    scores(b, 0)
                    scores(b, 1)
                    if not first:
                        project_out(b - 1)
                    for t in range(NS):
                        if t + AHEAD < NS:
                            scores(b, t + AHEAD)
                        if one_more and t in NEXT_AT:
                            unit(b + 1, NEXT_AT[t])
                        turn_probs(b, t)
                        if t >= 2 and t % 2 == 0:
                            weigh_values(b, t // 2 - 1)
                    weigh_values(b, GR - 1)

            for n in range(LU):
                unit(0, n)
            over_loop(pe, step)
            project_out(B - 1)

        @block.scalar
        def _(act):
            def cast(b):
                act.wait_ge(s["xq_landed"], 16 * b + 16)
                wait(act, s["unit_in_psum"], U * (b - 1) + LU)
                act.activation(xq[:, 0:NQ].rearrange("p v c t -> p v (c t)"), xq_raw[:, 0:NQ], ACT.Copy)\
                    .then_inc(s["xq_ready"], 1)

            def cast_for_values(b):
                act.wait_ge(s["xv_landed"], 16 * b + 16)
                wait(act, s["unit_in_psum"], U * b)
                act.activation(xq[:, 2].rearrange("p c t -> p (c t)"), xq_raw[:, 2], ACT.Copy).then_inc(s["xv_ready"], 1)

            def split_ctx(b):
                act.wait_ge(s["ctx_landed"], 16 * b + 16)
                wait(act, s["unit_in_psum"], U * b)
                act.activation(ctx_part[0][:], ctx_raw[:], ACT.Copy).then_inc(s["ctx_high"], 1)

            def take_values(b, j):
                act.wait_ge(s["unit_in_psum"], U * b + LU + j + 1)
                act.activation(v[:, j, :], unit_bank(LU + j)[0:KN, :], ACT.Copy).then_inc(s["v_ready"], 1)

            def take_turned(b):
                for n in range(TG):
                    act.wait_ge(s["turned_in_psum"], TG * b + n + 1)
                    if n < 2:
                        out = qT[:, 4 * n:4 * n + 4, :].rearrange("p h t -> p (h t)")
                        at = ln_q
                    else:
                        out = kT[:, KG[n - 2][0]:KG[n - 2][-1] + 1, :].rearrange("p g t -> p (g t)")
                        at = ln_k
                    act.activation(out, ps[TBANK[n]][:, 0:out.shape[1]], ACT.Identity, scale=head_ln[:, at:at + 1],
                                   bias=head_ln[:, at + 1:at + 2]).then_inc(s["turned_ready"], 1)

            def exponential(b, t):
                act.wait_ge(s["minus_max"], NS * b + t + 1)
                if t >= SLOTS:
                    act.wait_ge(s["probsT_in_psum"], NS * b + t - SLOTS + 1)
                for i in range(HS):
                    h = HS * t + i
                    op = act.activation(prob[:, t % SLOTS, i, :], score_bank(t)[0:S, i * NK:(i + 1) * NK], ACT.Exp,
                                        bias=neg_max[:, h:h + 1], accum_out=total[:, h:h + 1])
                op.then_inc(s["exp_done"], 1)

            def take_probsT(b, t):
                act.wait_ge(s["probsT_in_psum"], NS * b + t + 1)
                if own:
                    act.activation(probT[:, t, 0].rearrange("p a t -> p (a t)"), ps[5][0:KN, 0:HS * S],
                                   ACT.Copy).then_inc(s["probsT_ready"], 1)
                else:
                    act.activation(probT[:, (t // 2) % 2, :, t % 2, :], ps[5][0:KN, 0:KT * S].rearrange(
                        "p (j t) -> p j t", t=S), ACT.Copy).then_inc(s["probsT_ready"], 1)

            def step(b, one_more):
                if one_more:
                    cast(b + 1)
                if not own:
                    take_values(b, 0)
                take_turned(b)
                for j in range(0 if own else 1, KT):
                    take_values(b, j)
                exponential(b, 0)
                exponential(b, 1)
                if one_more:
                    if own:
                        cast_for_values(b + 1)
                    else:
                        split_ctx(b + 1)
                for t in range(NS):
                    if t + AHEAD < NS:
                        exponential(b, t + AHEAD)
                    take_probsT(b, t)
            act.preload_act_table(ACT.Exp)
            cast(0)
            if own:
                cast_for_values(0)
            else:
                split_ctx(0)
            over_loop(act, step)

        @block.vector
        def _(dve):
            def split_ctx(b):
                dve.wait_ge(s["ctx_high"], b + 1)
                dve.tensor_tensor(ctx_part[1][:], ctx_raw[:], ctx_part[0][:].bitcast(F32), ALU.subtract)\
                    .then_inc(s["ctx_low"], 1)

            def measure(b, n):
                rows = unit_rows(n)
                dve.wait_ge(s["unit_in_psum"], U * b + n + 1)
                for h in range(4):
                    dve.bn_stats(stats[0:rows, n, h, :], unit_bank(n)[0:rows, h * P:(h + 1) * P]).then_inc(s["stat"], 1)

            def aggregate(b, n):
                rows = unit_rows(n)
                dve.wait_ge(s["stat"], 4 * (LU * b + n + 1))
                dve.tensor_copy(carry[0:1, :], k.eps[0:1, 0:1])
                for h in range(4):
                    dve.bn_aggr(mv[0:rows, n, h, :], stats[0:rows, n, h, :]).then_inc(s["centre"], 1)

            def normalise(b, n):
                rows = unit_rows(n)
                if n == 0:
                    wait(dve, s["turned_in_psum"], TG * b)
                dve.wait_ge(s["rooted"], LU * b + n + 1)
                for h in range(4):
                    out = qn[:, 4 * n + h, :] if n < 2 else kn[:, n - 2, h, :]
                    op = dve.tensor_scalar(out, unit_bank(n)[0:rows, h * P:(h + 1) * P], mv[0:rows, n, h, 0:1],
                                           rstd[0:rows, n, h:h + 1], ALU.subtract, ALU.mult)
                op.then_inc(s["normed"], 1)

            def top(b, t):
                dve.wait_ge(s["scores_in_psum"], NS * b + t + 1)
                dve.tensor_reduce(neg_max[:, HS * t:HS * (t + 1)],
                                  score_bank(t)[0:S, 0:HS * NK].rearrange("p (h n) -> p h n", h=HS), AX.X, ALU.max,
                                  negate=True).then_inc(s["minus_max"], 1)

            def invert(b, t):
                dve.wait_ge(s["exp_done"], NS * b + t + 1)
                dve.reciprocal(inverse[:, HS * t:HS * (t + 1)], total[:, HS * t:HS * (t + 1)]).then_inc(s["inverse"], 1)

            def probabilities(b, t):
                dve.wait_ge(s["inverse"], NS * b + t + 1)
                slot = prob[:, t % SLOTS]
                if own:
                    dve.tensor_tensor(slot, slot, inverse[:, HS * t:HS * (t + 1), None].to_broadcast([S, HS, NK]),
                                      ALU.mult).then_inc(s["probs_ready"], 1)
                else:
                    dve.tensor_scalar(slot[:, 0, :], slot[:, 0, :], inverse[:, t:t + 1], None, ALU.mult)\
                        .then_inc(s["probs_ready"], 1)

            def scale_cat(b, i):
                dve.wait_ge(s["cat_in_psum"], 2 * b + i + 1)
                if i == 0:
                    wait(dve, s["cat_rounded"], b)
                dve.tensor_tensor(scaled[:, 4 * i:4 * i + 4, :], ps[6 + i][:, 0:4 * S].rearrange("p (h t) -> p h t", t=S),
                                  smooth_inverse[:, 4 * i:4 * i + 4, None].to_broadcast([P, 4, S]), ALU.mult)\
                    .then_inc(s["cat_scaled"], 1)

            def round_cat(b):
                dve.wait_ge(s["cat_scaled"], 2 * b + 2)
                dve.tensor_scalar(clipped[:], scaled[:], FP8_MAX, -FP8_MAX, ALU.min, ALU.max).then_inc(s["cat_clipped"], 1)
                dve.wait_ge(s["cat_clipped"], b + 1)
                dve.tensor_scalar(expo[:].bitcast(U16), clipped[:].bitcast(U16), 0x7F80, 0x7F80,
                                  ALU.bitwise_and, ALU.bitwise_and).then_inc(s["cat_exponent"], 1)
                dve.wait_ge(s["cat_exponent"], b + 1)
                dve.tensor_scalar(magic[:], expo[:], 2.0 ** -6, 1.5 * 2.0 ** 20, ALU.max, ALU.mult)\
                    .then_inc(s["cat_magic"], 1)

            def add_out(b):
                dve.wait_ge(s["y_in_psum"], b + 1)
                dve.tensor_tensor(x[:, b, :], ps[Y_BANK][0:S, :], x[:, b, :], ALU.add).then_inc(s["x_done"], 1)

            def step(b, one_more):
                first = isinstance(b, int) and b == 0
                top(b, 0)
                top(b, 1)
                invert(b, 0)
                probabilities(b, 0)
                if own:
                    if one_more:
                        measure(b + 1, 0)
                        aggregate(b + 1, 0)
                    invert(b, 1)
                    probabilities(b, 1)
                    if one_more:
                        measure(b + 1, 1)
                        aggregate(b + 1, 1)
                        normalise(b + 1, 0)
                        measure(b + 1, 2)
                        aggregate(b + 1, 2)
                        normalise(b + 1, 1)
                    if not first:
                        add_out(b - 1)
                    if one_more:
                        normalise(b + 1, 2)
                    scale_cat(b, 0)
                else:
                    invert(b, 1)
                    probabilities(b, 1)
                    if one_more:
                        split_ctx(b + 1)
                    if not first:
                        add_out(b - 1)
                    for t in range(NS):
                        if t + AHEAD < NS:
                            top(b, t + AHEAD)
                        if 1 <= t and t + 1 < NS:
                            invert(b, t + 1)
                            probabilities(b, t + 1)
                        if one_more:
                            if t - 1 in NEXT_AT:
                                normalise(b + 1, NEXT_AT[t - 1])
                            if t in NEXT_AT:
                                measure(b + 1, NEXT_AT[t])
                                aggregate(b + 1, NEXT_AT[t])
                        if t == 6:
                            scale_cat(b, 0)
                scale_cat(b, 1)
                round_cat(b)

            if not own:
                split_ctx(0)
            for n in range(LU):
                measure(0, n)
                aggregate(0, n)
                normalise(0, n)
            over_loop(dve, step)
            add_out(B - 1)
            dve.wait_ge(s["x_done"], B)


def cross_attention_layer(k, x, io, x1):
    nc = k.nc
    xq_dram = nc.dram_tensor("L0_quantised_inputs", (4, B, P, DC * S), BF16, kind="Internal").ap()
    with ExitStack() as ctx:
        cols = k.sb(ctx, "cols", [P, COLUMNS], F32)
        raw_scale = k.sb(ctx, "raw_scale", [P, 4, DC], F32)
        in_inverse = k.sb(ctx, "in_inverse", [P, 16], F32)
        smooth_inverse = k.sb(ctx, "smooth_inverse", [P, 32], F32)
        proj_scale = k.sb(ctx, "proj_scale", [P, 1], F32)
        head_ln = k.sb(ctx, "head_ln", [P, 8], F32)
        column_products(k, cols, io["L0x_columns"], raw_scale, in_inverse, smooth_inverse, proj_scale, head_ln)
        prepare(k, "x0stats", None, [], rows=(x, S, B), loads=[(x[:], x1.rearrange("(s b) d -> s b d", b=B))])
        quantise_inputs(k, x, cols, in_inverse, xq_dram)
        k.recycle_semaphores()
        for phase in ("self", "cross"):
            for half in range(2):
                name = f"{phase}{half}"
                with ExitStack() as weights:
                    w = [k.sb(weights, f"{name}_w{i}", [P, DC, 2048], F32R) for i in range(2)]
                    wo = [k.sb(weights, f"{name}_wo{i}", [P, HALF_HEADS, D], F32R) for i in range(2)]
                    kinds = [0, 1, 2] if phase == "self" else [3]
                    src = io[f"L0x_{phase}"][half]
                    pieces = []
                    for c in range(DC):
                        parts = [(0, 1024, kinds[0])]
                        parts += [(1024, 1536, 1), (1536, 2048, 2)] if phase == "self" else [(1024, 2048, None)]
                        for a, b, kind in parts:
                            pieces.append((src[:, c * 2048 + a:c * 2048 + b], w[0][:, c, a:b], w[1][:, c, a:b],
                                           None if kind is None else raw_scale[:, kind, c:c + 1]))
                    first = (16 if phase == "cross" else 0) + HALF_HEADS * half
                    for h in range(0, HALF_HEADS, 2):
                        n = first + h
                        pieces.append((io["L0x_proj"][:, n * D:(n + 2) * D],
                                       wo[0][:, h:h + 2, :].rearrange("p h n -> p (h n)"),
                                       wo[1][:, h:h + 2, :].rearrange("p h n -> p (h n)"), proj_scale[:]))
                    with ExitStack() as stage:
                        raw = k.sb(stage, f"{name}_raw", [P, 6, 1024], F32)
                        prepare(k, f"{name}w", raw, pieces)
                    normed_attention(k, name, x, xq_dram, kinds, [h[:, :, 0:1024] for h in w],
                                     [h[:, :, 1024:1536] for h in w], [h[:, :, 1536:2048] for h in w],
                                     [h[:] for h in wo], 0 if phase == "self" else 4, 2 if phase == "self" else 6,
                                     smooth_inverse[:, first:first + HALF_HEADS], head_ln,
                                     io["ctxT"] if phase == "cross" else None)
                k.recycle_semaphores()


EXPERTS = 8
HID = 448
HC = 4
HT = HID - 3 * P
TOKENS = B * S


def route(k, x, io, zT, scores_dram):
    nc, ps = k.nc, k.ps
    E = EXPERTS
    names = ("loaded", "gate_high", "gate_low", "z_ready", "zT_in_psum", "z_high", "z_low", "logitsT_in_psum",
             "logitsT_ready", "logits_in_psum", "exp_done", "chain", "chosen", "chosenT_in_psum", "chosenT_ready",
             "iota_ready", "stored")
    s = {n: k.sem(f"route_{n}") for n in names}
    with ExitStack() as ctx:
        def sb(n, shape, dt=F32):
            return k.sb(ctx, f"route_{n}", shape, dt)
        gate_raw = sb("gate_raw", [P, DC * E])
        gate = [sb(f"gate{i}", [P, DC, E], F32R) for i in range(2)]
        bias = sb("bias", [S, E])
        z = sb("z", [S, 4, D])
        logitsT = sb("logitsT", [E, B, S])
        rank = sb("rank", [S, E])
        a = sb("a", [S, B, E])
        score = sb("score", [S, B, E])
        biased = sb("biased", [S, B, E])
        hit = sb("hit", [S, B, E])
        first = sb("first", [S, B, E])
        row = sb("row", [S, B])
        row2 = sb("row2", [S, B])
        chosenT = sb("chosenT", [E, B, S])
        shared = sb("shared", [1, TOKENS])
        block = ctx.enter_context(nc.Block())

        @block.sync
        def _(sp):
            sp.dma_start(gate_raw[:], io["moe_gate"]).then_inc(s["loaded"], 16)
            sp.dma_start(bias[:], io["moe_bias"].to_broadcast([S, E])).then_inc(s["loaded"], 16)
            sp.wait_ge(s["iota_ready"], 2)
            sp.dma_start(scores_dram[E:E + 1, :], shared[:]).then_inc(s["stored"], 16)
            sp.wait_ge(s["chosenT_ready"], 4)
            sp.dma_start(scores_dram[0:E, :], chosenT[:].rearrange("e b t -> e (b t)")).then_inc(s["stored"], 16)
            sp.wait_ge(s["stored"], 32)

        @block.gpsimd
        def _(pool):
            pool.memset(shared[:], 1.0).then_inc(s["iota_ready"], 1)
            pool.iota(rank[:], pattern=[[-1, E]], base=E, channel_multiplier=0,
                      allow_small_or_imprecise_dtypes=True).then_inc(s["iota_ready"], 1)

        @block.scalar
        def _(act):
            act.wait_ge(s["loaded"], 32)
            act.activation(gate[0][:].rearrange("p c e -> p (c e)"), gate_raw[:], ACT.Copy).then_inc(s["gate_high"], 1)
            for b in range(B):
                act.wait_ge(s["zT_in_psum"], b + 1)
                act.activation(zT[0][:, :, b, :], ps[b % 4][:, 0:DC * S].rearrange("p (c t) -> p c t", t=S),
                               ACT.Copy).then_inc(s["z_high"], 1)
            for g in range(4):
                act.wait_ge(s["logitsT_in_psum"], g + 1)
                act.activation(logitsT[:, 4 * g:4 * g + 4, :].rearrange("e b t -> e (b t)"), ps[2 + g][0:E, 0:4 * S],
                               ACT.Copy).then_inc(s["logitsT_ready"], 1)
            act.wait_ge(s["chain"], 2)
            act.activation(a[:], a[:], ACT.Exp).then_inc(s["exp_done"], 1)
            for g in range(4):
                act.wait_ge(s["chosenT_in_psum"], g + 1)
                act.activation(chosenT[:, 4 * g:4 * g + 4, :].rearrange("e b t -> e (b t)"), ps[2 + g][0:E, 0:4 * S],
                               ACT.Copy).then_inc(s["chosenT_ready"], 1)

        @block.tensor
        def _(pe):
            for b in range(B):
                pe.wait_ge(s["z_ready"], b + 1)
                wait(pe, s["z_low"], b - 3)
                for c in range(DC):
                    mm = pe.transpose(ps[b % 4][:, c * S:(c + 1) * S], z[:, b % 4, c * P:(c + 1) * P], k.ident[0:S, 0:S])
                mm.then_inc(s["zT_in_psum"], 1)
            pe.wait_ge(s["z_low"], B)
            pe.wait_ge(s["gate_low"], 1)
            for g in range(4):
                for c in range(DC):
                    mm = product(pe, ps[2 + g][0:E, 0:4 * S], [h[:, c, :] for h in gate],
                                 [t[:, c, 4 * g:4 * g + 4, :].rearrange("p b t -> p (b t)") for t in zT],
                                 c == 0, c == DC - 1)
                mm.then_inc(s["logitsT_in_psum"], 1)
            for b in range(B):
                pe.wait_ge(s["logitsT_ready"], b // 4 + 1)
                mm = pe.transpose(ps[0][0:S, b * E:(b + 1) * E], logitsT[:, b, :], k.ident[0:E, 0:E])
            mm.then_inc(s["logits_in_psum"], 1)
            pe.wait_ge(s["chosen"], 1)
            for b in range(B):
                mm = pe.transpose(ps[2 + b // 4][0:E, (b % 4) * S:(b % 4 + 1) * S], first[:, b, :], k.ident[0:S, 0:S])
                if b % 4 == 3:
                    mm.then_inc(s["chosenT_in_psum"], 1)

        @block.vector
        def _(dve):
            def z_low(b):
                dve.wait_ge(s["z_high"], b + 1)
                dve.tensor_tensor(zT[1][:, :, b, :], ps[b % 4][:, 0:DC * S].rearrange("p (c t) -> p c t", t=S),
                                  zT[0][:, :, b, :].bitcast(F32), ALU.subtract).then_inc(s["z_low"], 1)
            for b in range(B):
                wait(dve, s["zT_in_psum"], b - 3)
                dve.tensor_scalar(z[:, b % 4, :], x[:, b, :], k.mean_var[0:S, b, 0:1], k.rstd[0:S, b:b + 1],
                                  ALU.subtract, ALU.mult).then_inc(s["z_ready"], 1)
                if b >= 2:
                    z_low(b - 2)
            z_low(B - 2)
            z_low(B - 1)
            dve.wait_ge(s["gate_high"], 1)
            dve.tensor_tensor(gate[1][:].rearrange("p c e -> p (c e)"), gate_raw[:],
                              gate[0][:].rearrange("p c e -> p (c e)").bitcast(F32), ALU.subtract)\
                .then_inc(s["gate_low"], 1)

            done = [0]

            def after(op):
                op.then_inc(s["chain"], 1)
                done[0] += 1
                dve.wait_ge(s["chain"], done[0])

            def every(column):
                return column[:, :, None].to_broadcast([S, B, E])

            def each(line):
                return line[:, None, :].to_broadcast([S, B, E])
            dve.wait_ge(s["logits_in_psum"], 1)
            logits = ps[0][0:S, 0:B * E].rearrange("p (b e) -> p b e", e=E)
            after(dve.tensor_reduce(row[:], logits, AX.X, ALU.max))
            after(dve.tensor_tensor(a[:], logits, every(row), ALU.subtract))
            dve.wait_ge(s["exp_done"], 1)
            after(dve.tensor_reduce(row[:], a[:], AX.X, ALU.add))
            after(dve.reciprocal(row2[:], row[:]))
            after(dve.tensor_tensor(score[:], a[:], every(row2), ALU.mult))
            after(dve.tensor_tensor(biased[:], score[:], each(bias), ALU.add))
            dve.wait_ge(s["iota_ready"], 2)
            for turn in range(2):
                after(dve.tensor_reduce(row[:], biased[:], AX.X, ALU.max))
                after(dve.tensor_tensor(hit[:], biased[:], every(row), ALU.is_equal))
                after(dve.tensor_tensor(hit[:], hit[:], each(rank), ALU.mult))
                after(dve.tensor_reduce(row[:], hit[:], AX.X, ALU.max))
                out = first if turn == 0 else a
                after(dve.tensor_tensor(out[:], hit[:], every(row), ALU.is_equal))
                if turn == 0:
                    after(dve.scalar_tensor_tensor(out=biased[:].rearrange("p b e -> p (b e)"),
                                                   in0=first[:].rearrange("p b e -> p (b e)"), scalar=MASKED,
                                                   in1=biased[:].rearrange("p b e -> p (b e)"),
                                                   op0=ALU.mult, op1=ALU.add))
            after(dve.tensor_tensor(a[:], a[:], first[:], ALU.add))
            dve.tensor_tensor(first[:], a[:], score[:], ALU.mult).then_inc(s["chosen"], 1)


def hidden_rows(c):
    return P if c < HC - 1 else HT


def expert_layer(k, x, io):
    nc, ps = k.nc, k.ps
    E1 = EXPERTS + 1
    G, GB = 4, B // 4
    N = GB * S
    scores_dram = nc.dram_tensor("expert_scores", (E1, TOKENS), F32, kind="Internal").ap()
    names = ("score_landed", "up_landed", "w2_landed", "up_high", "up_low", "down_high", "down_low", "up_in_psum",
             "gate_in_psum", "up_scaled", "gate_scaled", "silu_ready", "h_ready", "h_high", "h_low", "y_in_psum",
             "x_done")
    with ExitStack() as ctx:
        zT = [k.sb(ctx, f"moe_zT{i}", [P, DC, B, S], F32R) for i in range(2)]
        prepare(k, "moestats", None, [], rows=(x, S, B))
        route(k, x, io, zT, scores_dram)
        k.recycle_semaphores()
        s = {n: k.sem(f"moe_{n}") for n in names}

        def sb(n, shape, dt=F32):
            return k.sb(ctx, f"moe_{n}", shape, dt)
        raw_up = sb("raw_up", [P, DC * 2 * HID])
        raw_down = sb("raw_down", [P, HC * D])
        up = [sb(f"up{i}", [P, DC, 2 * HID], F32R) for i in range(2)]
        down = [sb(f"down{i}", [P, HC, D], F32R) for i in range(2)]
        score = sb("score", [P, TOKENS])
        u = sb("u", [P, 2, N])
        g3 = sb("g3", [P, 2, N])
        silu = sb("silu", [P, 2, N])
        h = sb("h", [P, 2, N])
        hT = [sb(f"hT{i}", [P, 2, HC, N], F32R) for i in range(2)]
        block = ctx.enter_context(nc.Block())

        def over_loop(eng, step):
            step(0)
            with eng.Fori(1, E1) as e:
                step(e)

        @block.sync
        def _(sp):
            def step(e):
                wait(sp, s["up_low"], e)
                sp.dma_start(raw_up[:], io["moe_up"][e]).then_inc(s["up_landed"], 16)
                wait(sp, s["down_low"], 2 * e)
                sp.dma_start(raw_down[:, 0:3 * D], io["moe_w2"][e]).then_inc(s["w2_landed"], 16)
                sp.dma_start(raw_down[0:HT, 3 * D:], io["moe_w2_tail"][e]).then_inc(s["w2_landed"], 16)
                wait(sp, s["gate_scaled"], 16 * e)
                sp.dma_start(score[:], scores_dram[bass.ts(e, 1), :].to_broadcast([P, TOKENS]))\
                    .then_inc(s["score_landed"], 16)
            over_loop(sp, step)

        @block.tensor
        def _(pe):
            def down_group(e, g):
                if g == 0:
                    pe.wait_ge(s["down_low"], 2 * e + 2)
                pe.wait_ge(s["h_low"], 16 * e + 4 * g + 4)
                for j in range(GB):
                    wait(pe, s["x_done"], 16 * e + 4 * (g - 1) + j + 1)
                    for c in range(HC):
                        mm = product(pe, ps[4 + j][0:S, :], [t[0:hidden_rows(c), g % 2, c, j * S:(j + 1) * S] for t in hT],
                                     [w[0:hidden_rows(c), c, :] for w in down], c == 0, c == HC - 1)
                    mm.then_inc(s["y_in_psum"], 1)

            def step(e):
                pe.wait_ge(s["up_low"], e + 1)
                for g in range(G):
                    for c in range(HC):
                        n = 16 * e + 4 * g + c
                        tail = c == HC - 1
                        if c == 1:
                            wait(pe, s["gate_scaled"], n - 1)
                        for i, sem, used in ((0, "up_in_psum", "up_scaled"), (1, "gate_in_psum", "gate_scaled")):
                            if tail and i == 1:
                                continue
                            wait(pe, s[used], n - 1)
                            for kc in range(DC):
                                mm = product(pe, ps[2 * i + c % 2][:, 0:N],
                                             [w[:, kc, (HC * i + c) * P:(HC * i + c + 1) * P] for w in up],
                                             [t[:, kc, GB * g:GB * (g + 1), :].rearrange("p b t -> p (b t)") for t in zT],
                                             kc == 0, kc == DC - 1)
                            mm.then_inc(s[sem], 1)
                    if g:
                        down_group(e, g - 1)
                down_group(e, G - 1)
            over_loop(pe, step)

        @block.scalar
        def _(act):
            def step(e):
                act.wait_ge(s["up_landed"], 16 * e + 16)
                wait(act, s["up_in_psum"], 16 * e)
                act.activation(up[0][:].rearrange("p c n -> p (c n)"), raw_up[:],
                               ACT.Copy).then_inc(s["up_high"], 1)
                for g in range(G):
                    for c in range(HC):
                        n = 16 * e + 4 * g + c
                        act.wait_ge(s["up_scaled"], n + 1)
                        wait(act, s["h_ready"], n - 1)
                        rows = slice(0, hidden_rows(c))
                        act.activation(silu[rows, c % 2, :], u[rows, c % 2, :], ACT.Silu).then_inc(s["silu_ready"], 1)
                        if g == 0 and c == 0:
                            act.wait_ge(s["w2_landed"], 32 * e + 32)
                            wait(act, s["y_in_psum"], 16 * e)
                            for part, free in ((slice(0, P), slice(0, HC - 1)), (slice(0, HT), slice(HC - 1, HC))):
                                act.activation(down[0][part, free, :].rearrange("p c n -> p (c n)"),
                                               raw_down[part, free.start * D:free.stop * D], ACT.Copy)\
                                    .then_inc(s["down_high"], 1)
                        act.wait_ge(s["h_ready"], n + 1)
                        if c == 0 and g >= 2:
                            act.wait_ge(s["y_in_psum"], 16 * e + 4 * (g - 1))
                        act.activation(hT[0][rows, g % 2, c, :], h[rows, c % 2, :], ACT.Copy).then_inc(s["h_high"], 1)
            act.preload_act_table(ACT.Silu)
            over_loop(act, step)

        @block.vector
        def _(dve):
            def split_up(e):
                dve.wait_ge(s["up_high"], e + 1)
                dve.tensor_tensor(up[1][:].rearrange("p c n -> p (c n)"), raw_up[:],
                                  up[0][:].rearrange("p c n -> p (c n)").bitcast(F32), ALU.subtract)\
                    .then_inc(s["up_low"], 1)

            def step(e, one_more):
                def add(g):
                    for j in range(GB):
                        dve.wait_ge(s["y_in_psum"], 16 * e + 4 * g + j + 1)
                        dve.tensor_tensor(x[:, GB * g + j, :], ps[4 + j][0:S, :], x[:, GB * g + j, :], ALU.add)\
                            .then_inc(s["x_done"], 1)
                for g in range(G):
                    for c in range(HC):
                        n = 16 * e + 4 * g + c
                        for out, bank, ready, used in ((u, 0, "up_scaled", "silu_ready"),
                                                            (g3, 2, "gate_scaled", "h_ready")):
                            if g == 0 and c == 0 and bank == 0:
                                dve.wait_ge(s["score_landed"], 16 * e + 16)
                            wait(dve, s[used], n - 1)
                            rows = slice(0, hidden_rows(c))
                            source = rows
                            if c == HC - 1:
                                if bank:
                                    source = slice(HT, 2 * HT)
                                    bank = 0
                            elif bank:
                                dve.wait_ge(s["gate_in_psum"], (HC - 1) * (G * e + g) + c + 1)
                            if not bank:
                                dve.wait_ge(s["up_in_psum"], n + 1)
                            dve.tensor_tensor(out[rows, c % 2, :], ps[bank + c % 2][source, 0:N],
                                              score[source, g * N:(g + 1) * N], ALU.mult).then_inc(s[ready], 1)
                        if g == 0 and c == 0:
                            dve.wait_ge(s["down_high"], 2 * e + 2)
                            for part, free in ((slice(0, P), slice(0, HC - 1)), (slice(0, HT), slice(HC - 1, HC))):
                                dve.tensor_tensor(down[1][part, free, :].rearrange("p c n -> p (c n)"),
                                                  raw_down[part, free.start * D:free.stop * D],
                                                  down[0][part, free, :].rearrange("p c n -> p (c n)").bitcast(F32),
                                                  ALU.subtract).then_inc(s["down_low"], 1)
                    if g:
                        add(g - 1)
                if one_more:
                    split_up(e + 1)
                add(G - 1)
            split_up(0)
            step(0, True)
            with dve.Fori(1, E1 - 1) as e:
                step(e, True)
            step(E1 - 1, False)
            dve.wait_ge(s["x_done"], 16 * E1)

        @block.gpsimd
        def _(pool):
            def step(e):
                for g in range(G):
                    for c in range(HC):
                        n = 16 * e + 4 * g + c
                        pool.wait_ge(s["gate_scaled"], n + 1)
                        pool.wait_ge(s["silu_ready"], n + 1)
                        wait(pool, s["h_low"], n - 1)
                        rows = slice(0, hidden_rows(c))
                        pool.tensor_tensor(h[rows, c % 2, :], g3[rows, c % 2, :], silu[rows, c % 2, :], ALU.mult)\
                            .then_inc(s["h_ready"], 1)
                        pool.wait_ge(s["h_high"], n + 1)
                        pool.tensor_tensor(hT[1][rows, g % 2, c, :], h[rows, c % 2, :],
                                           hT[0][rows, g % 2, c, :].bitcast(F32),
                                           ALU.subtract).then_inc(s["h_low"], 1)
            over_loop(pool, step)
    k.recycle_semaphores()


def causal_mask(k, mask, done):
    with k.nc.Block() as block:
        @block.gpsimd
        def _(pool):
            pool.memset(mask[:], 0.0).then_inc(done, 1)
            pool.wait_ge(done, 1)
            pool.affine_select(out=mask[:], in_=mask[:], compare_op=ALU.is_ge, fill=MASKED, base=0,
                               pattern=[[-1, S]], channel_multiplier=1).then_inc(done, 1)
            pool.wait_ge(done, 2)


def flat(t):
    return t[:].rearrange("p c n -> p (c n)")


def second_attention_layer(k, x, io):
    with ExitStack() as ctx:
        w = [[k.sb(ctx, f"a1_{n}{i}", [P, DC, D], F32R) for i in range(2)] for n in ("q", "k", "v", "o")]
        mask = k.sb(ctx, "a1_mask", [S, S], F32)
        bias_cols = k.sb(ctx, "a1_bias_cols", [P, 2 * DC], F32)
        bias_v = k.sb(ctx, "a1_bias_v", [S, D], F32)
        bias_o = k.sb(ctx, "a1_bias_o", [S, D], F32)
        causal_mask(k, mask, k.sem("mask1_done"))
        with ExitStack() as stage:
            raw = k.sb(stage, "a1_raw", [P, 6, 1024], F32)
            prepare(k, "a1w", raw, [(io[f"L1_{n}"], flat(h), flat(lo), None) for n, (h, lo) in zip("qkvo", w)],
                    rows=(x, S, B), loads=[
                        (bias_cols[:], io["L1_bias_cols"]),
                        (bias_v[:], io["L1_bias_v"].to_broadcast([S, D])),
                        (bias_o[:], io["L1_bias_o"].to_broadcast([S, D]))])
        full = [[h[:] for h in part] for part in w]
        small_head_attention(k, "a1", x, B, S, *full, DC, lambda r, c: 4 * c + r, lambda r, c: 32 * (4 * c + r), mask,
                             bias_q=bias_cols[:, 0:DC], bias_k=bias_cols[:, DC:2 * DC], bias_v=bias_v, bias_o=bias_o)
        k.recycle_semaphores()


def wide_attention_layer(k, x, io):
    nc, ps = k.nc, k.ps
    JN, J = KEYS // 3, 3
    NK = KEYS + S
    names = ("z_ready", "zT_in_psum", "z_high", "z_low", "ctxT_landed", "ctx_landed", "q_in_psum", "k_in_psum",
             "q_taken", "k_taken", "qT_in_psum", "kT_in_psum", "v_in_psum", "q_ready", "k_ready", "v_ready", "scores_in_psum", "minus_max", "exp_done", "inverse_ready",
             "probsT_in_psum", "probsT_ready", "out_in_psum", "out_ready", "outT_in_psum", "out_high", "out_low",
             "y_in_psum", "x_done")
    with ExitStack() as ctx:
        def sb(n, shape, dt=F32):
            return k.sb(ctx, f"wide_{n}", shape, dt)
        wq, wk, wv, wo = [[sb(f"w{n}{i}", [P, DC, D], F32R) for i in range(2)] for n in "qkvo"]
        with ExitStack() as stage:
            raw = k.sb(stage, "wide_raw", [P, 6, 1024], F32)
            prepare(k, "widew", raw, [(io[f"L1x_{n}"], flat(h), flat(lo), None)
                                      for n, (h, lo) in zip("qkvo", (wq, wk, wv, wo))], rows=(x, S, B))
        k.recycle_semaphores()
        s = {n: k.sem(f"wide_{n}") for n in names}
        z = sb("z", [S, D])
        zT = [sb(f"zT{i}", [P, DC, S], F32R) for i in range(2)]
        ctxT = sb("ctxT", [P, DC, KEYS])
        ctx_rows = sb("ctx_rows", [JN, J, D])
        q = sb("q", [S, D])
        key = sb("key", [S, D])
        qT = sb("qT", [P, DC, S])
        kT = sb("kT", [P, DC, S])
        v = sb("v", [S, D])
        prob = sb("prob", [S, NK])
        probT = sb("probT", [JN, J + 1, S])
        neg_max = sb("neg_max", [S, 1])
        total = sb("total", [S, 1])
        inverse = sb("inverse", [S, 1])
        o = sb("o", [S, D])
        oT = [sb(f"oT{i}", [P, DC, S], F32R) for i in range(2)]
        block = ctx.enter_context(nc.Block())

        def over_loop(eng, step):
            step(0, True, True)
            with eng.Fori(1, B - 2) as b:
                step(b, True, True)
            step(B - 2, True, False)
            step(B - 1, False, False)

        def tiled(bank):
            return ps[bank][:, 0:DC * S].rearrange("p (c t) -> p c t", t=S)

        @block.sync
        def _(sp):
            def load(b):
                wait(sp, s["scores_in_psum"], b)
                sp.dma_start(ctxT[:], io["ctxT"][b].rearrange("p (c n) -> p c n", c=DC)).then_inc(s["ctxT_landed"], 16)
                wait(sp, s["out_in_psum"], b)
                sp.dma_start(ctx_rows[:], io["ctx"][b].rearrange("(j p) d -> p j d", p=JN)).then_inc(s["ctx_landed"], 16)
            load(0)
            with sp.Fori(1, B) as b:
                load(b)

        @block.tensor
        def _(pe):
            def transpose_z(b):
                pe.wait_ge(s["z_ready"], b + 1)
                for c in range(DC):
                    mm = pe.transpose(tiled(6)[:, c, :], z[:, c * P:(c + 1) * P], k.ident[0:S, 0:S])
                mm.then_inc(s["zT_in_psum"], 1)

            def rows(b, bank, w, sem):
                pe.wait_ge(s["z_low"], b + 1)
                for c in range(DC):
                    mm = product(pe, ps[bank][0:S, :], [h[:, c, :] for h in zT], [h[:, c, :] for h in w],
                                 c == 0, c == DC - 1)
                mm.then_inc(s[sem], 1)

            def turn(b, bank, source, taken, sem):
                pe.wait_ge(s[taken], b + 1)
                for c in range(DC):
                    mm = pe.transpose(tiled(bank)[:, c, :], source[:, c * P:(c + 1) * P], k.ident[0:S, 0:S])
                mm.then_inc(s[sem], 1)

            def transpose_out(b):
                pe.wait_ge(s["out_ready"], b + 1)
                for c in range(DC):
                    mm = pe.transpose(tiled(6)[:, c, :], o[:, c * P:(c + 1) * P], k.ident[0:S, 0:S])
                mm.then_inc(s["outT_in_psum"], 1)

            def project_out(b):
                wait(pe, s["x_done"], b)
                pe.wait_ge(s["out_low"], b + 1)
                for c in range(DC):
                    mm = product(pe, ps[7][0:S, :], [h[:, c, :] for h in oT], [h[:, c, :] for h in wo],
                                 c == 0, c == DC - 1)
                mm.then_inc(s["y_in_psum"], 1)

            def step(b, one_more, two_more):
                first = isinstance(b, int) and b == 0
                pe.wait_ge(s["ctxT_landed"], 16 * b + 16)
                pe.wait_ge(s["q_ready"], b + 1)
                wait(pe, s["exp_done"], b)
                for c in range(DC):
                    pe.matmul(ps[3][0:S, 0:KEYS], qT[:, c, :], ctxT[:, c, :], start=c == 0, stop=c == DC - 1)
                pe.wait_ge(s["k_ready"], b + 1)
                for c in range(DC):
                    mm = pe.matmul(ps[3][0:S, KEYS:NK], qT[:, c, :], kT[:, c, :], start=c == 0, stop=c == DC - 1)
                mm.then_inc(s["scores_in_psum"], 1)
                if one_more:
                    pe.wait_ge(s["z_low"], b + 2)
                if not first:
                    transpose_out(b - 1)
                if one_more:
                    rows(b + 1, 0, wq, "q_in_psum")
                    rows(b + 1, 1, wk, "k_in_psum")
                    wait(pe, s["probsT_ready"], 2 * b)
                    turn(b + 1, 4, q, "q_taken", "qT_in_psum")
                    turn(b + 1, 0, key, "k_taken", "kT_in_psum")
                if not first:
                    project_out(b - 1)
                pe.wait_ge(s["exp_done"], b + 1)
                if one_more:
                    pe.wait_ge(s["q_ready"], b + 2)
                for j in range(J + 1):
                    n = JN if j < J else S
                    mm = pe.transpose(tiled(4)[0:n, j, :], prob[:, j * JN:j * JN + n], k.ident[0:S, 0:S])
                mm.then_inc(s["probsT_in_psum"], 1)
                if two_more:
                    wait(pe, s["out_low"], b)
                    transpose_z(b + 2)
                pe.wait_ge(s["ctx_landed"], 16 * b + 16)
                pe.wait_ge(s["v_ready"], b + 1)
                pe.wait_ge(s["probsT_ready"], 2 * b + 2)
                wait(pe, s["out_ready"], b)
                for j in range(J + 1):
                    n = JN if j < J else S
                    mm = pe.matmul(ps[5][0:S, :], probT[0:n, j, :], ctx_rows[:, j, :] if j < J else v[:],
                                   start=j == 0, stop=j == J)
                mm.then_inc(s["out_in_psum"], 1)
                if one_more:
                    rows(b + 1, 2, wv, "v_in_psum")

            transpose_z(0)
            rows(0, 0, wq, "q_in_psum")
            rows(0, 1, wk, "k_in_psum")
            turn(0, 4, q, "q_taken", "qT_in_psum")
            turn(0, 0, key, "k_taken", "kT_in_psum")
            rows(0, 2, wv, "v_in_psum")
            transpose_z(1)
            over_loop(pe, step)
            transpose_out(B - 1)
            project_out(B - 1)

        @block.scalar
        def _(act):
            def z_high(b):
                act.wait_ge(s["zT_in_psum"], b + 1)
                act.activation(zT[0][:], tiled(6), ACT.Copy).then_inc(s["z_high"], 1)

            def take_rows(b):
                act.wait_ge(s["q_in_psum"], b + 1)
                act.activation(q[:], ps[0][0:S, :], ACT.Copy, scale=D ** -0.5).then_inc(s["q_taken"], 1)
                act.wait_ge(s["k_in_psum"], b + 1)
                act.activation(key[:], ps[1][0:S, :], ACT.Copy).then_inc(s["k_taken"], 1)

            def take_turned(b):
                act.wait_ge(s["qT_in_psum"], b + 1)
                act.activation(qT[:], tiled(4), ACT.Copy).then_inc(s["q_ready"], 1)
                act.wait_ge(s["kT_in_psum"], b + 1)
                act.activation(kT[:], tiled(0), ACT.Copy).then_inc(s["k_ready"], 1)

            def take_v(b):
                act.wait_ge(s["v_in_psum"], b + 1)
                act.activation(v[:], ps[2][0:S, :], ACT.Copy).then_inc(s["v_ready"], 1)

            def out_high(b):
                act.wait_ge(s["outT_in_psum"], b + 1)
                act.activation(oT[0][:], tiled(6), ACT.Copy).then_inc(s["out_high"], 1)

            def step(b, one_more, two_more):
                if not (isinstance(b, int) and b == 0):
                    out_high(b - 1)
                act.wait_ge(s["minus_max"], b + 1)
                wait(act, s["probsT_in_psum"], b)
                act.activation(prob[:], ps[3][0:S, 0:NK], ACT.Exp, bias=neg_max[:], accum_out=total[:])\
                    .then_inc(s["exp_done"], 1)
                if one_more:
                    take_rows(b + 1)
                    take_turned(b + 1)
                act.wait_ge(s["probsT_in_psum"], b + 1)
                act.activation(probT[:, 0:J, :], tiled(4)[0:JN, 0:J, :], ACT.Copy).then_inc(s["probsT_ready"], 1)
                act.activation(probT[0:S, J, :], tiled(4)[0:S, J, :], ACT.Copy).then_inc(s["probsT_ready"], 1)
                if one_more:
                    take_v(b + 1)
                if two_more:
                    z_high(b + 2)

            act.preload_act_table(ACT.Exp)
            z_high(0)
            take_rows(0)
            take_turned(0)
            take_v(0)
            z_high(1)
            over_loop(act, step)
            out_high(B - 1)

        @block.vector
        def _(dve):
            def normalise(b):
                wait(dve, s["zT_in_psum"], b)
                dve.tensor_scalar(z[:], x[:, b, :], k.mean_var[0:S, b, 0:1], k.rstd[0:S, bass.ts(b, 1)],
                                  ALU.subtract, ALU.mult).then_inc(s["z_ready"], 1)

            def z_low(b):
                dve.wait_ge(s["z_high"], b + 1)
                dve.tensor_tensor(zT[1][:], tiled(6), zT[0][:].bitcast(F32), ALU.subtract).then_inc(s["z_low"], 1)

            def out_low(b):
                dve.wait_ge(s["out_high"], b + 1)
                dve.tensor_tensor(oT[1][:], tiled(6), oT[0][:].bitcast(F32), ALU.subtract).then_inc(s["out_low"], 1)

            def add_out(b):
                dve.wait_ge(s["y_in_psum"], b + 1)
                dve.tensor_tensor(x[:, b, :], ps[7][0:S, :], x[:, b, :], ALU.add).then_inc(s["x_done"], 1)

            def step(b, one_more, two_more):
                first = isinstance(b, int) and b == 0
                dve.wait_ge(s["scores_in_psum"], b + 1)
                dve.tensor_reduce(neg_max[:], ps[3][0:S, 0:NK], AX.X, ALU.max, negate=True).then_inc(s["minus_max"], 1)
                if not first:
                    out_low(b - 1)
                if two_more:
                    normalise(b + 2)
                dve.wait_ge(s["exp_done"], b + 1)
                dve.reciprocal(inverse[:], total[:]).then_inc(s["inverse_ready"], 1)
                if not first:
                    add_out(b - 1)
                dve.wait_ge(s["inverse_ready"], b + 1)
                dve.wait_ge(s["out_in_psum"], b + 1)
                dve.tensor_scalar(o[:], ps[5][0:S, :], inverse[:], None, ALU.mult).then_inc(s["out_ready"], 1)
                if two_more:
                    z_low(b + 2)

            normalise(0)
            z_low(0)
            normalise(1)
            z_low(1)
            over_loop(dve, step)
            out_low(B - 1)
            add_out(B - 1)
            dve.wait_ge(s["x_done"], B)
    k.recycle_semaphores()


HIDDEN = 2048
MC = HIDDEN // P


def ternary(k, x, sources, signs, neg_scale, half):
    nc, ps = k.nc, k.ps
    N = DC * HIDDEN
    CH = 4
    W = N // CH
    names = ("row_stat", "row_centre", "row_var", "row_rooted", "sums_ready", "sum_ready", "total_in_psum", "mean_ready", "scale_ready", "above", "pattern")
    s = {n: k.sem(f"tern_{n}") for n in names}
    landed = [k.sem(f"tern_landed{i}") for i in range(CH)]
    with ExitStack() as ctx:
        raw = k.sb(ctx, "tern_raw", [P, 2, N], F32)
        above = k.sb(ctx, "tern_above", [P, W], F32)
        sums = k.sb(ctx, "tern_sums", [P, 3, CH], F32)
        magnitude = k.sb(ctx, "tern_magnitude", [P, W], BF16)
        stats = k.sb(ctx, "tern_stats", [S, B, 6], F32)
        ve = k.sb(ctx, "tern_ve", [S, B], F32)
        one = k.sb(ctx, "tern_sum", [P, 3], F32)
        mean = k.sb(ctx, "tern_mean", [P, 3], F32)
        raws = [raw[:, 0], raw[:, 1], raw[:, 0]]
        block = ctx.enter_context(nc.Block())

        @block.sync
        def _(sp):
            for m, src in enumerate(sources):
                for i in range(CH):
                    if m == 2:
                        sp.wait_ge(s["pattern"], i + 1)
                    if m:
                        sp.wait_ge(landed[i], 16 * m)
                    sp.dma_start(raws[m][:, i * W:(i + 1) * W], src[:, i * W:(i + 1) * W]).then_inc(landed[i], 16)

        @block.scalar
        def _(act):
            for m in range(3):
                for i in range(CH):
                    act.wait_ge(landed[i], 16 * (m + 1))
                    wait(act, s["sums_ready"], CH * m + i)
                    act.activation(magnitude[:], raws[m][:, i * W:(i + 1) * W], ACT.Abs,
                                   accum_out=sums[:, m, i:i + 1]).then_inc(s["sums_ready"], 1)

        @block.gpsimd
        def _(pool):
            pool.wait_ge(s["row_var"], 1)
            pool.tensor_tensor(k.rstd[0:S, 0:B], ve[:], k.half[0:S, 0:B], ALU.pow).then_inc(s["row_rooted"], 1)
            pool.wait_ge(s["row_rooted"], 1)

        @block.vector
        def _(dve):
            for b in range(B):
                dve.bn_stats(stats[:, b, :], x[:, b, :]).then_inc(s["row_stat"], 1)
            for b in range(B):
                dve.wait_ge(s["row_stat"], b + 1)
                dve.bn_aggr(k.mean_var[0:S, b, :], stats[:, b, :]).then_inc(s["row_centre"], 1)
            dve.wait_ge(s["row_centre"], B)
            dve.tensor_scalar(ve[:], k.mean_var[0:S, 0:B, 1], EPS, None, ALU.add).then_inc(s["row_var"], 1)
            for m in range(3):
                dve.wait_ge(s["sums_ready"], CH * (m + 1))
                dve.tensor_reduce(one[:, m:m + 1], sums[:, m, :], AX.X, ALU.add).then_inc(s["sum_ready"], 1)
                dve.wait_ge(s["total_in_psum"], m + 1)
                dve.tensor_scalar(mean[:, m:m + 1], ps[0][:, m:m + 1], 1.0 / (P * N), 1e-8, ALU.mult, ALU.add)\
                    .then_inc(s["mean_ready"], 1)
                dve.wait_ge(s["mean_ready"], m + 1)
                dve.tensor_scalar(neg_scale[:, m:m + 1], mean[:, m:m + 1], -1.0, None, ALU.mult)\
                    .then_inc(s["scale_ready"], 1)
                dve.tensor_scalar(half[:, m, 0:1], mean[:, m:m + 1], 0.5, None, ALU.mult).then_inc(s["scale_ready"], 1)
                dve.tensor_scalar(half[:, m, 1:2], mean[:, m:m + 1], -0.5, None, ALU.mult).then_inc(s["scale_ready"], 1)
                dve.wait_ge(s["scale_ready"], 3 * (m + 1))
                for i in range(CH):
                    n = CH * m + i
                    wait(dve, s["pattern"], n)
                    dve.tensor_scalar(above[:], raws[m][:, i * W:(i + 1) * W], half[:, m, 0:1], None,
                                      ALU.is_gt).then_inc(s["above"], 1)
                    dve.wait_ge(s["above"], n + 1)
                    dve.scalar_tensor_tensor(out=signs[m][:, i * W:(i + 1) * W], in0=raws[m][:, i * W:(i + 1) * W],
                                             scalar=half[:, m, 1:2], in1=above[:], op0=ALU.is_lt,
                                             op1=ALU.subtract).then_inc(s["pattern"], 1)
            dve.wait_ge(s["pattern"], 3 * CH)

        @block.tensor
        def _(pe):
            for m in range(3):
                pe.wait_ge(s["sum_ready"], m + 1)
                wait(pe, s["mean_ready"], m)
                pe.matmul(ps[0][:, m:m + 1], k.ones[:], one[:, m:m + 1], start=True, stop=True)\
                    .then_inc(s["total_in_psum"], 1)


def ternary_mlp_layer(k, x, io):
    nc, ps = k.nc, k.ps
    GB = 4
    G = B // GB
    names = ("z_ready", "zT_in_psum", "z_high", "z_low", "up_in_psum", "gate_in_psum", "silu_ready", "h_ready",
             "h_high", "h_low", "y_in_psum", "x_done", "x_stored")
    with ExitStack() as ctx:
        signs = [k.sb(ctx, f"signs_{n}", [P, DC * HIDDEN], F32R) for n in ("up", "gate", "down")]
        neg_scale = k.sb(ctx, "neg_scale", [P, 3], F32)
        half = k.sb(ctx, "half_scale", [P, 3, 2], F32)
        ternary(k, x, [io["L1f_up"], io["L1f_gate"], io["L1f_down"]], [w[:] for w in signs], neg_scale, half)
        k.recycle_semaphores()
        s = {n: k.sem(f"mlp_{n}") for n in names}
        up_w, gate_w = [w[:].rearrange("p (c n) -> p c n", c=DC) for w in signs[0:2]]
        down_w = signs[2][:].rearrange("p (m n) -> p m n", m=MC)
        z = k.sb(ctx, "mlp_z", [S, GB, D], F32)
        zT = [k.sb(ctx, f"mlp_zT{i}", [P, DC, GB, S], F32R) for i in range(2)]
        silu = k.sb(ctx, "mlp_silu", [P, 2, GB * S], F32)
        h = k.sb(ctx, "mlp_h", [P, 2, GB * S], F32)
        hT = [k.sb(ctx, f"mlp_hT{i}", [P, 2, GB * S], F32R) for i in range(2)]
        block = ctx.enter_context(nc.Block())
        N = GB * S

        def over_loop(eng, step):
            step(0, True)
            with eng.Fori(1, G - 1) as g:
                step(g, True)
            step(G - 1, False)

        @block.tensor
        def _(pe):
            def down(g, m):
                n = MC * g + m
                pe.wait_ge(s["h_low"], n + 1)
                for j in range(GB):
                    if m == 0:
                        wait(pe, s["x_done"], GB * (g - 1) + j + 1)
                    mm = product(pe, ps[4 + j][0:S, :], [t[:, m % 2, j * S:(j + 1) * S] for t in hT],
                                 [down_w[:, m, :]], m == 0, m == MC - 1)
                mm.then_inc(s["y_in_psum"], 1)

            def transpose_z(g):
                for j in range(GB):
                    pe.wait_ge(s["z_ready"], GB * g + j + 1)
                    wait(pe, s["silu_ready" if j < 2 else "h_ready"], MC * g)
                    for c in range(DC):
                        mm = pe.transpose(ps[j][:, c * S:(c + 1) * S], z[:, j, c * P:(c + 1) * P], k.ident[0:S, 0:S])
                    mm.then_inc(s["zT_in_psum"], 1)

            def step(g, one_more):
                for m in range(MC):
                    n = MC * g + m
                    for w, bank, sem, used in ((up_w, 0, "up_in_psum", "silu_ready"),
                                               (gate_w, 2, "gate_in_psum", "h_ready")):
                        if m == 0:
                            pe.wait_ge(s["z_low"], GB * g + GB)
                        if m >= 2:
                            pe.wait_ge(s[used], n - 1)
                        for c in range(DC):
                            mm = product(pe, ps[bank + m % 2][:, 0:N], [w[:, c, m * P:(m + 1) * P]],
                                         [t[:, c].rearrange("p b t -> p (b t)") for t in zT], c == 0, c == DC - 1)
                        mm.then_inc(s[sem], 1)
                    if m:
                        down(g, m - 1)
                if one_more:
                    transpose_z(g + 1)
                down(g, MC - 1)
            transpose_z(0)
            over_loop(pe, step)

        @block.scalar
        def _(act):
            def z_high(g):
                for j in range(GB):
                    act.wait_ge(s["zT_in_psum"], GB * g + j + 1)
                    act.activation(zT[0][:, :, j, :], ps[j][:, 0:DC * S].rearrange("p (c t) -> p c t", t=S),
                                   ACT.Copy).then_inc(s["z_high"], 1)

            def step(g, one_more):
                def high(m):
                    act.wait_ge(s["h_ready"], MC * g + m + 1)
                    if m >= 2:
                        act.wait_ge(s["y_in_psum"], MC * g + m - 1)
                    act.activation(hT[0][:, m % 2, :], h[:, m % 2, :], ACT.Copy).then_inc(s["h_high"], 1)
                for m in range(MC):
                    if m:
                        high(m - 1)
                    act.wait_ge(s["up_in_psum"], MC * g + m + 1)
                    act.activation(silu[:, m % 2, :], ps[m % 2][:, 0:N], ACT.Silu, scale=neg_scale[:, 0:1])\
                        .then_inc(s["silu_ready"], 1)
                high(MC - 1)
                if one_more:
                    z_high(g + 1)
            act.preload_act_table(ACT.Silu)
            z_high(0)
            over_loop(act, step)

        @block.vector
        def _(dve):
            def normalise(g, j):
                b = GB * g + j
                wait(dve, s["zT_in_psum"], GB * (g - 1) + j + 1)
                dve.tensor_scalar(z[:, j, :], x[:, b, :], k.mean_var[0:S, b, 0:1], k.rstd[0:S, bass.ts(b, 1)],
                                  ALU.subtract, ALU.mult).then_inc(s["z_ready"], 1)

            def z_low(g):
                for j in range(GB):
                    dve.wait_ge(s["z_high"], GB * g + j + 1)
                    dve.tensor_tensor(zT[1][:, :, j, :], ps[j][:, 0:DC * S].rearrange("p (c t) -> p c t", t=S),
                                      zT[0][:, :, j, :].bitcast(F32), ALU.subtract).then_inc(s["z_low"], 1)

            def step(g, one_more):
                def low(m):
                    dve.wait_ge(s["h_high"], MC * g + m + 1)
                    dve.tensor_tensor(hT[1][:, m % 2, :], h[:, m % 2, :], hT[0][:, m % 2, :].bitcast(F32),
                                      ALU.subtract).then_inc(s["h_low"], 1)
                for m in range(MC):
                    n = MC * g + m
                    if m:
                        low(m - 1)
                    if one_more and 4 <= m < 4 + GB:
                        normalise(g + 1, m - 4)
                    dve.wait_ge(s["gate_in_psum"], n + 1)
                    dve.wait_ge(s["silu_ready"], n + 1)
                    dve.scalar_tensor_tensor(out=h[:, m % 2, :], in0=ps[2 + m % 2][:, 0:N], scalar=neg_scale[:, 1:2],
                                             in1=silu[:, m % 2, :], op0=ALU.mult, op1=ALU.mult).then_inc(s["h_ready"], 1)
                low(MC - 1)
                if one_more:
                    z_low(g + 1)
                dve.wait_ge(s["y_in_psum"], MC * g + MC)
                for j in range(GB):
                    dve.scalar_tensor_tensor(out=x[:, GB * g + j, :], in0=ps[4 + j][0:S, :], scalar=neg_scale[0:S, 2:3],
                                             in1=x[:, GB * g + j, :], op0=ALU.mult, op1=ALU.add).then_inc(s["x_done"], 1)
            for j in range(GB):
                normalise(0, j)
            z_low(0)
            over_loop(dve, step)

        @block.sync
        def _(sp):
            with sp.Fori(0, B) as b:
                sp.wait_ge(s["x_done"], b + 1)
                sp.dma_start(io["out"][b], x[:, b, :]).then_inc(s["x_stored"], 16)
            sp.wait_ge(s["x_stored"], 16 * B)
    k.recycle_semaphores()


def decoder(nc, io):
    with ExitStack() as top:
        k = Core(nc, top)
        constants(k)
        x1 = nc.dram_tensor("x_after_L0_attention", (S * B, D), F32, kind="Internal").ap()

        with ExitStack() as ctx:
            T, NT = P, S * B // P
            xt = k.sb(ctx, "x_by_position", [P, NT, D], F32)
            raw = k.sb(ctx, "a0_raw", [P, 6, 1024], F32)
            w = [k.sb(ctx, f"a0_qkv{i}", [P, DC, 768], F32R) for i in range(2)]
            wo = [k.sb(ctx, f"a0_o{i}", [P, DC, D], F32R) for i in range(2)]
            mask = k.sb(ctx, "a0_mask", [P, P], F32)
            block_causal_mask(k, mask)

            def flat(t):
                return t[:].rearrange("p c n -> p (c n)")
            prepare(k, "a0w", raw, [(io["L0_qkv"], flat(w[0]), flat(w[1]), None),
                                    (io["L0_proj"], flat(wo[0]), flat(wo[1]), None)],
                    rows=(xt, T, NT), loads=[(xt[:], io["x_by_position"].rearrange("(t p) d -> p t d", p=P))])
            small_head_attention(
                k, "a0", xt, NT, T, [h[:, :, 0:512] for h in w], [h[:, :, 512:640] for h in w],
                [h[:, :, 640:768] for h in w], [h[:] for h in wo], 1, lambda r, c: 4 * r + c, lambda r, c: 32 * r,
                mask, store=x1.rearrange("(t p) d -> t p d", p=P))

        k.recycle_semaphores()
        x = k.sb(top, "x", [S, B, D], F32)
        cross_attention_layer(k, x, io, x1)
        expert_layer(k, x, io)
        second_attention_layer(k, x, io)
        wide_attention_layer(k, x, io)
        ternary_mlp_layer(k, x, io)


def block_causal_mask(k, mask):
    nc = k.nc
    done = k.sem("mask0_done")
    with nc.Block() as block:
        @block.gpsimd
        def _(pool):
            pool.memset(mask[:], 0.0).then_inc(done, 1)
            pool.wait_ge(done, 1)
            pool.affine_select(out=mask[:], in_=mask[:], compare_op=ALU.is_ge, fill=MASKED, base=0,
                               pattern=[[-1, P]], channel_multiplier=1).then_inc(done, 1)
            pool.wait_ge(done, 2)
            pool.affine_select(out=mask[:], in_=mask[:], compare_op=ALU.is_ge, fill=MASKED, base=15,
                               pattern=[[B, P // B], [0, B]], channel_multiplier=-1).then_inc(done, 1)
            pool.wait_ge(done, 3)


def _columns(w):
    n_out, n_in = w.shape
    return w.T.reshape(n_in // 128, 128, n_out).transpose(1, 0, 2).reshape(128, -1)


def kernel(**inputs):
    import numpy as np
    import concourse.bacc as _bacc
    from concourse import mybir as _mybir
    from concourse.bass_utils import run_bass_kernel_spmd as _run

    a = {n: np.asarray(v) for n, v in inputs.items()}
    lay = {}
    lay["x_by_position"] = a["x"].transpose(1, 0, 2).reshape(1792, 512)
    g = a["L0_attn_weight_qkv"].reshape(4, 6, 32, 512)
    lay["L0_qkv"] = _columns(np.concatenate([g[:, 0:4].transpose(1, 0, 2, 3).reshape(512, 512),
                                             g[:, 4].reshape(128, 512), g[:, 5].reshape(128, 512)]))
    lay["L0_proj"] = _columns(a["L0_attn_weight_proj"])
    kx, vx = a["L0_xattn_w_kv_x"][:1024], a["L0_xattn_w_kv_x"][1024:]
    for phase, q, key, val in (("self", a["L0_xattn_wq"], a["L0_xattn_wk"], a["L0_xattn_wv"]),
                               ("cross", a["L0_xattn_wqx"], kx, vx)):
        lay[f"L0x_{phase}"] = np.stack([_columns(np.concatenate(
            [q[1024 * i:1024 * (i + 1)], key[512 * i:512 * (i + 1)], val[512 * i:512 * (i + 1)]])) for i in range(2)])
    lay["L0x_proj"] = _columns(a["L0_xattn_wproj"])

    def chunks(v):
        return v.reshape(-1, 128).T

    def everywhere(v):
        return np.broadcast_to(v.reshape(1, 1), (128, 1))
    lay["L0x_columns"] = np.concatenate(
        [chunks(a[f"L0_xattn_{n}_in_scale"]) for n in ("q", "k", "v", "qx")]
        + [everywhere(a[f"L0_xattn_{n}_scale"]) for n in ("wq", "wk", "wv", "wqx")]
        + [everywhere(a["L0_xattn_proj_in_scale"]), everywhere(a["L0_xattn_proj_w_scale"])]
        + [chunks(a["L0_xattn_ln_w"]), chunks(a["L0_xattn_ln_b"])]
        + [a[f"L0_xattn_{n}ln_{p}"].reshape(128, 1) for n in ("q", "k", "qx", "kx") for p in "wb"]
        + [chunks(a["L0_xattn_proj_smooth"])], axis=1)
    ctx = a["ctx_2048"]
    lay["ctxT"] = ctx.transpose(0, 2, 1).reshape(16, 4, 128, 375).transpose(0, 2, 1, 3).reshape(16, 128, 1500)
    lay["ctx"] = ctx
    for n in "qkvo":
        lay[f"L1_{n}"] = _columns(a[f"L1_attn_W{n}"])
        lay[f"L1x_{n}"] = _columns(a[f"L1_xattn_w{n}"])
    lay["L1_bias_cols"] = np.concatenate([chunks(a["L1_attn_bq"]), chunks(a["L1_attn_bk"])], axis=1)
    lay["L1_bias_v"], lay["L1_bias_o"] = a["L1_attn_bv"].reshape(1, 512), a["L1_attn_bo"].reshape(1, 512)
    lay["L1f_up"], lay["L1f_gate"], lay["L1f_down"] = (_columns(a[f"L1_ffn_W_{n}"]) for n in ("up", "gate", "down"))
    w1, w3 = (np.concatenate([a[f"L0_ffn_{n}"], a[f"L0_ffn_s{n}"][None]]) for n in ("w1", "w3"))
    lay["moe_up"] = np.concatenate([w1, w3[:, :, 384:448], w3[:, :, 0:384]], axis=2).reshape(9, 4, 128, 896)\
        .transpose(0, 2, 1, 3).reshape(9, 128, 3584)
    down = np.concatenate([a["L0_ffn_w2"], a["L0_ffn_sw2"][None]])
    lay["moe_w2"] = down[:, 0:384].reshape(9, 3, 128, 512).transpose(0, 2, 1, 3).reshape(9, 128, 1536)
    lay["moe_w2_tail"] = down[:, 384:448]
    lay["moe_gate"] = _columns(a["L0_ffn_gate_w"].T)
    lay["moe_bias"] = a["L0_ffn_expert_bias"].reshape(1, 8)
    lay = {n: np.ascontiguousarray(v) for n, v in lay.items()}
    nc = _bacc.Bacc("TRN2", target_bir_lowering=False, num_devices=1)
    io = {n: nc.dram_tensor(f"in_{n}", v.shape, _mybir.dt.from_np(v.dtype), kind="ExternalInput").ap()
          for n, v in lay.items()}
    out = nc.dram_tensor("out", (16, 112, 512), _mybir.dt.float32, kind="ExternalOutput").ap()
    io["out"] = out
    decoder(nc, io)
    r = _run(nc, [{f"in_{n}": v for n, v in lay.items()}], core_ids=[0])
    return r.results[0]["out"]
```
